# Optimizing a Trainium2 kernel written in Bass

```python
import numpy as np
import jax
import jax.numpy as jnp

def _softmax(x, axis=-1):
    return jax.nn.softmax(x, axis=axis)

def _gelu(x):
    return jax.nn.gelu(x, approximate=True)

def _silu(x):
    return jax.nn.silu(x)

def _sigmoid(x):
    return jax.nn.sigmoid(x)

def _layernorm(x, axis=-1, eps=1e-05):
    m = jnp.mean(x, axis=axis, keepdims=True)
    v = jnp.var(x, axis=axis, keepdims=True)
    return (x - m) / jnp.sqrt(v + eps)

def _scatter_add(tgt, idx, src, axis=0):
    return tgt.at[idx].add(src)

def _segment_sum(src, seg, n):
    return jax.ops.segment_sum(src, seg, n)
kernel_name = 'mk_perceiver_d2_seqx_r8_890e76'

def setup_inputs(seed: int=0):
    np.random.seed(seed)
    _w = jnp.asarray

    def _rec_inputs():
        import jax
        import jax.numpy as jnp
        _rk = jax.random.key(seed)
        x = -0.0002928 + 1 * jax.random.normal(jax.random.fold_in(_rk, 1), (32, 64, 256), jnp.float32)
        _lenS = 64 - jax.random.randint(jax.random.fold_in(_rk, 7), (32,), 0, max(1, 64 // 4) + 1, jnp.int32)
        _lenS2 = 1601 - jax.random.randint(jax.random.fold_in(_rk, 8), (32,), 0, max(1, 1601 // 4) + 1, jnp.int32)
        _ctx_512P = jax.random.normal(jax.random.fold_in(_rk, 11), (32, 16, 64), jnp.float32)
        _ctx_512c = jax.random.dirichlet(jax.random.fold_in(_rk, 511), 0.3 * jnp.ones((16,), jnp.float32), (32, 1601))
        _ctx_512t = jnp.einsum('bsk,bkd->bsd', _ctx_512c, _ctx_512P)
        _ctx_512t = _ctx_512t * jax.lax.rsqrt(jnp.mean(jnp.square(_ctx_512t)) + 1e-12) * 0.953939
        ctx_512 = 0.000227908 + 0.99994 * (_ctx_512t + 0.3 * jax.random.normal(jax.random.fold_in(_rk, 611), (32, 1601, 64), jnp.float32))
        return (x, ctx_512)
    x, ctx_512 = _rec_inputs()

    def _L0_xattn_setup():
        import jax, jax.numpy as jnp
        import numpy as np
        B, S, L = (2, 128, 128)
        DIM_Q, H, K, D_C, D_CQ, R = (256, 16, 128, 64, 192, 64)

        def _rope_tables(seq_len, dim, dtype):
            inv_freq = 1.0 / 10000.0 ** (jnp.arange(0, dim, 2, dtype=dtype) / dim)
            t = jnp.arange(seq_len, dtype=dtype)
            freqs = t[:, None] * inv_freq[None, :]
            sin = jnp.repeat(jnp.sin(freqs), 2, axis=-1)
            cos = jnp.repeat(jnp.cos(freqs), 2, axis=-1)
            return (sin, cos)

        def _rotate_half(x):
            h = x.shape[-1] // 2
            return jnp.concatenate([-x[..., h:], x[..., :h]], axis=-1)
        key = jax.random.key(seed)
        ks = jax.random.split(key, 8)
        s_in = 1.0 / np.sqrt(DIM_Q)
        s_k = 1.0 / np.sqrt(K)
        s_cq = 1.0 / np.sqrt(D_CQ)
        s_c = 1.0 / np.sqrt(D_C)
        return {'hidden_q': jax.random.normal(ks[0], (B, S, DIM_Q), jnp.float32), 'kv_c': jax.random.normal(ks[1], (B, L, D_C), jnp.float32), 'Wq': jax.random.normal(ks[2], (H * K, DIM_Q), jnp.float32) * s_in, 'w_kc_q': jax.random.normal(ks[3], (H, K, D_CQ), jnp.float32) * s_k, 'w_kc_kv': jax.random.normal(ks[4], (H, K, D_C), jnp.float32) * s_k, 'W_qr': jax.random.normal(ks[5], (H, D_CQ, R), jnp.float32) * s_cq / np.sqrt(R), 'W_kr': jax.random.normal(ks[6], (H, D_C, R), jnp.float32) * s_c, 'Wo': jax.random.normal(ks[7], (DIM_Q, H * K), jnp.float32) * s_k}
    _L0_xattn_all = _L0_xattn_setup()
    _L0_xattn_in = {k: v for k, v in _L0_xattn_all.items() if k in ('Wq', 'w_kc_q', 'w_kc_kv', 'W_qr', 'W_kr', 'Wo')}
    del _L0_xattn_all

    def _L0_attn_setup():
        import jax, jax.numpy as jnp
        import numpy as np
        B, S, H = (4, 256, 256)
        key = jax.random.key(seed)
        k1, k2, k3 = jax.random.split(key, 3)
        xav_qkv = float(np.sqrt(6.0 / (H + 3 * H)))
        xav_out = float(np.sqrt(6.0 / (H + H)))
        return {'hidden_states': jax.random.normal(k1, (B, S, H), dtype=jnp.float32), 'w_qkv': jax.random.uniform(k2, (3 * H, H), minval=-xav_qkv, maxval=xav_qkv, dtype=jnp.float32), 'b_qkv': jnp.zeros((3 * H,), dtype=jnp.float32), 'w_out': jax.random.uniform(k3, (H, H), minval=-xav_out, maxval=xav_out, dtype=jnp.float32), 'b_out': jnp.zeros((H,), dtype=jnp.float32)}
    _L0_attn_all = _L0_attn_setup()
    _L0_attn_in = {k: v for k, v in _L0_attn_all.items() if k in ('w_qkv', 'b_qkv', 'w_out', 'b_out')}
    del _L0_attn_all

    def _L0_ffn_setup():
        import jax, jax.numpy as jnp
        import numpy as np
        N_BLOCKS = 16
        BLOCK_SIZE = 64
        TOP_K = N_BLOCKS // 4
        key = jax.random.key(seed)
        k1, k2, k3, k4, k5 = jax.random.split(key, 5)
        in_f, out_f = (256, 1024)
        x = jax.random.normal(k1, (2, 512, in_f), dtype=jnp.float32)
        Wr = jax.random.normal(k2, (N_BLOCKS, in_f), dtype=jnp.float32) * in_f ** (-0.5)
        br = jnp.zeros((N_BLOCKS,), dtype=jnp.float32)
        W1 = jax.random.normal(k3, (out_f, in_f), dtype=jnp.float32) * in_f ** (-0.5)
        W2 = jax.random.normal(k4, (in_f, out_f), dtype=jnp.float32) * out_f ** (-0.5)
        return {'x': x, 'Wr': Wr, 'br': br, 'W1': W1, 'W2': W2}
    _L0_ffn_all = _L0_ffn_setup()
    _L0_ffn_in = {k: v for k, v in _L0_ffn_all.items() if k in ('Wr', 'br', 'W1', 'W2')}
    del _L0_ffn_all

    def _L1_xattn_setup():
        import jax, jax.numpy as jnp
        import numpy as np
        B, S, H, NH, L = (2, 256, 256, 16, 64)
        HD = H // NH
        key = jax.random.key(seed)
        k1, k2, k3, k4, k5 = jax.random.split(key, 5)
        scale = 0.02
        return {'q': jax.random.normal(k1, (B, S, H), dtype=jnp.float32), 'latent_kv': jax.random.normal(k2, (B, S, L), dtype=jnp.float32), 'Wq': jax.random.normal(k3, (H, H), dtype=jnp.float32) * scale, 'Wkv_expand': jax.random.normal(k4, (2 * H, L), dtype=jnp.float32) * scale, 'Wout': jax.random.normal(k5, (H, H), dtype=jnp.float32) * scale}
    _L1_xattn_all = _L1_xattn_setup()
    _L1_xattn_in = {k: v for k, v in _L1_xattn_all.items() if k in ('Wq', 'Wkv_expand', 'Wout')}
    del _L1_xattn_all

    def _L1_attn_setup():
        import jax, jax.numpy as jnp
        import numpy as np
        B, S, DIN = (2, 256, 256)
        HQ, HKV, DH = (16, 1, 128)
        key = jax.random.key(seed)
        ks = jax.random.split(key, 9)
        sc_in = 1.0 / np.sqrt(DIN)
        sc_o = 1.0 / np.sqrt(HQ * DH)
        return {'q': jax.random.normal(ks[0], (B, S, DIN), dtype=jnp.float32), 'Wq': jax.random.normal(ks[1], (DIN, HQ * DH), dtype=jnp.float32) * sc_in, 'bq': jnp.zeros((HQ * DH,), dtype=jnp.float32), 'Wk': jax.random.normal(ks[2], (DIN, HKV * DH), dtype=jnp.float32) * sc_in, 'bk': jnp.zeros((HKV * DH,), dtype=jnp.float32), 'Wv': jax.random.normal(ks[3], (DIN, HKV * DH), dtype=jnp.float32) * sc_in, 'bv': jnp.zeros((HKV * DH,), dtype=jnp.float32), 'Wo': jax.random.normal(ks[4], (HQ * DH, DIN), dtype=jnp.float32) * sc_o, 'bo': jnp.zeros((DIN,), dtype=jnp.float32)}
    _L1_attn_all = _L1_attn_setup()
    _L1_attn_in = {k: v for k, v in _L1_attn_all.items() if k in ('Wq', 'bq', 'Wk', 'bk', 'Wv', 'bv', 'Wo', 'bo')}
    del _L1_attn_all

    def _L1_ffn_setup():
        import jax, jax.numpy as jnp
        import numpy as np
        K_TOP = 2
        key = jax.random.key(seed)
        k0, k1, k2 = jax.random.split(key, 3)
        B, S, D, E, F = (4, 256, 256, 8, 256)
        x = jax.random.normal(k0, (B, S, D), dtype=jnp.float32)
        Wr = jax.random.normal(k1, (D, E), dtype=jnp.float32) * 0.02
        We = jax.random.normal(k2, (E, D, F), dtype=jnp.float32) * 0.02
        be = jnp.zeros((E, F), dtype=jnp.float32)
        return {'x': x, 'Wr': Wr, 'We': We, 'be': be}
    _L1_ffn_all = _L1_ffn_setup()
    _L1_ffn_in = {k: v for k, v in _L1_ffn_all.items() if k in ('Wr', 'We', 'be')}
    del _L1_ffn_all
    return {'x': x, 'ctx_512': ctx_512, 'L0_xattn_Wq': _L0_xattn_in['Wq'], 'L0_xattn_w_kc_q': _L0_xattn_in['w_kc_q'], 'L0_xattn_w_kc_kv': _L0_xattn_in['w_kc_kv'], 'L0_xattn_W_qr': _L0_xattn_in['W_qr'], 'L0_xattn_W_kr': _L0_xattn_in['W_kr'], 'L0_xattn_Wo': _L0_xattn_in['Wo'], 'L0_attn_w_qkv': _L0_attn_in['w_qkv'], 'L0_attn_b_qkv': _L0_attn_in['b_qkv'], 'L0_attn_w_out': _L0_attn_in['w_out'], 'L0_attn_b_out': _L0_attn_in['b_out'], 'L0_ffn_Wr': _L0_ffn_in['Wr'], 'L0_ffn_br': _L0_ffn_in['br'], 'L0_ffn_W1': _L0_ffn_in['W1'], 'L0_ffn_W2': _L0_ffn_in['W2'], 'L1_xattn_Wq': _L1_xattn_in['Wq'], 'L1_xattn_Wkv_expand': _L1_xattn_in['Wkv_expand'], 'L1_xattn_Wout': _L1_xattn_in['Wout'], 'L1_attn_Wq': _L1_attn_in['Wq'], 'L1_attn_bq': _L1_attn_in['bq'], 'L1_attn_Wk': _L1_attn_in['Wk'], 'L1_attn_bk': _L1_attn_in['bk'], 'L1_attn_Wv': _L1_attn_in['Wv'], 'L1_attn_bv': _L1_attn_in['bv'], 'L1_attn_Wo': _L1_attn_in['Wo'], 'L1_attn_bo': _L1_attn_in['bo'], 'L1_ffn_Wr': _L1_ffn_in['Wr'], 'L1_ffn_We': _L1_ffn_in['We'], 'L1_ffn_be': _L1_ffn_in['be']}

def reference(x, ctx_512, L0_xattn_Wq, L0_xattn_w_kc_q, L0_xattn_w_kc_kv, L0_xattn_W_qr, L0_xattn_W_kr, L0_xattn_Wo, L0_attn_w_qkv, L0_attn_b_qkv, L0_attn_w_out, L0_attn_b_out, L0_ffn_Wr, L0_ffn_br, L0_ffn_W1, L0_ffn_W2, L1_xattn_Wq, L1_xattn_Wkv_expand, L1_xattn_Wout, L1_attn_Wq, L1_attn_bq, L1_attn_Wk, L1_attn_bk, L1_attn_Wv, L1_attn_bv, L1_attn_Wo, L1_attn_bo, L1_ffn_Wr, L1_ffn_We, L1_ffn_be):
    import jax
    import jax.numpy as jnp

    def _L0_xattn_ref(hidden_q, kv_c, Wq, w_kc_q, w_kc_kv, W_qr, W_kr, Wo):
        import jax, jax.numpy as jnp
        import numpy as np
        B, S, L = (2, 128, 128)
        DIM_Q, H, K, D_C, D_CQ, R = (256, 16, 128, 64, 192, 64)

        def _rope_tables(seq_len, dim, dtype):
            inv_freq = 1.0 / 10000.0 ** (jnp.arange(0, dim, 2, dtype=dtype) / dim)
            t = jnp.arange(seq_len, dtype=dtype)
            freqs = t[:, None] * inv_freq[None, :]
            sin = jnp.repeat(jnp.sin(freqs), 2, axis=-1)
            cos = jnp.repeat(jnp.cos(freqs), 2, axis=-1)
            return (sin, cos)

        def _rotate_half(x):
            h = x.shape[-1] // 2
            return jnp.concatenate([-x[..., h:], x[..., :h]], axis=-1)
        b, s, _ = hidden_q.shape
        l = kv_c.shape[1]
        q_hk = (hidden_q @ Wq.T).reshape(b, s, H, K)
        q_big = jnp.einsum('bshk,hkq->bshq', q_hk, w_kc_q)
        sin, cos = _rope_tables(l, D_C, kv_c.dtype)
        kv_rope = kv_c * cos[None] + _rotate_half(kv_c) * sin[None]
        q_r = jnp.einsum('bshq,hqr->bhsr', q_big, W_qr)
        k_r = jnp.einsum('bld,hdr->bhlr', kv_rope, W_kr)
        scores = jnp.einsum('bhsr,bhlr->bhsl', q_r, k_r)
        attn = jax.nn.softmax(scores, axis=-1)
        ctx_c = jnp.einsum('bhsl,bld->bhsd', attn, kv_rope)
        ctx_lat = jnp.einsum('bhsd,hkd->bshk', ctx_c, w_kc_kv)
        out = ctx_lat.reshape(b, s, H * K) @ Wo.T
        return out

    def _L0_attn_ref(hidden_states, w_qkv, b_qkv, w_out, b_out):
        import jax, jax.numpy as jnp
        import numpy as np
        B, S, H = (4, 256, 256)
        Bc, Sc, Hc = hidden_states.shape
        scaling = jnp.sqrt(jnp.asarray(Hc, hidden_states.dtype))
        qkv = jnp.einsum('bsh,oh->bso', hidden_states, w_qkv) + b_qkv
        q, k, v = jnp.split(qkv, 3, axis=-1)
        scores = jnp.einsum('bqh,bkh->bqk', q, k) / scaling
        probs = jax.nn.softmax(scores, axis=-1)
        context = jnp.einsum('bqk,bkh->bqh', probs, v)
        out = jnp.einsum('bsh,oh->bso', context, w_out) + b_out
        return out

    def _L0_ffn_ref(x, Wr, br, W1, W2):
        import jax, jax.numpy as jnp
        import numpy as np
        N_BLOCKS = 16
        BLOCK_SIZE = 64
        TOP_K = N_BLOCKS // 4
        x_shape = x.shape
        in_f = x_shape[-1]
        xf = x.reshape(-1, in_f)
        n = xf.shape[0]
        prob = jax.nn.softmax(xf @ Wr.T + br, axis=-1)
        _, idx = jax.lax.top_k(prob, TOP_K)
        mask = jnp.zeros((n, N_BLOCKS), dtype=xf.dtype)
        mask = mask.at[jnp.arange(n)[:, None], idx].set(1.0)
        W1b = W1.reshape(N_BLOCKS, BLOCK_SIZE, in_f)
        h = jnp.einsum('nf,ibf->nib', xf, W1b)
        h = jax.nn.gelu(h, approximate=False) * mask[:, :, None]
        W2b = W2.reshape(in_f, N_BLOCKS, BLOCK_SIZE)
        y = jnp.einsum('nib,fib->nf', h, W2b)
        return y.reshape(x_shape)

    def _L1_xattn_ref(q, latent_kv, Wq, Wkv_expand, Wout):
        import jax, jax.numpy as jnp
        import numpy as np
        B, S, H, NH, L = (2, 256, 256, 16, 64)
        HD = H // NH
        b, sq, _ = q.shape
        sk = latent_kv.shape[1]
        qp = q @ Wq.T
        kv = latent_kv @ Wkv_expand.T
        k, v = jnp.split(kv, 2, axis=-1)
        qh = qp.reshape(b, sq, NH, HD).transpose(0, 2, 1, 3)
        kh = k.reshape(b, sk, NH, HD).transpose(0, 2, 1, 3)
        vh = v.reshape(b, sk, NH, HD).transpose(0, 2, 1, 3)
        inv_sqrt_d = 1.0 / jnp.sqrt(jnp.float32(HD))
        scores = jnp.einsum('bhqd,bhkd->bhqk', qh, kh) * inv_sqrt_d
        causal = jnp.tril(jnp.ones((sq, sk), dtype=bool))
        scores = jnp.where(causal, scores, jnp.finfo(scores.dtype).min)
        attn = jax.nn.softmax(scores, axis=-1)
        out = jnp.einsum('bhqk,bhkd->bhqd', attn, vh)
        out = out.transpose(0, 2, 1, 3).reshape(b, sq, H)
        return out @ Wout.T

    def _L1_attn_ref(q, Wq, bq, Wk, bk, Wv, bv, Wo, bo):
        import jax, jax.numpy as jnp
        import numpy as np
        B, S, DIN = (2, 256, 256)
        HQ, HKV, DH = (16, 1, 128)
        r = HQ // HKV
        lead = q.shape[:-1]
        k_lin = (q @ Wk + bk).reshape(*lead, HKV, DH)
        v_lin = (q @ Wv + bv).reshape(*lead, HKV, DH)
        qx = jnp.swapaxes(v_lin, -3, -2)
        kx = jnp.repeat(jnp.swapaxes(k_lin, -3, -2), r, axis=-3)
        vx = jnp.repeat(qx, r, axis=-3)
        scores = jnp.einsum('...jd,...id->...ji', qx, kx) / DH
        attn = jax.nn.softmax(scores, axis=-1)
        out = jnp.einsum('...jk,...kd->...jd', attn, vx)
        out = jnp.swapaxes(out, -3, -2).reshape(*lead, HQ * DH)
        return out @ Wo + bo

    def _L1_ffn_ref(x, Wr, We, be):
        import jax, jax.numpy as jnp
        import numpy as np
        K_TOP = 2
        logits = jnp.einsum('bsd,de->bse', x, Wr)
        w, sel = jax.lax.top_k(logits, K_TOP)
        w = jax.nn.softmax(w, axis=-1)
        E = We.shape[0]
        gate = jnp.einsum('bsk,bske->bse', w, jax.nn.one_hot(sel, E, dtype=w.dtype))
        out = jnp.zeros(x.shape[:2] + (We.shape[2],), dtype=x.dtype)
        for e in range(E):
            out = out + gate[..., e:e + 1] * (jnp.einsum('bsd,df->bsf', x, We[e]) + be[e])
        return out
    x = x + _L0_xattn_ref(_layernorm(x, axis=-1), ctx_512, L0_xattn_Wq, L0_xattn_w_kc_q, L0_xattn_w_kc_kv, L0_xattn_W_qr, L0_xattn_W_kr, L0_xattn_Wo)
    x = x + _L0_attn_ref(_layernorm(x, axis=-1), L0_attn_w_qkv, L0_attn_b_qkv, L0_attn_w_out, L0_attn_b_out)
    x = x + _L0_ffn_ref(_layernorm(x, axis=-1), L0_ffn_Wr, L0_ffn_br, L0_ffn_W1, L0_ffn_W2)
    x = x + _L1_xattn_ref(_layernorm(x, axis=-1), ctx_512, L1_xattn_Wq, L1_xattn_Wkv_expand, L1_xattn_Wout)
    x = x + _L1_attn_ref(_layernorm(x, axis=-1), L1_attn_Wq, L1_attn_bq, L1_attn_Wk, L1_attn_bk, L1_attn_Wv, L1_attn_bv, L1_attn_Wo, L1_attn_bo)
    x = x + _L1_ffn_ref(_layernorm(x, axis=-1), L1_ffn_Wr, L1_ffn_We, L1_ffn_be)
    return x

_drawn_inputs = setup_inputs


def setup_inputs(seed=0):
    import zlib

    import numpy as np

    out = dict(_drawn_inputs(seed))
    spreads = {'L0_attn_b_qkv': (0.0, 0.1),
     'L0_attn_b_out': (0.0, 0.1),
     'L0_ffn_br': (0.0, 0.1),
     'L1_attn_bq': (0.0, 0.1),
     'L1_attn_bk': (0.0, 2.0),
     'L1_attn_bv': (0.0, 0.1),
     'L1_attn_bo': (0.0, 0.1),
     'L1_ffn_be': (0.0, 0.1)}
    factors = {'L1_xattn_Wq': 50.594, 'L1_attn_Wk': 4.837}
    for name, (base, spread) in spreads.items():
        noise = np.random.default_rng([zlib.crc32(name.encode()), seed]).standard_normal(out[name].shape)
        drawn = base * np.exp(spread * noise) if base else spread * noise
        out[name] = jnp.asarray(drawn.astype(out[name].dtype))
    for name, factor in factors.items():
        out[name] = (out[name] * factor).astype(out[name].dtype)
    return out
```

```python
from contextlib import ExitStack

import concourse.bass as bass
from concourse import mybir

ALU = mybir.AluOpType
ACT = mybir.ActivationFunctionType
AX = mybir.AxisListType
F32 = mybir.dt.float32
F16 = mybir.dt.float16
I32 = mybir.dt.int32

P = 128
B, S, D = 32, 64, 256
L, DC = 1601, 64
H = 16
TOK = B * S
NT = TOK // P
KT = -(-L // P)
KEYS = KT * P
FULL_P = L // KT
QC = H * S
PAIRS = 2 * (-(-KT // 2))
UNITS = 2 * KT
CH = 416
NCH = KEYS // CH
QT = QC // P
MAXES = QT * NCH
RING = PAIRS // 2
GT = 4
NG = NT // GT
GTOK = GT * P
EPS = 1e-5


def pair_of(u):
    return divmod(u, 2) if u < UNITS - 2 else (PAIRS - 2 + u - (UNITS - 2), 0)


def units_through(k):
    return min(2 * k + 2, UNITS - 2) + max(0, k - (PAIRS - 3))


FIRST_U = (5, 6)
LAST_U = 22
TURN_U = (1, 2)
SUMS_U, SPREAD_U, OUT_U = 7, 10, 15


SLOTS = [[(u, place) for u in range(FIRST_U[j], LAST_U + 1) for place in range(2) if place == 0 or u % 2 == 1] for j in range(2)]


def chunks_in(j, u, place):
    return [n for n in range(MAXES) if SLOTS[j][n * len(SLOTS[j]) // MAXES] == (u, place)]


class Steps:

    def __init__(self, engine, sem, base=0):
        self.engine, self.sem, self.base, self.n = engine, sem, base, 0

    def then(self, instruction, passed=None):
        instruction.then_inc(self.sem, 1)
        self.n += 1
        self.engine.wait_ge(self.sem, self.base + self.n)
        if passed:
            self.engine.sem_inc(passed, 1)


LN_STEPS = 14


def layernorm_rows(dve, steps, x_tiles, out_tiles, stats, mv, half_var, root, work, passed=None):
    n = len(x_tiles)
    for t in range(n - 1):
        dve.bn_stats(stats[:, t, :], x_tiles[t])
    steps.then(dve.bn_stats(stats[:, n - 1, :], x_tiles[n - 1]), passed)
    for t in range(n - 1):
        dve.bn_aggr(mv[:, t, :], stats[:, t, :])
    steps.then(dve.bn_aggr(mv[:, n - 1, :], stats[:, n - 1, :]))
    v = mv[:, 0:n, 1]
    dve.tensor_scalar(half_var[:, 0:n], v, EPS, -0.5, ALU.add, ALU.mult)
    steps.then(dve.tensor_scalar(work[:, 0:n], v, EPS, None, ALU.add))
    steps.then(dve.tensor_scalar(root[:, 0:n].bitcast(I32), work[:, 0:n].bitcast(I32), 1, None, ALU.logical_shift_right))
    steps.then(dve.tensor_scalar(root[:, 0:n].bitcast(I32), root[:, 0:n].bitcast(I32), -1.0, float(0x5F3759DF), ALU.mult, ALU.add))
    for _ in range(3):
        steps.then(dve.tensor_tensor(work[:, 0:n], root[:, 0:n], root[:, 0:n], ALU.mult))
        steps.then(dve.tensor_tensor(work[:, 0:n], work[:, 0:n], half_var[:, 0:n], ALU.mult))
        steps.then(dve.scalar_tensor_tensor(out=root[:, 0:n], in0=work[:, 0:n], scalar=1.5, in1=root[:, 0:n], op0=ALU.add, op1=ALU.mult))
    for t in range(n):
        last = dve.tensor_scalar(out_tiles[t], x_tiles[t], mv[:, t, 0:1], root[:, t:t + 1], ALU.subtract, ALU.mult)
    return last


def part_one(nc, a, x_res, ident):
    with ExitStack() as ctx:
        def sb(name, shape, dt=F32):
            return ctx.enter_context(nc.sbuf_tensor(name, shape, dt))

        def sem(name):
            return ctx.enter_context(nc.semaphore(name))

        to_query = sb("to_query", [P, 2, H, DC])
        to_out = sb("to_out", [P, H, D])
        y_cols = sb("y_cols", [P, 2, TOK])
        fold(nc, a, x_res, ident, to_query, to_out, y_cols)

        cos = sb("cos", [P, KT, DC])
        sin = sb("sin", [P, KT, DC])
        raw = [sb(f"raw{j}", [P, KT, DC]) for j in range(2)]
        turned = sb("turned", [P, KT, DC])
        kv_pair = sb("kv_pair", [P, KT, 2, DC])
        kv = [sb(f"kv{j}", [P, KT, DC]) for j in range(2)]
        k_high = [sb(f"k_high{j}", [P, KEYS], F16) for j in range(2)]
        k_low = [sb(f"k_low{j}", [P, KEYS], F16) for j in range(2)]
        q_both = [sb(f"q_both{j}", [P, H, S], F16) for j in range(2)]
        q_shift = [sb(f"q_shift{j}", [P, H, S], F16) for j in range(2)]
        q_hi = sb("q_hi", [P, H // 2, P], F16)
        q_lo = sb("q_lo", [P, H // 2, P], F16)
        ident16 = sb("ident16", [P, P], F16)
        pick = sb("pick", [P, QT, QT])
        unpick = sb("unpick", [P, QT, P])
        maxes = sb("maxes", [P, QT, NCH])
        neg_max = sb("neg_max", [P, QT])
        neg_max2 = sb("neg_max2", [P, QT, 2], F16)
        probs = [sb(f"probs{r}", [P, 2, 512]) for r in range(RING)]
        sums = [sb(f"sums{j}", [P, 2, 2, 512]) for j in range(2)]
        held = sb("held", [P, 2, 512])
        inv = sb("inv", [P, P])
        mixed = sb("mixed", [P, H, 2, S])

        s_bank = [ctx.enter_context(nc.psum_tensor(f"s_bank{k}", [P, 512], F32)) for k in range(2)]
        m_bank = [ctx.enter_context(nc.psum_tensor(f"m_bank{k}", [P, 512], F32)) for k in range(2)]
        v_bank = [ctx.enter_context(nc.psum_tensor(f"v_bank{k}", [P, 512], F32)) for k in range(2)]
        w_bank = [ctx.enter_context(nc.psum_tensor(f"w_bank{k}", [P, 512], F32)) for k in range(2)]

        consts_in = sem("consts_in")
        keys_in = [sem(f"keys_in{j}") for j in range(2)]
        rope_products = sem("rope_products")
        rope_done = sem("rope_done")
        const_made = sem("const_made")
        query_ready = sem("query_ready")
        query_high = sem("query_high")
        query_low = sem("query_low")
        stacked = sem("stacked")
        turned_ready = sem("turned_ready")
        key_high = sem("key_high")
        key_low = sem("key_low")
        chunk_ready = sem("chunk_ready")
        chunk_max = sem("chunk_max")
        max_steps = sem("max_steps")
        shift_known = sem("shift_known")
        shift_ready = sem("shift_ready")
        shift_placed = sem("shift_placed")
        score_ready = sem("score_ready")
        exp_done = sem("exp_done")
        value_done = sem("value_done")
        held_done = sem("held_done")
        sum_added = sem("sum_added")
        sum_ready = sem("sum_ready")
        inverted = sem("inverted")
        spread_ready = sem("spread_ready")
        doubled = sem("doubled")
        kv_filled = sem("kv_filled")
        norm_done = sem("norm_done")
        out_ready = sem("out_ready")
        x_added = sem("x_added")

        block = ctx.enter_context(nc.Block())

        def walk(engine, first, step):
            first()
            step(0, True, False)
            with engine.Fori(1, NT - 1) as i:
                step(i, False, False)
            step(NT - 1, False, True)

        @block.sync
        def _(sp):
            sp.dma_start(cos[:, :, :], a["cos"]).then_inc(consts_in, 16)
            sp.dma_start(sin[:, :, :], a["sin"]).then_inc(consts_in, 16)
            sp.dma_start(ident16[:, :], a["ident16"]).then_inc(consts_in, 16)
            sp.dma_start(pick[:, :, :], a["pick"]).then_inc(consts_in, 16)
            sp.dma_start(unpick[:, :, :], a["unpick"]).then_inc(consts_in, 16)
            for j in range(2):
                sp.dma_start(k_low[j][DC:P, :], a["k_rows"]).then_inc(consts_in, 16)
                sp.dma_start(q_shift[j][DC:P, :, :], a["q_rows"]).then_inc(consts_in, 16)

            def load(b, j):
                src = a["ctx"][bass.ds(b, 1), :, :].rearrange("a l d -> (a l) d")
                sp.dma_start(raw[j][0:FULL_P, :, :], src[0:FULL_P * KT, :].rearrange("(p t) d -> p t d", t=KT)).then_inc(keys_in[j], 16)
                sp.dma_start(raw[j][FULL_P:P, :, :], src[L - (P - FULL_P) * KT:L, :].rearrange("(p t) d -> p t d", t=KT)).then_inc(keys_in[j], 16)

            def first():
                load(0, 0)
                load(1, 1)

            def step(i, is_first, is_last):
                for j in range(2):
                    if not is_last:
                        sp.wait_ge(rope_done, 2 * i + j + 1)
                        load(2 * i + j + 2, j)

            walk(sp, first, step)

        @block.gpsimd
        def _(pool):
            def step(i, is_first, is_last):
                for j in range(2):
                    b = 2 * i + j
                    done = PAIRS * b
                    for k in range(2, PAIRS):
                        tp, half = divmod(k, 2)
                        pool.wait_ge(exp_done, UNITS * b + units_through(k))
                        if tp == 1:
                            if not is_first:
                                pool.wait_ge(sum_ready, b - 1)
                            op = pool.tensor_tensor(sums[j][:, half, :, :], probs[half][:, :, :], probs[k % RING][:, :, :], ALU.add)
                        else:
                            pool.wait_ge(sum_added, done + k - 3)
                            w = 2 if 2 * tp + 1 < KT else 1
                            op = pool.tensor_tensor(sums[j][:, half, 0:w, :], sums[j][:, half, 0:w, :], probs[k % RING][:, 0:w, :], ALU.add)
                        op.then_inc(sum_added, 1)
                        if k >= PAIRS - 2:
                            pool.wait_ge(sum_added, done + (PAIRS - 3 if half == 0 else PAIRS - 1))
                            pool.tensor_tensor(sums[j][:, half, 0, :], sums[j][:, half, 0, :], sums[j][:, half, 1, :], ALU.add).then_inc(sum_added, 1)

            walk(pool, lambda: None, step)

        @block.scalar
        def _(act):
            def query_copy(tile):
                for piece in range(2):
                    act.wait_ge(query_ready, 2 * tile + piece + 1)
                    if not (isinstance(tile, int) and tile == 0):
                        act.wait_ge(stacked, 2 * tile)
                    act.activation(q_hi[:, 4 * piece:4 * piece + 4, :].rearrange("p a t -> p (a t)"), w_bank[piece][:, :], ACT.Copy).then_inc(query_high, 1)

            def key_copy(b, j, n):
                w = min(4 * P, KEYS - 512 * n)
                act.wait_ge(turned_ready, 4 * b + n + 1)
                act.activation(k_high[j][:, 512 * n:512 * n + w], w_bank[n % 2][:, 0:w], ACT.Copy).then_inc(key_high, 1)

            def double(b, j):
                act.wait_ge(rope_done, b + 1)
                act.activation(kv_pair[:, :, 1, :], kv_pair[:, :, 0, :], ACT.Copy).then_inc(doubled, 1)

            def fill_kv(b, j, first_use=False):
                if not first_use:
                    act.wait_ge(value_done, PAIRS * (b - 1))
                act.activation(kv[j][:, :, :], kv_pair[:, :, 0, :], ACT.Copy).then_inc(kv_filled, 1)

            def shift_copy(b, j):
                for c in range(2):
                    act.wait_ge(shift_ready, 2 * b + c + 1)
                    act.activation(q_shift[j][DC:DC + 2, 8 * c:8 * c + 8, :].rearrange("p h s -> p (h s)"), w_bank[c][0:2, :], ACT.Copy).then_inc(shift_placed, 1)

            def first():
                act.wait_ge(consts_in, 16 * 9)
                query_copy(0)
                double(0, 0)
                fill_kv(0, 0, first_use=True)
                for n in range(4):
                    key_copy(0, 0, n)
                shift_copy(0, 0)

            def step(i, is_first, is_last):
                for j in range(2):
                    b = 2 * i + j
                    ahead = not (is_last and j == 1)
                    if ahead:
                        double(b + 1, 1 - j)
                    for u in range(UNITS):
                        k, t2 = pair_of(u)
                        act.wait_ge(score_ready, UNITS * b + u + 1)
                        if t2 == 0 and not (is_first and j == 0 and k < RING):
                            act.wait_ge(value_done, PAIRS * b + k - RING + 1)
                            kk = k - RING
                            bb = b
                            if kk < 0:
                                kk, bb = kk + PAIRS, b - 1
                            done = kk + 1 if kk < 2 else (kk if kk == PAIRS - 1 else kk - 1)
                            act.wait_ge(sum_added, PAIRS * bb + done)
                        act.activation(probs[k % RING][:, t2, :], s_bank[u % 2][:, :], ACT.Exp).then_inc(exp_done, 1)
                        if ahead:
                            if j == 1 and u == 1:
                                query_copy(i + 1)
                            if u == 1:
                                fill_kv(b + 1, 1 - j, first_use=is_first and j == 0)
                            if u == 24:
                                shift_copy(b + 1, 1 - j)
                            if 0 <= u - TURN_U[j] < 4:
                                key_copy(b + 1, 1 - j, u - TURN_U[j])
                    for half in range(2):
                        act.wait_ge(value_done, PAIRS * (b + 1))
                        if not (is_first and j == 0):
                            act.wait_ge(norm_done, 2 * b)
                        act.activation(held[:, half, :], v_bank[half][:, :], ACT.Copy).then_inc(held_done, 1)

            walk(act, first, step)

        @block.vector
        def _(dve):
            def rope(b, j):
                dve.wait_ge(keys_in[j], 32 * ((b - j) // 2 + 1) if isinstance(b, int) else 16 * (b - j) + 32)
                if not (isinstance(b, int) and b == 0):
                    dve.wait_ge(turned_ready, 4 * b)
                    dve.wait_ge(kv_filled, b)
                dve.tensor_tensor(kv_pair[:, :, 0, :], raw[j][:, :, :], cos[:, :, :], ALU.mult).then_inc(rope_products, 1)
                dve.tensor_tensor(turned[:, :, 0:32], raw[j][:, :, 32:64], sin[:, :, 0:32], ALU.mult).then_inc(rope_products, 1)
                dve.tensor_tensor(turned[:, :, 32:64], raw[j][:, :, 0:32], sin[:, :, 32:64], ALU.mult).then_inc(rope_products, 1)
                dve.wait_ge(rope_products, 3 * b + 3)
                dve.tensor_tensor(kv_pair[:, :, 0, :], kv_pair[:, :, 0, :], turned[:, :, :], ALU.add).then_inc(rope_done, 1)

            def query_lows(tile):
                for piece in range(2):
                    dve.wait_ge(query_high, 2 * tile + piece + 1)
                    hi = q_hi[:, 4 * piece:4 * piece + 4, :].rearrange("p a t -> p (a t)")
                    lo = q_lo[:, 4 * piece:4 * piece + 4, :].rearrange("p a t -> p (a t)")
                    dve.tensor_tensor(lo, w_bank[piece][:, :], hi, ALU.subtract).then_inc(query_low, 1)

            def stack(b, j):
                if not (isinstance(b, int) and b < 2):
                    dve.wait_ge(score_ready, UNITS * (b - 1))
                dve.wait_ge(query_low, 2 * (b // 2) + 2 if isinstance(b, int) else b - j + 2)
                for e in range(2):
                    src = slice(DC * e, DC * e + DC)
                    dve.tensor_copy(q_both[j][0:DC, e::2, :], q_hi[src, :, S * j:S * j + S])
                    dve.tensor_copy(q_shift[j][0:DC, e::2, :], q_hi[src, :, S * j:S * j + S])
                    last = dve.tensor_copy(q_both[j][DC:P, e::2, :], q_lo[src, :, S * j:S * j + S])
                last.then_inc(stacked, 1)

            def key_lows(b, j):
                for n in range(4):
                    w = min(4 * P, KEYS - 512 * n)
                    dve.wait_ge(key_high, 4 * b + n + 1)
                    dve.tensor_tensor(k_low[j][0:DC, 512 * n:512 * n + w], w_bank[n % 2][0:DC, 0:w], k_high[j][0:DC, 512 * n:512 * n + w], ALU.subtract).then_inc(key_low, 1)

            def chunk(b, n):
                dve.wait_ge(chunk_ready, MAXES * b + n + 1)
                dve.tensor_reduce(maxes[:, n // NCH, n % NCH:n % NCH + 1], m_bank[n % 2][:, 0:CH], AX.X, ALU.max).then_inc(chunk_max, 1)

            def shift(b):
                dve.wait_ge(chunk_max, MAXES * (b + 1))
                dve.tensor_reduce(neg_max[:, :], maxes[:, :, :], AX.X, ALU.max, negate=True).then_inc(max_steps, 1)
                dve.wait_ge(max_steps, 2 * b + 1)
                dve.tensor_copy(neg_max2[:, :, 0], neg_max[:, :]).then_inc(max_steps, 1)
                dve.wait_ge(max_steps, 2 * b + 2)
                dve.tensor_tensor(neg_max2[:, :, 1], neg_max[:, :], neg_max2[:, :, 0], ALU.subtract).then_inc(shift_known, 1)

            def invert(b):
                dve.wait_ge(sum_ready, b + 1)
                dve.reciprocal(inv[0:QT, :], w_bank[0][0:QT, 0:P]).then_inc(inverted, 1)

            def normalise(b, j, half, tile):
                dve.wait_ge(spread_ready, 2 * b + half + 1)
                dve.wait_ge(held_done, 2 * b + half + 1)
                if j == 0 and not (isinstance(b, int) and b == 0) and half == 0:
                    dve.wait_ge(out_ready, tile)
                dve.tensor_tensor(mixed[:, 8 * half:8 * half + 8, j, :], held[:, half, :].rearrange("p (h s) -> p h s", h=8),
                                  w_bank[half][:, :].rearrange("p (h s) -> p h s", h=8), ALU.mult).then_inc(norm_done, 1)

            def add_out(tile):
                dve.wait_ge(out_ready, tile + 1)
                xt = x_res[:, bass.ds(tile, 1), :].rearrange("p a d -> p (a d)")
                dve.tensor_tensor(xt, w_bank[0][:, 0:D], xt, ALU.add).then_inc(x_added, 1)

            def first():
                dve.memset(inv[:, :], 0.0).then_inc(const_made, 1)
                dve.wait_ge(consts_in, 16 * 9)
                rope(0, 0)
                query_lows(0)
                stack(0, 0)
                key_lows(0, 0)
                for n in range(MAXES):
                    chunk(0, n)
                shift(0)
                rope(1, 1)

            def step(i, is_first, is_last):
                for j in range(2):
                    b = 2 * i + j
                    ahead = not (is_last and j == 1)
                    behind = not (is_first and j == 0)
                    if ahead:
                        if j == 1:
                            query_lows(i + 1)
                        stack(b + 1, 1 - j)
                        key_lows(b + 1, 1 - j)
                    for u in range(UNITS):
                        if ahead:
                            for n in chunks_in(j, u, 0) + chunks_in(j, u, 1):
                                chunk(b + 1, n)
                        if behind and u == SUMS_U:
                            invert(b - 1)
                        if behind and u in (SPREAD_U, SPREAD_U + 1):
                            normalise(b - 1, 1 - j, u - SPREAD_U, i)
                        if u == OUT_U and j == 0 and not is_first:
                            add_out(i - 1)
                    if ahead:
                        shift(b + 1)
                    if not is_last:
                        rope(b + 2, j)

            walk(dve, first, step)
            invert(B - 1)
            for half in range(2):
                normalise(B - 1, 1, half, NT - 1)
            add_out(NT - 1)

        @block.tensor
        def _(pe):
            def queries(tile, after):
                for piece in range(2):
                    after(piece)
                    for pair in range(4):
                        for c in range(2):
                            h = 8 * piece + 2 * pair
                            last = pe.matmul(w_bank[piece][:, P * pair:P * pair + P],
                                             to_query[:, c, h:h + 2, :].rearrange("p h d -> p (h d)"),
                                             y_cols[:, c, bass.ds(tile * P, P)], start=(c == 0), stop=(c == 1))
                    last.then_inc(query_ready, 1)

            def turn_keys(b, j, n):
                for t in range(4 * n, min(4 * n + 4, KT)):
                    last = pe.transpose(w_bank[n % 2][:, P * (t % 4):P * (t % 4) + P],
                                        kv_pair[:, t, :, :].rearrange("p a d -> p (a d)"), ident[:, :])
                last.then_inc(turned_ready, 1)

            def chunk(b, j, n, first_batch=False):
                if n >= 2:
                    pe.wait_ge(chunk_max, MAXES * b + n - 1)
                elif not first_batch:
                    pe.wait_ge(chunk_max, MAXES * b + n - 1)
                g, c = divmod(n, NCH)
                pe.matmul(m_bank[n % 2][:, 0:CH], q_both[j][:, 2 * g:2 * g + 2, :].rearrange("p h s -> p (h s)"),
                          k_high[j][:, CH * c:CH * c + CH], start=True, stop=True).then_inc(chunk_ready, 1)

            def shift_rows(b, j):
                pe.wait_ge(shift_known, b + 1)
                for c in range(2):
                    for g in range(4 * c, 4 * c + 4):
                        last = pe.matmul(w_bank[c][0:2, P * (g % 4):P * (g % 4) + P], neg_max2[:, g, :], ident16[:, :], start=True, stop=True)
                    last.then_inc(shift_ready, 1)

            def score(b, j, u):
                k, t2 = pair_of(u)
                tp, half = divmod(k, 2)
                t = 2 * tp + t2
                keys = slice(P * t, P * t + P)
                cols = slice(8 * half, 8 * half + 8)
                pe.matmul(s_bank[u % 2][:, :], k_high[j][:, keys], q_both[j][:, cols, :].rearrange("p h s -> p (h s)"), start=True, stop=False)
                pe.matmul(s_bank[u % 2][:, :], k_low[j][:, keys], q_shift[j][:, cols, :].rearrange("p h s -> p (h s)"), start=False, stop=True).then_inc(score_ready, 1)

            def values(b, j, k):
                tp, half = divmod(k, 2)
                for t2 in range(2):
                    t = 2 * tp + t2
                    if t < KT:
                        last = pe.matmul(v_bank[half][DC * t2:DC * t2 + DC, :], kv[j][:, t, :], probs[k % RING][:, t2, :],
                                         start=(tp == 0), stop=(t + 2 >= KT))
                last.then_inc(value_done, 1)

            def add_keys(b, j):
                pe.wait_ge(sum_added, PAIRS * (b + 1))
                for g in range(QT):
                    last = pe.matmul(w_bank[0][0:QT, 0:P], pick[:, g, :], sums[j][:, g // 4, 0, P * (g % 4):P * (g % 4) + P], start=(g == 0), stop=(g == QT - 1))
                last.then_inc(sum_ready, 1)

            def spread_inverse(b, half):
                pe.wait_ge(inverted, b + 1)
                for g in range(4):
                    last = pe.matmul(w_bank[half][:, P * g:P * g + P], unpick[:, 4 * half + g, :], inv[:, :], start=True, stop=True)
                last.then_inc(spread_ready, 1)

            def project(tile):
                pe.wait_ge(norm_done, 4 * tile + 4)
                for h in range(H):
                    last = pe.matmul(w_bank[0][:, 0:D], mixed[:, h, :, :].rearrange("p j s -> p (j s)"), to_out[:, h, :], start=(h == 0), stop=(h == H - 1))
                last.then_inc(out_ready, 1)

            def first():
                pe.wait_ge(consts_in, 16 * 9)
                queries(0, lambda piece: None)
                pe.wait_ge(doubled, 1)
                for n in range(4):
                    if n < 2:
                        pe.wait_ge(query_low, n + 1)
                    else:
                        pe.wait_ge(key_low, n - 1)
                    turn_keys(0, 0, n)
                pe.wait_ge(key_high, 4)
                pe.wait_ge(stacked, 1)
                for n in range(MAXES):
                    chunk(0, 0, n, first_batch=True)
                pe.wait_ge(key_low, 4)
                shift_rows(0, 0)
                pe.wait_ge(const_made, 1)

            def step(i, is_first, is_last):
                for j in range(2):
                    b = 2 * i + j
                    nb = b + 1
                    ahead = not (is_last and j == 1)
                    behind = not (is_first and j == 0)
                    pe.wait_ge(shift_placed, 2 * b + 2)
                    for u in range(UNITS):
                        if not (is_first and j == 0 and u < 2):
                            pe.wait_ge(exp_done, UNITS * b + u - 1)
                        score(b, j, u)
                        if ahead and j == 1 and u == 0:
                            queries(i + 1, lambda piece: None)
                        if ahead and 0 <= u - TURN_U[j] < 4:
                            n = u - TURN_U[j]
                            if n == 0:
                                pe.wait_ge(doubled, nb + 1)
                            if n < 2:
                                if j == 1:
                                    pe.wait_ge(query_low, 2 * (i + 1) + n + 1)
                            else:
                                pe.wait_ge(key_low, 4 * nb + n - 1)
                            turn_keys(nb, 1 - j, n)
                        if ahead:
                            for n in chunks_in(j, u, 0):
                                if n == 0:
                                    pe.wait_ge(stacked, nb + 1)
                                if n < NCH:
                                    pe.wait_ge(key_high, 4 * nb + (CH * (n + 1) - 1) // 512 + 1)
                                chunk(nb, 1 - j, n)
                        k = pair_of(u)[0]
                        if (u < UNITS - 2 and u % 2 == 1 and k >= 1) or u >= UNITS - 2:
                            pe.wait_ge(exp_done, UNITS * b + units_through(k - 1))
                            if k - 1 < 2 and behind:
                                pe.wait_ge(held_done, 2 * b)
                            if k - 1 == 0:
                                pe.wait_ge(kv_filled, b + 1)
                            values(b, j, k - 1)
                        if behind and u == SUMS_U:
                            if ahead:
                                pe.wait_ge(key_low, 4 * nb + 3)
                            add_keys(b - 1, 1 - j)
                        if behind and u in (SPREAD_U, SPREAD_U + 1):
                            if ahead:
                                pe.wait_ge(key_low, 4 * nb + 4)
                            spread_inverse(b - 1, u - SPREAD_U)
                        if ahead:
                            for n in chunks_in(j, u, 1):
                                if n < NCH:
                                    pe.wait_ge(key_high, 4 * nb + (CH * (n + 1) - 1) // 512 + 1)
                                chunk(nb, 1 - j, n)
                        if u == OUT_U and j == 0 and not is_first:
                            project(i - 1)
                        if ahead and u == 24:
                            if j == 0 and not is_first:
                                pe.wait_ge(x_added, i)
                            elif behind:
                                pe.wait_ge(norm_done, 2 * b)
                            shift_rows(nb, 1 - j)
                    pe.wait_ge(exp_done, UNITS * (b + 1))
                    values(b, j, PAIRS - 1)

            walk(pe, first, step)
            pe.wait_ge(norm_done, 2 * (B - 1))
            add_keys(B - 1, 1)
            for half in range(2):
                spread_inverse(B - 1, half)
            project(NT - 1)


def fold(nc, a, x_res, ident, to_query, to_out, y_cols):
    HG = 8
    with ExitStack() as ctx:
        def sb(name, shape, dt=F32):
            return ctx.enter_context(nc.sbuf_tensor(name, shape, dt))

        def sem(name):
            return ctx.enter_context(nc.semaphore(name))

        wq = sb("wq", [P, H, D])
        wkc = sb("wkc", [96, 2, H, P])
        wqr = sb("wqr", [DC, H, 192])
        wkr = sb("wkr", [DC, H, DC])
        wkv = sb("wkv", [P, H, 2, DC])
        wo = sb("wo", [P, H, D])
        qr_kr = sb("qr_kr", [96, 2, H, DC])
        kc_kr = sb("kc_kr", [P, H, DC])
        y = sb("y", [P, 2, GT, D])
        stats = sb("stats", [P, GT, 6])
        mv = sb("mv", [P, GT, 2])
        half_var = sb("half_var", [P, GT])
        root = sb("root", [P, GT])
        work = sb("work", [P, GT])
        bank = [ctx.enter_context(nc.psum_tensor(f"fold_bank{k}", [P, 512], F32)) for k in range(8)]

        x_in = sem("x_in")
        weights_in = sem("weights_in")
        job_ready = sem("job_ready")
        job_copied = sem("job_copied")
        ln_steps = sem("ln_steps")
        rows_ready = sem("rows_ready")
        cols_ready = sem("cols_ready")
        cols_copied = sem("cols_copied")
        block = ctx.enter_context(nc.Block())

        dests = [qr_kr[:, c, HG * g:HG * g + HG, :] for c in range(2) for g in range(2)]
        dests += [kc_kr[:, HG * g:HG * g + HG, :] for g in range(2)]
        dests += [to_query[:, c, HG * g:HG * g + HG, :] for c in range(2) for g in range(2)]
        dests += [to_out[:, 2 * g:2 * g + 2, :] for g in range(HG)]
        FB = 4

        @block.sync
        def _(sp):
            sp.dma_start(ident[:, :], a["ident"]).then_inc(x_in, 16)
            sp.dma_start(x_res[:, :, :], a["x"].rearrange("(t p) d -> p t d", p=P)).then_inc(x_in, 16)
            for dst, name in ((wqr[:, :, :], "wqr"), (wkr[:, :, :], "wkr"), (wkc[:, :, :, :], "wkc"), (wq[:, :, :], "wq"),
                              (wkv[:, :, 0, :], "wkv"), (wkv[:, :, 1, :], "wkv"), (wo[:, :, :], "wo")):
                sp.dma_start(dst, a[name]).then_inc(weights_in, 16)

        @block.tensor
        def _(pe):
            pe.wait_ge(weights_in, 16 * 7)
            n = 0

            def begin():
                if n >= FB:
                    pe.wait_ge(job_copied, n - FB + 1)
                return bank[n % FB]

            for c in range(2):
                for g in range(2):
                    out = begin()
                    for h in range(HG):
                        last = pe.matmul(out[0:96, DC * h:DC * h + DC], wqr[:, HG * g + h, 96 * c:96 * c + 96], wkr[:, HG * g + h, :], start=True, stop=True)
                    last.then_inc(job_ready, 1)
                    n += 1
            for g in range(2):
                out = begin()
                pe.wait_ge(job_copied, 4)
                for h in range(HG):
                    for c in range(2):
                        last = pe.matmul(out[:, DC * h:DC * h + DC], wkc[:, c, HG * g + h, :], qr_kr[:, c, HG * g + h, :], start=(c == 0), stop=(c == 1))
                last.then_inc(job_ready, 1)
                n += 1
            for c in range(2):
                for g in range(2):
                    out = begin()
                    pe.wait_ge(job_copied, 6)
                    for h in range(HG):
                        last = pe.matmul(out[:, DC * h:DC * h + DC], wq[:, HG * g + h, P * c:P * c + P], kc_kr[:, HG * g + h, :], start=True, stop=True)
                    last.then_inc(job_ready, 1)
                    n += 1
            for g in range(HG):
                out = begin()
                for h in range(2):
                    last = pe.matmul(out[:, D * h:D * h + D], wkv[:, 2 * g + h, :, :].rearrange("p a d -> p (a d)"), wo[:, 2 * g + h, :], start=True, stop=True)
                last.then_inc(job_ready, 1)
                n += 1
            pe.wait_ge(x_in, 32)
            for g in range(NG):
                pe.wait_ge(rows_ready, g + 1)
                for c in range(2):
                    if g >= 2:
                        pe.wait_ge(cols_copied, 2 * (g - 2) + c + 1)
                    out = bank[FB + (2 * g + c) % 4]
                    for t in range(GT):
                        last = pe.transpose(out[:, P * t:P * t + P], y[:, g % 2, t, P * c:P * c + P], ident[:, :])
                    last.then_inc(cols_ready, 1)

        @block.scalar
        def _(act):
            for n, dst in enumerate(dests):
                act.wait_ge(job_ready, n + 1)
                src = bank[n % FB][0:dst.shape[0], :]
                act.activation(dst, src.rearrange("p (h d) -> p h d", d=dst.shape[-1]), ACT.Copy).then_inc(job_copied, 1)
            for g in range(NG):
                for c in range(2):
                    act.wait_ge(cols_ready, 2 * g + c + 1)
                    act.activation(y_cols[:, c, GTOK * g:GTOK * g + GTOK], bank[FB + (2 * g + c) % 4][:, :], ACT.Copy).then_inc(cols_copied, 1)

        @block.vector
        def _(dve):
            dve.wait_ge(x_in, 32)
            for g in range(NG):
                if g >= 2:
                    dve.wait_ge(cols_ready, 2 * (g - 1))
                steps = Steps(dve, ln_steps, LN_STEPS * g)
                last = layernorm_rows(dve, steps, [x_res[:, GT * g + t, :] for t in range(GT)], [y[:, g % 2, t, :] for t in range(GT)],
                                      stats, mv, half_var, root, work)
                assert steps.n == LN_STEPS
                last.then_inc(rows_ready, 1)


LN2 = 5
NB0, TOP0 = 16, 4
NE, TOP1 = 8, 2
HF = 1024
HC = HF // P
HD = D // H
HPC = P // HD
PV = 2 * HD + 2
SM = GT * 2
RANK_STEPS = 5
ATT_STEPS = 4
GATE_STEPS = 6


def rank_below(dve, steps, logits, n, tri, diff, order, rank, keep, top):
    shape = [P, GT, n, n]
    flat = [t.rearrange("p t i j -> p (t i j)") for t in (diff, order)]
    steps.then(dve.tensor_tensor(diff, logits.unsqueeze(2).broadcast_to(shape), logits.unsqueeze(3).broadcast_to(shape), ALU.subtract))
    steps.then(dve.scalar_tensor_tensor(out=order.rearrange("p t i j -> p t (i j)"), in0=diff.rearrange("p t i j -> p t (i j)"), scalar=0.0,
                                        in1=tri.unsqueeze(1).broadcast_to([P, GT, n * n]), op0=ALU.is_equal, op1=ALU.mult))
    steps.then(dve.scalar_tensor_tensor(out=flat[1], in0=flat[0], scalar=0.0, in1=flat[1], op0=ALU.is_gt, op1=ALU.add))
    steps.then(dve.tensor_reduce(rank, order, AX.X, ALU.add))
    steps.then(dve.tensor_scalar(keep, rank, top - 0.5, None, ALU.is_lt))


def part_two(nc, a, out_dram, x_res, ident):
    with ExitStack() as ctx:
        def sb(name, shape, dt=F32):
            return ctx.enter_context(nc.sbuf_tensor(name, shape, dt))

        def sem(name):
            return ctx.enter_context(nc.semaphore(name))

        att_w = [sb("att0_w", [P, 2, 4, P]), sb("att1_w", [P, 2, 2, P])]
        att_b = [sb("att0_b", [P, 4]), sb("att1_b", [P, 2])]
        router0 = sb("router0", [P, 2, NB0])
        router0_b = sb("router0_b", [P, NB0])
        w1 = sb("w1", [P, 2, HF])
        w2 = sb("w2", [P, HC, D])
        x_wq = sb("x_wq", [P, 2, D])
        x_wk = sb("x_wk", [DC, D])
        x_wv = sb("x_wv", [DC, D])
        x_wo = sb("x_wo", [P, 2, D])
        router1 = sb("router1", [P, 2, NE])
        experts = sb("experts", [P, 2, NE, D])
        expert_b = sb("expert_b", [NE, D])
        block_mask = sb("block_mask", [P, P])
        causal = sb("causal", [P, S])
        head_mask = sb("head_mask", [P, HPC])
        pair_mask = sb("pair_mask", [P, D])
        tri0 = sb("tri0", [P, NB0 * NB0])
        tri1 = sb("tri1", [P, NE * NE])
        spread = sb("spread", [NB0, HC, P], F16)
        att_vo = [sb(f"att{s}_vo", [P, 2, D]) for s in range(2)]
        att_row = [sb(f"att{s}_row", [P, D]) for s in range(2)]

        bank = [ctx.enter_context(nc.psum_tensor(f"bank{k}", [P, 512], F32)) for k in range(8)]
        loads = [(att_w[0][:, :, :, :], "att0_w"), (att_w[1][:, :, :, :], "att1_w"), (att_b[0][:, :], "att0_b"), (att_b[1][:, :], "att1_b"),
                 (router0[:, :, :], "router0"), (router0_b[:, :], "router0_b"), (w1[:, :, :], "w1"), (w2[:, :, :], "w2"),
                 (x_wq[:, :, :], "x_wq"), (x_wk[:, :], "x_wk"), (x_wv[:, :], "x_wv"), (x_wo[:, :, :], "x_wo"),
                 (router1[:, :, :], "router1"), (experts[:, :, :, :], "experts"), (expert_b[:, :], "expert_b"),
                 (block_mask[:, :], "block_mask"), (causal[:, :], "causal"), (head_mask[:, :], "head_mask"), (pair_mask[:, :], "pair_mask"),
                 (tri0[:, :], "tri0"), (tri1[:, :], "tri1"), (spread[:, :, :], "spread")]
        fold_values(nc, a, bank, att_vo, att_row, loads)

        y = sb("y2", [P, GT, D])
        yt = sb("yt", [P, 2, GTOK])
        stats = sb("stats2", [P, GT, 6])
        mv = sb("mv2", [P, GT, 2])
        half_var = sb("half_var2", [P, GT])
        root = sb("root2", [P, GT])
        work = sb("work2", [P, GT])
        lin = sb("lin", [P, 4, GTOK])
        vals = sb("vals", [P, GT, D])
        masked = sb("masked", [P, GT, P])
        att_shift = sb("att_shift", [P, GT])
        att_sum = sb("att_sum", [P, GT])
        att_inv = sb("att_inv", [P, GT])
        att_p = sb("att_p", [P, GT, P])
        att_pt = sb("att_pt", [P, GTOK])
        logits = sb("logits", [P, GT, NB0])
        diff = sb("diff", [P, GT * NB0 * NB0])
        order = sb("order", [P, GT * NB0 * NB0])
        rank = sb("rank", [P, GT, NB0])
        keep = sb("keep", [P, GT, NB0])
        keep_t = sb("keep_t", [NB0, GTOK], F16)
        hidden = sb("hidden", [P, HC, GTOK])
        ctx_first = sb("ctx_first", [DC, 2 * GT, 2, S])
        xq = sb("xq", [P, 2, GTOK])
        xk1 = sb("xk1", [P, GTOK])
        wide_k = [sb(f"wide_k{c}", [P, 2 * GT, HPC, S]) for c in range(2)]
        pair_v = sb("pair_v", [P, 2 * GT, HPC, PV])
        xs = [sb(f"xs{k}", [P, HPC, S]) for k in range(2)]
        xmax = sb("xmax", [P, 2, HPC])
        xp = [sb(f"xp{k}", [P, HPC * S]) for k in range(2)]
        xpt = [sb(f"xpt{k}", [P, 4, P]) for k in range(2)]
        xinv = sb("xinv", [P, GT, H])
        xo = sb("xo", [P, GT, D])
        xot = sb("xot", [P, 2, GTOK])
        top = sb("top", [P, GT])
        gate = sb("gate", [P, GT, NE])
        gsum = sb("gsum", [P, GT])
        ginv = sb("ginv", [P, GT])
        gate_t = sb("gate_t", [NE, GTOK])

        ln_steps = sem("ln2_steps")
        dve_passed = sem("dve_passed")
        pool_passed = sem("pool_passed")
        rows_ready = sem("rows2_ready")
        cols_ready = sem("cols2_ready")
        cols_by_act = sem("cols_by_act")
        cols_by_dve = sem("cols_by_dve")
        bias_added = sem("bias_added")
        lin_ready = sem("lin_ready")
        lin_copied = sem("lin_copied")
        vals_ready = sem("vals_ready")
        vals_copied = sem("vals_copied")
        att_ready = sem("att_ready")
        att_steps = sem("att_steps")
        att_exp = sem("att_exp")
        att_turned = sem("att_turned")
        att_turned_copied = sem("att_turned_copied")
        att_mixed = sem("att_mixed")
        att_x = sem("att_x")
        x_new = sem("x_new")
        logits0_ready = sem("logits0_ready")
        logits_steps = sem("logits_steps")
        rank_steps = sem("rank_steps")
        hidden_ready = sem("hidden_ready")
        gelu_done = sem("gelu_done")
        keep_turned = sem("keep_turned")
        keep_copied = sem("keep_copied")
        spread_ready = sem("spread_ready")
        hidden_masked = sem("hidden_masked")
        ffn_ready = sem("ffn_ready")
        first_in = sem("first_in")
        pair_v_const = sem("pair_v_const")
        xq_ready = sem("xq_ready")
        xk_ready = sem("xk_ready")
        xv_ready = sem("xv_ready")
        xq_copied = sem("xq_copied")
        xk1_copied = sem("xk1_copied")
        wide0_done = sem("wide0_done")
        wide1_done = sem("wide1_done")
        pair_v_done = sem("pair_v_done")
        xs_ready = sem("xs_ready")
        xs_masked = sem("xs_masked")
        xs_max = sem("xs_max")
        xs_shifted = sem("xs_shifted")
        xp_done = sem("xp_done")
        xpt_ready = sem("xpt_ready")
        xpt_copied = sem("xpt_copied")
        xo_ready = sem("xo_ready")
        xinv_done = sem("xinv_done")
        xo_done = sem("xo_done")
        xot_ready = sem("xot_ready")
        xot_by_act = sem("xot_by_act")
        xot_by_dve = sem("xot_by_dve")
        xout_ready = sem("xout_ready")
        logits1_ready = sem("logits1_ready")
        gate_steps = sem("gate_steps")
        gate_shifted = sem("gate_shifted")
        gate_exp = sem("gate_exp")
        gate_turned = sem("gate_turned")
        gate_copied = sem("gate_copied")
        gate_bias_ready = sem("gate_bias_ready")
        expert_ready = sem("expert_ready")
        expert_added = sem("expert_added")
        stored = sem("stored")

        block = ctx.enter_context(nc.Block())
        SCALE = [float(D) ** -0.5, 1.0 / P]

        def x_tile(g, t):
            return x_res[:, bass.ds(g * GT + t, 1), :].rearrange("p a d -> p (a d)")

        def x_tiles(g, t, n):
            return x_res[:, bass.ds(g * GT + t, n), :].rearrange("p a d -> p (a d)")

        @block.sync
        def _(sp):
            def load(g):
                sp.dma_start(ctx_first[:, :, :, :], a["ctx_first"][:, bass.ds(g * 2 * GT, 2 * GT), :, :]).then_inc(first_in, 16)

            def step(g, ahead):
                if ahead:
                    sp.wait_ge(xv_ready, 4 * g + 4)
                    load(g + 1)
                sp.wait_ge(x_new, LN2 * g + LN2)
                sp.dma_start(out_dram[bass.ds(g * GTOK, GTOK), :].rearrange("(t p) d -> p t d", p=P), x_res[:, bass.ds(g * GT, GT), :]).then_inc(stored, 16)

            sp.dma_start(pair_v[:, :, :, :], a["pair_v"]).then_inc(pair_v_const, 16)
            load(0)
            with sp.Fori(0, NG - 1) as g:
                step(g, True)
            step(NG - 1, False)
            sp.wait_ge(stored, 16 * NG)

        @block.gpsimd
        def _(pool):
            with pool.Fori(0, NG) as g:
                def add_row(s, n):
                    pool.wait_ge(rows_ready, n + 1)
                    pool.sem_inc(pool_passed, 1)
                    rows = x_res[:, bass.ds(g * GT, GT), :]
                    pool.tensor_tensor(rows, rows, att_row[s][:, :].unsqueeze(1).broadcast_to([P, GT, D]), ALU.add).then_inc(bias_added, 1)

                add_row(0, LN2 * g)
                pool.wait_ge(xk1_copied, g + 1)
                pool.tensor_tensor(wide_k[1][:, :, :, :], xk1[:, :].rearrange("p (b s) -> p b s", s=S).unsqueeze(2).broadcast_to([P, 2 * GT, HPC, S]),
                                   head_mask[:, :].unsqueeze(1).unsqueeze(3).broadcast_to([P, 2 * GT, HPC, S]), ALU.mult).then_inc(wide1_done, 1)
                for n in range(SM):
                    pool.wait_ge(xs_max, SM * g + n + 1)
                    pool.tensor_tensor(xs[n % 2][:, :, :], xs[n % 2][:, :, :], xmax[:, n % 2, :].unsqueeze(2).broadcast_to([P, HPC, S]), ALU.subtract).then_inc(xs_shifted, 1)
                add_row(1, LN2 * g + 3)

        @block.scalar
        def _(act):
            with act.Fori(0, NG) as g:
                def cols(n):
                    act.wait_ge(cols_ready, 2 * n + 1)
                    act.activation(yt[:, 0, :], bank[0][:, :], ACT.Copy).then_inc(cols_by_act, 1)

                def attention(s, n):
                    cols(LN2 * g + 3 * s)
                    lins = 4 - 2 * s
                    before = 6 * g + 4 * s
                    for c in range(lins):
                        act.wait_ge(lin_ready, before + c + 1)
                        act.activation(lin[:, c, :], bank[2 + c][:, :], ACT.Identity, bias=att_b[s][:, c:c + 1]).then_inc(lin_copied, 1)
                    act.wait_ge(att_steps, ATT_STEPS * n + 3)
                    for t in range(GT):
                        last = act.activation(att_p[:, t, :], masked[:, t, :], ACT.Exp, bias=att_shift[:, t:t + 1], scale=SCALE[s], accum_out=att_sum[:, t:t + 1])
                    last.then_inc(att_exp, 1)
                    act.wait_ge(att_turned, n + 1)
                    act.activation(att_pt[:, :], bank[1][:, :], ACT.Copy).then_inc(att_turned_copied, 1)

                attention(0, 2 * g)

                cols(LN2 * g + 1)
                for c in range(HC):
                    act.wait_ge(hidden_ready, HC * g + c + 1)
                    act.activation(hidden[:, c, :], bank[3 + c % 2][:, :], ACT.Gelu).then_inc(gelu_done, 1)
                    if c == 3:
                        act.wait_ge(keep_turned, g + 1)
                        act.activation(keep_t[:, :], bank[7][0:NB0, :], ACT.Copy).then_inc(keep_copied, 1)

                cols(LN2 * g + 2)
                for c in range(2):
                    act.wait_ge(xq_ready, 2 * g + c + 1)
                    act.activation(xq[:, c, :], bank[2 + c][:, :], ACT.Copy).then_inc(xq_copied, 1)
                act.wait_ge(xk_ready, 2 * g + 2)
                act.activation(xk1[:, :], bank[5][:, :], ACT.Copy).then_inc(xk1_copied, 1)
                for n in range(SM + 1):
                    if n < SM:
                        act.wait_ge(xs_shifted, SM * g + n + 1)
                        act.activation(xp[n % 2][:, :], xs[n % 2][:, :, :].rearrange("p h s -> p (h s)"), ACT.Exp, scale=float(HD) ** -0.5).then_inc(xp_done, 1)
                    if n >= 1:
                        act.wait_ge(xpt_ready, SM * g + n)
                        act.activation(xpt[(n - 1) % 2][:, :, :].rearrange("p a q -> p (a q)"), bank[4 + (n - 1) % 2][:, :], ACT.Copy).then_inc(xpt_copied, 1)
                act.wait_ge(xot_ready, 2 * g + 1)
                act.activation(xot[:, 0, :], bank[0][:, :], ACT.Copy).then_inc(xot_by_act, 1)

                attention(1, 2 * g + 1)

                cols(LN2 * g + 4)
                act.wait_ge(gate_shifted, g + 1)
                act.activation(gate[:, :, :], gate[:, :, :], ACT.Exp).then_inc(gate_exp, 1)
                act.wait_ge(gate_turned, g + 1)
                act.activation(gate_t[:, :], bank[7][0:NE, :], ACT.Copy).then_inc(gate_copied, 1)

        @block.vector
        def _(dve):
            with dve.Fori(0, NG) as g:
                def normalised(n, first=False):
                    if not first:
                        dve.wait_ge(x_new, n)
                        dve.sem_inc(dve_passed, 1)
                    last = layernorm_rows(dve, Steps(dve, ln_steps, LN_STEPS * n), [x_tile(g, t) for t in range(GT)], [y[:, t, :] for t in range(GT)],
                                          stats, mv, half_var, root, work, passed=dve_passed)
                    last.then_inc(rows_ready, 1)
                    dve.wait_ge(cols_ready, 2 * n + 2)
                    dve.tensor_copy(yt[:, 1, :], bank[1][:, :]).then_inc(cols_by_dve, 1)

                def attention(s, n):
                    normalised(LN2 * g + 3 * s, first=(s == 0))
                    for k in range(2):
                        dve.wait_ge(vals_ready, 2 * n + k + 1)
                        dve.tensor_copy(vals[:, 2 * k:2 * k + 2, :].rearrange("p t d -> p (t d)"), bank[6 + k][:, :]).then_inc(vals_copied, 1)
                    dve.wait_ge(att_ready, n + 1)
                    steps = Steps(dve, att_steps, ATT_STEPS * n)
                    steps.then(dve.tensor_tensor(masked[:, :, :], bank[0][:, :].rearrange("p (t k) -> p t k", t=GT),
                                                 block_mask[:, :].unsqueeze(1).broadcast_to([P, GT, P]), ALU.add))
                    steps.then(dve.tensor_reduce(att_shift[:, :], masked[:, :, :], AX.X, ALU.max, negate=True))
                    steps.then(dve.tensor_scalar(att_shift[:, :], att_shift[:, :], SCALE[s], None, ALU.mult))
                    dve.wait_ge(att_exp, n + 1)
                    steps.then(dve.reciprocal(att_inv[:, :], att_sum[:, :]))
                    dve.wait_ge(bias_added, n + 1)
                    for t in range(GT):
                        if t % 2 == 0:
                            dve.wait_ge(att_mixed, 2 * n + t // 2 + 1)
                        last = dve.scalar_tensor_tensor(out=x_tile(g, t), in0=bank[2 + t // 2][:, D * (t % 2):D * (t % 2) + D], scalar=att_inv[:, t:t + 1],
                                                        in1=x_tile(g, t), op0=ALU.mult, op1=ALU.add)
                    last.then_inc(x_new, 1)

                attention(0, 2 * g)

                normalised(LN2 * g + 1)
                dve.wait_ge(logits0_ready, g + 1)
                lsteps = Steps(dve, logits_steps, g)
                lsteps.then(dve.tensor_tensor(logits[:, :, :], bank[2][:, 0:GT * NB0].rearrange("p (t n) -> p t n", n=NB0),
                                              router0_b[:, :].unsqueeze(1).broadcast_to([P, GT, NB0]), ALU.add))
                square = "p (t i j) -> p t i j"
                rank_below(dve, Steps(dve, rank_steps, 2 * RANK_STEPS * g), logits[:, :, :], NB0, tri0[:, :],
                           diff[:, :].rearrange(square, t=GT, i=NB0), order[:, :].rearrange(square, t=GT, i=NB0),
                           rank[:, :, :], keep[:, :, :], TOP0)
                for c in range(HC):
                    dve.wait_ge(spread_ready, HC * g + c + 1)
                    dve.wait_ge(gelu_done, HC * g + c + 1)
                    dve.tensor_tensor(hidden[:, c, :], bank[5 + c % 2][:, :], hidden[:, c, :], ALU.mult).then_inc(hidden_masked, 1)
                dve.wait_ge(ffn_ready, g + 1)
                for t, k in enumerate((0, 1, 2, 7)):
                    last = dve.tensor_tensor(x_tile(g, t), bank[k][:, 0:D], x_tile(g, t), ALU.add)
                last.then_inc(x_new, 1)

                normalised(LN2 * g + 2)
                dve.wait_ge(xk_ready, 2 * g + 1)
                dve.tensor_tensor(wide_k[0][:, :, :, :], bank[4][:, :].rearrange("p (b s) -> p b s", s=S).unsqueeze(2).broadcast_to([P, 2 * GT, HPC, S]),
                                  head_mask[:, :].unsqueeze(1).unsqueeze(3).broadcast_to([P, 2 * GT, HPC, S]), ALU.mult).then_inc(wide0_done, 1)
                for k in range(4):
                    dve.wait_ge(xv_ready, 4 * g + k + 1)
                    for b2 in range(2):
                        last = dve.tensor_tensor(pair_v[:, 2 * k + b2, :, 0:2 * HD], bank[(6 + k) % 8][:, D * b2:D * b2 + D].rearrange("p (a d) -> p a d", a=HPC),
                                                 pair_mask[:, :].rearrange("p (a d) -> p a d", a=HPC), ALU.mult)
                    last.then_inc(pair_v_done, 1)

                def finish(t):
                    dve.wait_ge(xo_ready, 2 * GT * g + 2 * t + 2)
                    pv = bank[6 + t % 2][:, 0:HPC * PV].rearrange("p (a v) -> p a v", v=PV)
                    dve.reciprocal(xinv[:, t, :].rearrange("p (a e) -> p a e", e=2), pv[:, :, 2 * HD:PV]).then_inc(xinv_done, 1)
                    dve.wait_ge(xinv_done, GT * g + t + 1)
                    for e in range(2):
                        last = dve.tensor_tensor(xo[:, t, :].rearrange("p (a e d) -> p a e d", e=2, d=HD)[:, :, e, :], pv[:, :, HD * e:HD * e + HD],
                                                 xinv[:, t, e::2].unsqueeze(2).broadcast_to([P, HPC, HD]), ALU.mult)
                    last.then_inc(xo_done, 1)

                for n in range(SM):
                    dve.wait_ge(xs_ready, SM * g + n + 1)
                    if n >= 2:
                        dve.wait_ge(xp_done, SM * g + n - 1)
                    dve.tensor_tensor(xs[n % 2][:, :, :], bank[2 + n % 2][:, :].rearrange("p (h s) -> p h s", s=S),
                                      causal[:, :].unsqueeze(1).broadcast_to([P, HPC, S]), ALU.add).then_inc(xs_masked, 1)
                    dve.wait_ge(xs_masked, SM * g + n + 1)
                    dve.tensor_reduce(xmax[:, n % 2, :], xs[n % 2][:, :, :], AX.X, ALU.max).then_inc(xs_max, 1)
                    if n >= 4 and n % 2 == 0:
                        finish(n // 2 - 2)
                finish(GT - 2)
                finish(GT - 1)
                dve.wait_ge(xot_ready, 2 * g + 2)
                dve.tensor_copy(xot[:, 1, :], bank[1][:, :]).then_inc(xot_by_dve, 1)
                for k in range(2):
                    dve.wait_ge(xout_ready, 2 * g + k + 1)
                    last = dve.tensor_tensor(x_tiles(g, 2 * k, 2), bank[2 + k][:, :], x_tiles(g, 2 * k, 2), ALU.add)
                last.then_inc(x_new, 1)

                attention(1, 2 * g + 1)

                normalised(LN2 * g + 4)
                dve.wait_ge(logits1_ready, g + 1)
                steps = Steps(dve, gate_steps, GATE_STEPS * g)
                lg = logits[:, :, 0:NE]
                steps.then(dve.tensor_copy(lg, bank[2][:, 0:GT * NE].rearrange("p (t n) -> p t n", n=NE)))
                steps.then(dve.tensor_reduce(top[:, :], lg, AX.X, ALU.max))
                dve.tensor_tensor(gate[:, :, :], lg, top[:, :].unsqueeze(2).broadcast_to([P, GT, NE]), ALU.subtract).then_inc(gate_shifted, 1)
                n2 = GT * NE * NE
                rank_below(dve, Steps(dve, rank_steps, 2 * RANK_STEPS * g + RANK_STEPS), lg, NE, tri1[:, :],
                           diff[:, 0:n2].rearrange(square, t=GT, i=NE), order[:, 0:n2].rearrange(square, t=GT, i=NE),
                           rank[:, :, 0:NE], keep[:, :, 0:NE], TOP1)
                dve.wait_ge(gate_exp, g + 1)
                steps.then(dve.tensor_tensor(gate[:, :, :], gate[:, :, :], keep[:, :, 0:NE], ALU.mult))
                steps.then(dve.tensor_reduce(gsum[:, :], gate[:, :, :], AX.X, ALU.add))
                steps.then(dve.reciprocal(ginv[:, :], gsum[:, :]))
                steps.then(dve.tensor_tensor(gate[:, :, :], gate[:, :, :], ginv[:, :].unsqueeze(2).broadcast_to([P, GT, NE]), ALU.mult))
                for t in range(GT):
                    for e in range(NE):
                        m = NE * t + e
                        if e % 2 == 0:
                            dve.wait_ge(expert_ready, GT * NE // 2 * g + m // 2 + 1)
                        if e > 0:
                            dve.wait_ge(expert_added, GT * NE * g + m)
                        dve.scalar_tensor_tensor(out=x_tile(g, t), in0=bank[3 + e // 2][:, D * (e % 2):D * (e % 2) + D], scalar=gate[:, t, e:e + 1],
                                                 in1=x_tile(g, t), op0=ALU.mult, op1=ALU.add).then_inc(expert_added, 1)
                dve.wait_ge(expert_added, GT * NE * (g + 1))
                dve.wait_ge(gate_bias_ready, g + 1)
                for k in range(2):
                    last = dve.tensor_tensor(x_tiles(g, 2 * k, 2), bank[k][:, :], x_tiles(g, 2 * k, 2), ALU.add)
                last.then_inc(x_new, 1)

        @block.tensor
        def _(pe):
            with pe.Fori(0, NG) as g:
                def tile(t):
                    return slice(P * t, P * t + P)

                def cols(n):
                    pe.wait_ge(rows_ready, n + 1)
                    for c in range(2):
                        for t in range(GT):
                            last = pe.transpose(bank[c][:, tile(t)], y[:, t, P * c:P * c + P], ident[:, :])
                        last.then_inc(cols_ready, 1)
                    pe.wait_ge(cols_by_act, n + 1)
                    pe.wait_ge(cols_by_dve, n + 1)

                def attention(s, n):
                    cols(LN2 * g + 3 * s)
                    lins = 4 - 2 * s
                    for c in range(lins):
                        for k in range(2):
                            last = pe.matmul(bank[2 + c][:, :], att_w[s][:, k, c, :], yt[:, k, :], start=(k == 0), stop=(k == 1))
                        last.then_inc(lin_ready, 1)
                    for t in range(GT):
                        for k in range(2):
                            last = pe.matmul(bank[6 + t // 2][:, D * (t % 2):D * (t % 2) + D], yt[:, k, tile(t)], att_vo[s][:, k, :], start=(k == 0), stop=(k == 1))
                        if t % 2:
                            last.then_inc(vals_ready, 1)
                    pe.wait_ge(lin_copied, 6 * g + 4 * s + lins)
                    parts = lins // 2
                    for t in range(GT):
                        for k in range(parts):
                            last = pe.matmul(bank[0][:, tile(t)], lin[:, k, tile(t)], lin[:, parts + k, tile(t)], start=(k == 0), stop=(k == parts - 1))
                    last.then_inc(att_ready, 1)
                    pe.wait_ge(att_exp, n + 1)
                    for t in range(GT):
                        last = pe.transpose(bank[1][:, tile(t)], att_p[:, t, :], ident[:, :])
                    last.then_inc(att_turned, 1)
                    pe.wait_ge(att_turned_copied, n + 1)
                    pe.wait_ge(vals_copied, 2 * n + 2)
                    for t in range(GT):
                        last = pe.matmul(bank[2 + t // 2][:, D * (t % 2):D * (t % 2) + D], att_pt[:, tile(t)], vals[:, t, :], start=True, stop=True)
                        if t % 2:
                            last.then_inc(att_mixed, 1)

                attention(0, 2 * g)

                cols(LN2 * g + 1)
                for t in range(GT):
                    for k in range(2):
                        last = pe.matmul(bank[2][:, NB0 * t:NB0 * t + NB0], yt[:, k, tile(t)], router0[:, k, :], start=(k == 0), stop=(k == 1))
                last.then_inc(logits0_ready, 1)

                def hidden_chunk(c):
                    if c >= 2:
                        pe.wait_ge(gelu_done, HC * g + c - 1)
                    for k in range(2):
                        last = pe.matmul(bank[3 + c % 2][:, :], w1[:, k, P * c:P * c + P], yt[:, k, :], start=(k == 0), stop=(k == 1))
                    last.then_inc(hidden_ready, 1)

                def hidden_out(c):
                    pe.wait_ge(hidden_masked, HC * g + c + 1)
                    for t, k in enumerate((0, 1, 2, 7)):
                        last = pe.matmul(bank[k][:, 0:D], hidden[:, c, tile(t)], w2[:, c, :], start=(c == 0), stop=(c == HC - 1))
                    if c == HC - 1:
                        last.then_inc(ffn_ready, 1)

                for c in range(4):
                    hidden_chunk(c)
                pe.wait_ge(rank_steps, 2 * RANK_STEPS * g + RANK_STEPS)
                for t in range(GT):
                    last = pe.transpose(bank[7][0:NB0, tile(t)], keep[:, t, :], ident[:, :])
                last.then_inc(keep_turned, 1)
                pe.wait_ge(keep_copied, g + 1)
                for c in range(HC):
                    if c >= 2:
                        pe.wait_ge(hidden_masked, HC * g + c - 1)
                    pe.matmul(bank[5 + c % 2][:, :], spread[:, c, :], keep_t[:, :], start=True, stop=True).then_inc(spread_ready, 1)
                    if c + 4 < HC:
                        hidden_chunk(c + 4)
                    if c >= 1:
                        hidden_out(c - 1)
                hidden_out(HC - 1)

                cols(LN2 * g + 2)
                for c in range(2):
                    for k in range(2):
                        last = pe.matmul(bank[2 + c][:, :], x_wq[:, k, P * c:P * c + P], yt[:, k, :], start=(k == 0), stop=(k == 1))
                    last.then_inc(xq_ready, 1)
                pe.wait_ge(first_in, 16 * g + 16)
                for c in range(2):
                    pe.matmul(bank[4 + c][:, :], x_wk[:, P * c:P * c + P], ctx_first[:, :, 0, :], start=True, stop=True).then_inc(xk_ready, 1)
                for k in range(4):
                    for b2 in range(2):
                        last = pe.matmul(bank[(6 + k) % 8][:, D * b2:D * b2 + D], ctx_first[:, 2 * k + b2, :, :].rearrange("p e s -> p (e s)"), x_wv[:, :],
                                         start=True, stop=True)
                    last.then_inc(xv_ready, 1)
                pe.wait_ge(xq_copied, 2 * g + 2)
                pe.wait_ge(wide0_done, g + 1)
                pe.wait_ge(wide1_done, g + 1)
                pe.wait_ge(pair_v_done, 4 * g + 4)
                for n in range(SM + 2):
                    if n < SM:
                        t, c = divmod(n, 2)
                        if n >= 2:
                            pe.wait_ge(xs_masked, SM * g + n - 1)
                        for b2 in range(2):
                            last = pe.matmul(bank[2 + n % 2][S * b2:S * b2 + S, :], xq[:, c, P * t + S * b2:P * t + S * b2 + S],
                                             wide_k[c][:, 2 * t + b2, :, :].rearrange("p h s -> p (h s)"), start=True, stop=True)
                        last.then_inc(xs_ready, 1)
                    if 1 <= n <= SM:
                        m = n - 1
                        pe.wait_ge(xp_done, SM * g + m + 1)
                        if m >= 2:
                            pe.wait_ge(xpt_copied, SM * g + m - 1)
                        for a2 in range(4):
                            last = pe.transpose(bank[4 + m % 2][:, tile(a2)], xp[m % 2][:, tile(a2)], ident[:, :])
                        last.then_inc(xpt_ready, 1)
                    if n >= 2:
                        m = n - 2
                        t, c = divmod(m, 2)
                        pe.wait_ge(xpt_copied, SM * g + m + 1)
                        if t >= 2 and c == 0:
                            pe.wait_ge(xo_done, GT * g + t - 1)
                        for a2 in range(4):
                            pair = 4 * c + a2
                            for b2 in range(2):
                                last = pe.matmul(bank[6 + t % 2][S * b2:S * b2 + S, PV * pair:PV * pair + PV], xpt[m % 2][:, a2, S * b2:S * b2 + S],
                                                 pair_v[:, 2 * t + b2, pair, :], start=True, stop=True)
                        last.then_inc(xo_ready, 1)
                pe.wait_ge(xo_done, GT * g + GT)
                for c in range(2):
                    for t in range(GT):
                        last = pe.transpose(bank[c][:, tile(t)], xo[:, t, P * c:P * c + P], ident[:, :])
                    last.then_inc(xot_ready, 1)
                pe.wait_ge(xot_by_act, g + 1)
                pe.wait_ge(xot_by_dve, g + 1)
                for t in range(GT):
                    for k in range(2):
                        last = pe.matmul(bank[2 + t // 2][:, D * (t % 2):D * (t % 2) + D], xot[:, k, tile(t)], x_wo[:, k, :], start=(k == 0), stop=(k == 1))
                    if t % 2:
                        last.then_inc(xout_ready, 1)

                attention(1, 2 * g + 1)

                cols(LN2 * g + 4)
                for t in range(GT):
                    for k in range(2):
                        last = pe.matmul(bank[2][:, NE * t:NE * t + NE], yt[:, k, tile(t)], router1[:, k, :], start=(k == 0), stop=(k == 1))
                last.then_inc(logits1_ready, 1)
                for t in range(GT):
                    for e2 in range(NE // 2):
                        if t > 0:
                            pe.wait_ge(expert_added, GT * NE * g + NE * (t - 1) + 2 * e2 + 2)
                        for k in range(2):
                            last = pe.matmul(bank[3 + e2][:, :], yt[:, k, tile(t)], experts[:, k, 2 * e2:2 * e2 + 2, :].rearrange("p e d -> p (e d)"),
                                             start=(k == 0), stop=(k == 1))
                        last.then_inc(expert_ready, 1)
                    if t == 0:
                        pe.wait_ge(gate_steps, GATE_STEPS * g + GATE_STEPS)
                        for t1 in range(GT):
                            last = pe.transpose(bank[7][0:NE, tile(t1)], gate[:, t1, :], ident[:, :])
                        last.then_inc(gate_turned, 1)
                        pe.wait_ge(gate_copied, g + 1)
                        for t1 in range(GT):
                            last = pe.matmul(bank[t1 // 2][:, D * (t1 % 2):D * (t1 % 2) + D], gate_t[:, tile(t1)], expert_b[:, :], start=True, stop=True)
                        last.then_inc(gate_bias_ready, 1)


def fold_values(nc, a, bank, att_vo, att_row, loads):
    with ExitStack() as ctx:
        def sb(name, shape, dt=F32):
            return ctx.enter_context(nc.sbuf_tensor(name, shape, dt))

        def sem(name):
            return ctx.enter_context(nc.semaphore(name))

        wv0 = sb("wv0", [P, 2, D])
        wo0 = sb("wo0", [P, 2, D])
        bv0 = sb("bv0", [P, 2, P])
        bo0 = sb("bo0", [P, D])
        wv1 = sb("wv1", [P, D])
        wo1 = sb("wo1", [P, H, D])
        bv1 = sb("bv1", [P, P])
        bo1 = sb("bo1", [P, D])
        wo1_sum = sb("wo1_sum", [P, D])
        own_in = sem("own_in")
        weights_in = sem("weights2_in")
        heads_summed = sem("heads_summed")
        joined = sem("joined")
        joined_copied = sem("joined_copied")
        rows_made = sem("rows_made")
        block = ctx.enter_context(nc.Block())
        own = [(wv0[:, :, :], "wv0"), (wo0[:, :, :], "wo0"), (bv0[:, :, :], "bv0"), (bo0[:, :], "bo0"),
               (wv1[:, :], "wv1"), (wo1[:, :, :], "wo1"), (bv1[:, :], "bv1"), (bo1[:, :], "bo1")]

        @block.sync
        def _(sp):
            for dst, name in own:
                sp.dma_start(dst, a[name]).then_inc(own_in, 16)
            for dst, name in loads:
                sp.dma_start(dst, a[name]).then_inc(weights_in, 16)
            sp.wait_ge(weights_in, 16 * len(loads))

        @block.tensor
        def _(pe):
            pe.wait_ge(own_in, 16 * len(own))
            for c in range(2):
                for k in range(2):
                    last = pe.matmul(bank[0][:, D * c:D * c + D], wv0[:, k, P * c:P * c + P], wo0[:, k, :], start=(k == 0), stop=(k == 1))
            last.then_inc(joined, 1)
            for k in range(2):
                last = pe.matmul(bank[1][:, 0:D], bv0[:, k, :], wo0[:, k, :], start=(k == 0), stop=(k == 1))
            last.then_inc(joined, 1)
            pe.wait_ge(heads_summed, 1)
            for c in range(2):
                last = pe.matmul(bank[2][:, D * c:D * c + D], wv1[:, P * c:P * c + P], wo1_sum[:, :], start=True, stop=True)
            last.then_inc(joined, 1)
            pe.matmul(bank[3][:, 0:D], bv1[:, :], wo1_sum[:, :], start=True, stop=True).then_inc(joined, 1)

        @block.scalar
        def _(act):
            for s in range(2):
                act.wait_ge(joined, 2 * s + 1)
                act.activation(att_vo[s][:, :, :].rearrange("p k d -> p (k d)"), bank[2 * s][:, :], ACT.Copy).then_inc(joined_copied, 1)

        @block.vector
        def _(dve):
            dve.wait_ge(own_in, 16 * len(own))
            dve.tensor_reduce(wo1_sum[:, :], wo1[:, :, :].rearrange("p h d -> p d h"), AX.X, ALU.add).then_inc(heads_summed, 1)
            for s, bo in enumerate((bo0, bo1)):
                dve.wait_ge(joined, 2 * s + 2)
                dve.tensor_tensor(att_row[s][:, :], bank[2 * s + 1][:, 0:D], bo[:, :], ALU.add).then_inc(rows_made, 1)


def bass_perceiver_two_layers(nc, a, out):
    with ExitStack() as ctx:
        x_res = ctx.enter_context(nc.sbuf_tensor("x_res", [P, NT, D], F32))
        ident = ctx.enter_context(nc.sbuf_tensor("ident", [P, P], F32))
        part_one(nc, a, x_res, ident)
        part_two(nc, a, out, x_res, ident)


def _layouts(i):
    import numpy as np

    c = np.ascontiguousarray
    f = np.float32
    pos = np.concatenate([np.arange(FULL_P * KT).reshape(FULL_P, KT),
                          np.arange(L - (P - FULL_P) * KT, L).reshape(P - FULL_P, KT)])
    inv = (f(1.0) / (f(10000.0) ** (np.arange(0, DC, 2, dtype=f) / f(DC)))).astype(f)
    freqs = (pos[:, :, None].astype(f) * inv).astype(f)
    sin = np.repeat(np.sin(freqs), 2, axis=-1).astype(f)
    cos = np.repeat(np.cos(freqs), 2, axis=-1).astype(f)
    sin[:, :, :DC // 2] *= -1
    repeated = np.zeros((P, KT), bool)
    repeated[FULL_P:] = pos[FULL_P:] < FULL_P * KT
    k_rows = np.zeros((P - DC, KT, P), np.float16)
    k_rows[0:2] = 1
    k_rows[2] = np.where(repeated.T, -30000.0, 0.0)
    q_rows = np.zeros((P - DC, H, S), np.float16)
    q_rows[2] = 1
    out = {
        "x": i["x"].reshape(TOK, D), "ctx": i["ctx_512"],
        "cos": cos, "sin": sin, "k_rows": k_rows.reshape(P - DC, KEYS), "q_rows": q_rows,
        "pick": np.broadcast_to(np.eye(QT, dtype=f)[None], (P, QT, QT)),
        "unpick": np.concatenate([np.broadcast_to(np.eye(QT, dtype=f)[:, :, None], (QT, QT, P)), np.zeros((P - QT, QT, P), f)]),
        "ident": np.eye(P, dtype=f), "ident16": np.eye(P, dtype=np.float16),
        "wq": i["L0_xattn_Wq"].reshape(H, P, D).transpose(1, 0, 2),
        "wkc": i["L0_xattn_w_kc_q"].reshape(H, P, 2, 96).transpose(3, 2, 0, 1),
        "wqr": i["L0_xattn_W_qr"].transpose(2, 0, 1), "wkr": i["L0_xattn_W_kr"].transpose(2, 0, 1),
        "wkv": i["L0_xattn_w_kc_kv"].transpose(1, 0, 2),
        "wo": i["L0_xattn_Wo"].reshape(D, H, P).transpose(2, 1, 0),
    }
    tok = np.arange(P)
    tri = lambda n: np.broadcast_to((np.arange(n)[None, :] < np.arange(n)[:, None]).astype(f).reshape(1, n * n), (P, n * n))
    rows = lambda v: np.broadcast_to(v[None, :], (P, v.shape[0]))
    chunks = lambda w: w.reshape(2, P, -1).transpose(1, 0, 2)
    spread = np.zeros((NB0, HC, P), np.float16)
    spread[(np.arange(HF) // (HF // NB0)), np.arange(HF) // P, np.arange(HF) % P] = 1
    pair_v = np.zeros((P, 2 * GT, HPC, PV), f)
    pair_v[:S, :, :, 2 * HD] = 1
    pair_v[S:, :, :, 2 * HD + 1] = 1
    w_qkv, b_qkv = i["L0_attn_w_qkv"], i["L0_attn_b_qkv"]
    first = i["ctx_512"][:, :S, :].transpose(2, 0, 1)
    out |= {
        "att0_w": w_qkv[:2 * D].reshape(4, P, 2, P).transpose(3, 2, 0, 1), "att0_b": b_qkv[:2 * D].reshape(4, P).T,
        "att1_w": np.stack([i["L1_attn_Wv"], i["L1_attn_Wk"]]).reshape(2, 2, P, P).transpose(2, 1, 0, 3),
        "att1_b": np.stack([i["L1_attn_bv"], i["L1_attn_bk"]], axis=1),
        "wv0": w_qkv[2 * D:].reshape(2, P, D).transpose(1, 0, 2), "wo0": chunks(i["L0_attn_w_out"].T),
        "bv0": np.broadcast_to(b_qkv[2 * D:].reshape(2, P).T[:, :, None], (P, 2, P)), "bo0": rows(i["L0_attn_b_out"]),
        "wv1": i["L1_attn_Wv"].T, "wo1": i["L1_attn_Wo"].reshape(H, P, D).transpose(1, 0, 2),
        "bv1": np.broadcast_to(i["L1_attn_bv"][:, None], (P, P)), "bo1": rows(i["L1_attn_bo"]),
        "router0": chunks(i["L0_ffn_Wr"].T), "router0_b": rows(i["L0_ffn_br"]),
        "w1": chunks(i["L0_ffn_W1"].T), "w2": i["L0_ffn_W2"].T.reshape(HC, P, D).transpose(1, 0, 2),
        "x_wq": chunks(i["L1_xattn_Wq"].T), "x_wk": i["L1_xattn_Wkv_expand"][:D].T, "x_wv": i["L1_xattn_Wkv_expand"][D:].T,
        "x_wo": chunks(i["L1_xattn_Wout"].T),
        "router1": chunks(i["L1_ffn_Wr"]), "experts": i["L1_ffn_We"].reshape(NE, 2, P, D).transpose(2, 1, 0, 3), "expert_b": i["L1_ffn_be"],
        "block_mask": np.where((tok[:, None] // S) == (tok[None, :] // S), 0.0, -1e30).astype(f),
        "causal": np.where(np.arange(S)[None, :] <= (tok % S)[:, None], 0.0, -1e30).astype(f),
        "head_mask": ((tok[:, None] // HD) == np.arange(HPC)[None, :]).astype(f),
        "pair_mask": ((np.arange(D)[None, :] // HD % 2) == (tok[:, None] // S)).astype(f),
        "tri0": tri(NB0), "tri1": tri(NE), "spread": spread, "pair_v": pair_v,
        "ctx_first": np.stack([first, first], axis=2),
    }
    return {k: c(v) for k, v in out.items()}


def kernel(**inputs):
    import numpy as _np
    import concourse.bacc as _bacc
    from concourse import mybir as _mybir
    from concourse.bass_utils import run_bass_kernel_spmd as _run

    nc = _bacc.Bacc("TRN2", target_bir_lowering=False, num_devices=1)
    arrays, args = {}, {}
    for name, v in _layouts({k: _np.asarray(v) for k, v in inputs.items()}).items():
        arrays[f"in_{name}"] = v
        args[name] = nc.dram_tensor(f"in_{name}", v.shape, _mybir.dt.from_np(v.dtype), kind="ExternalInput").ap()
    out = nc.dram_tensor("out", (TOK, D), _mybir.dt.float32, kind="ExternalOutput").ap()
    bass_perceiver_two_layers(nc, args, out)
    r = _run(nc, [arrays], core_ids=[0])
    return r.results[0]["out"].reshape(B, S, D)
```

```python
from contextlib import ExitStack

import concourse.bass as bass
from concourse import mybir

ALU = mybir.AluOpType
ACT = mybir.ActivationFunctionType
AX = mybir.AxisListType
F32 = mybir.dt.float32
F16 = mybir.dt.float16
I32 = mybir.dt.int32

P = 128
B, S, D = 32, 64, 256
L, DC = 1601, 64
H = 16
TOK = B * S
NT = TOK // P
KT = -(-L // P)
KEYS = KT * P
FULL_P = L // KT
QC = H * S
HH = H // 2
UNITS = 2 * KT
CH = 416
NCH = KEYS // CH
QT = QC // P
MAXES = QT * NCH
MR = 3
RING = 7
GT = 4
NG = NT // GT
GTOK = GT * P
EPS = 1e-5


FIRST_U = (6, 7)
LAST_U = 22
TURN_U = (2, 3)
SUMS_U, SPREAD_U, OUT_U = 8, 11, 15


SLOTS = [[(u, place) for u in range(FIRST_U[j], LAST_U + 1) for place in range(2) if place == 0 or u % 2 == 1] for j in range(2)]


def chunks_in(j, u, place):
    return [n for n in range(MAXES) if SLOTS[j][n * len(SLOTS[j]) // MAXES] == (u, place)]


class Steps:

    def __init__(self, engine, sem, base=0):
        self.engine, self.sem, self.base, self.n = engine, sem, base, 0

    def then(self, instruction, passed=None):
        instruction.then_inc(self.sem, 1)
        self.n += 1
        self.engine.wait_ge(self.sem, self.base + self.n)
        if passed:
            self.engine.sem_inc(passed, 1)


LN_STEPS = 14


def layernorm_rows(dve, steps, x_tiles, out_tiles, stats, mv, half_var, root, work, passed=None):
    n = len(x_tiles)
    for t in range(n - 1):
        dve.bn_stats(stats[:, t, :], x_tiles[t])
    steps.then(dve.bn_stats(stats[:, n - 1, :], x_tiles[n - 1]), passed)
    for t in range(n - 1):
        dve.bn_aggr(mv[:, t, :], stats[:, t, :])
    steps.then(dve.bn_aggr(mv[:, n - 1, :], stats[:, n - 1, :]))
    v = mv[:, 0:n, 1]
    dve.tensor_scalar(half_var[:, 0:n], v, EPS, -0.5, ALU.add, ALU.mult)
    steps.then(dve.tensor_scalar(work[:, 0:n], v, EPS, None, ALU.add))
    steps.then(dve.tensor_scalar(root[:, 0:n].bitcast(I32), work[:, 0:n].bitcast(I32), 1, None, ALU.logical_shift_right))
    steps.then(dve.tensor_scalar(root[:, 0:n].bitcast(I32), root[:, 0:n].bitcast(I32), -1.0, float(0x5F3759DF), ALU.mult, ALU.add))
    for _ in range(3):
        steps.then(dve.tensor_tensor(work[:, 0:n], root[:, 0:n], root[:, 0:n], ALU.mult))
        steps.then(dve.tensor_tensor(work[:, 0:n], work[:, 0:n], half_var[:, 0:n], ALU.mult))
        steps.then(dve.scalar_tensor_tensor(out=root[:, 0:n], in0=work[:, 0:n], scalar=1.5, in1=root[:, 0:n], op0=ALU.add, op1=ALU.mult))
    for t in range(n):
        last = dve.tensor_scalar(out_tiles[t], x_tiles[t], mv[:, t, 0:1], root[:, t:t + 1], ALU.subtract, ALU.mult)
    return last


def part_one(nc, a, x_res, ident):
    with ExitStack() as ctx:
        def sb(name, shape, dt=F32):
            return ctx.enter_context(nc.sbuf_tensor(name, shape, dt))

        def sem(name):
            return ctx.enter_context(nc.semaphore(name))

        to_query = sb("to_query", [P, 2, H, DC])
        to_out = sb("to_out", [P, HH, D])
        y_cols = sb("y_cols", [P, 2, TOK])
        fold(nc, a, x_res, ident, to_query, to_out, y_cols)

        cos = sb("cos", [P, KT, DC])
        sin = sb("sin", [P, KT, DC])
        raw = [sb(f"raw{j}", [P, KT, DC]) for j in range(2)]
        turned = sb("turned", [P, KT, DC])
        kv_pair = sb("kv_pair", [P, KT, 2, DC])
        kv = [sb(f"kv{j}", [P, KT, DC]) for j in range(2)]
        k_high = [sb(f"k_high{j}", [P, KEYS], F16) for j in range(2)]
        k_low = [sb(f"k_low{j}", [P, KEYS], F16) for j in range(2)]
        q_both = [sb(f"q_both{j}", [P, H, S], F16) for j in range(2)]
        q_shift = [sb(f"q_shift{j}", [P, H, S], F16) for j in range(2)]
        q_hi = sb("q_hi", [P, H // 2, P], F16)
        q_lo = sb("q_lo", [P, H // 2, P], F16)
        ident16 = sb("ident16", [P, P], F16)
        pick = sb("pick", [P, QT, QT])
        unpick = sb("unpick", [P, QT // 2, P])
        maxes = sb("maxes", [P, QT, NCH])
        neg_max = sb("neg_max", [P, QT])
        neg_max2 = sb("neg_max2", [P, QT, 2], F16)
        probs = [sb(f"probs{r}", [P, 2, 512]) for r in range(RING)]
        sums = [sb(f"sums{j}", [P, 2, 512]) for j in range(2)]
        held = sb("held", [P, 512])
        inv = sb("inv", [P, P])
        mixed = sb("mixed", [P, HH, 2, S])

        s_bank = [ctx.enter_context(nc.psum_tensor(f"s_bank{k}", [P, 512], F32)) for k in range(2)]
        m_bank = [ctx.enter_context(nc.psum_tensor(f"m_bank{k}", [P, 512], F32)) for k in range(MR)]
        v_bank = ctx.enter_context(nc.psum_tensor("v_bank", [P, 512], F32))
        w_bank = [ctx.enter_context(nc.psum_tensor(f"w_bank{k}", [P, 512], F32)) for k in range(2)]

        consts_in = sem("consts_in")
        keys_in = [sem(f"keys_in{j}") for j in range(2)]
        rope_products = sem("rope_products")
        rope_done = sem("rope_done")
        const_made = sem("const_made")
        query_ready = sem("query_ready")
        query_high = sem("query_high")
        query_low = sem("query_low")
        stacked = sem("stacked")
        turned_ready = sem("turned_ready")
        key_high = sem("key_high")
        key_low = sem("key_low")
        chunk_ready = sem("chunk_ready")
        chunk_max = sem("chunk_max")
        max_steps = sem("max_steps")
        shift_known = sem("shift_known")
        shift_ready = sem("shift_ready")
        shift_placed = sem("shift_placed")
        score_ready = sem("score_ready")
        exp_done = sem("exp_done")
        value_done = sem("value_done")
        held_done = sem("held_done")
        sum_added = sem("sum_added")
        sum_ready = sem("sum_ready")
        inverted = sem("inverted")
        spread_ready = sem("spread_ready")
        doubled = sem("doubled")
        kv_filled = sem("kv_filled")
        norm_done = sem("norm_done")
        out_ready = sem("out_ready")
        x_added = sem("x_added")

        block = ctx.enter_context(nc.Block())

        def walk(engine, first, step):
            first()
            step(0, True, False)
            with engine.Fori(1, NT - 1) as i:
                step(i, False, False)
            step(NT - 1, False, True)

        @block.sync
        def _(sp):
            sp.dma_start(cos[:, :, :], a["cos"]).then_inc(consts_in, 16)
            sp.dma_start(sin[:, :, :], a["sin"]).then_inc(consts_in, 16)
            sp.dma_start(ident16[:, :], a["ident16"]).then_inc(consts_in, 16)
            sp.dma_start(pick[:, :, :], a["pick"]).then_inc(consts_in, 16)
            sp.dma_start(unpick[:, :, :], a["unpick"]).then_inc(consts_in, 16)
            for j in range(2):
                sp.dma_start(k_low[j][DC:P, :], a["k_rows"]).then_inc(consts_in, 16)
                sp.dma_start(q_shift[j][DC:P, :, :], a["q_rows"]).then_inc(consts_in, 16)

            def load(b, j):
                src = a["ctx"][bass.ds(b, 1), :, :].rearrange("a l d -> (a l) d")
                sp.dma_start(raw[j][0:FULL_P, :, :], src[0:FULL_P * KT, :].rearrange("(p t) d -> p t d", t=KT)).then_inc(keys_in[j], 16)
                sp.dma_start(raw[j][FULL_P:P, :, :], src[L - (P - FULL_P) * KT:L, :].rearrange("(p t) d -> p t d", t=KT)).then_inc(keys_in[j], 16)

            def first():
                load(0, 0)
                load(1, 1)

            def step(i, is_first, is_last):
                for j in range(2):
                    if not is_last:
                        sp.wait_ge(rope_done, 2 * i + j + 1)
                        load(2 * i + j + 2, j)

            walk(sp, first, step)

        @block.gpsimd
        def _(pool):
            def step(i, is_first, is_last):
                for j in range(2):
                    b = 2 * i + j
                    for k in range(1, KT):
                        pool.wait_ge(exp_done, UNITS * b + 2 * k + 2)
                        if k == 1:
                            if not is_first:
                                pool.wait_ge(sum_ready, b - 1)
                            before = probs[0]
                        else:
                            pool.wait_ge(sum_added, (KT - 1) * b + k - 1)
                            before = sums[j]
                        pool.tensor_tensor(sums[j][:, :, :], before[:, :, :], probs[k % RING][:, :, :], ALU.add).then_inc(sum_added, 1)

            walk(pool, lambda: None, step)

        @block.scalar
        def _(act):
            def query_copy(tile):
                for piece in range(2):
                    act.wait_ge(query_ready, 2 * tile + piece + 1)
                    if not (isinstance(tile, int) and tile == 0):
                        act.wait_ge(stacked, 2 * tile)
                    act.activation(q_hi[:, 4 * piece:4 * piece + 4, :].rearrange("p a t -> p (a t)"), w_bank[piece][:, :], ACT.Copy).then_inc(query_high, 1)

            def key_copy(b, j, n):
                w = min(4 * P, KEYS - 512 * n)
                act.wait_ge(turned_ready, 4 * b + n + 1)
                act.activation(k_high[j][:, 512 * n:512 * n + w], w_bank[n % 2][:, 0:w], ACT.Copy).then_inc(key_high, 1)

            def double(b, j):
                act.wait_ge(rope_done, b + 1)
                act.activation(kv_pair[:, :, 1, :], kv_pair[:, :, 0, :], ACT.Copy).then_inc(doubled, 1)

            def fill_kv(b, j, first_use=False):
                if not first_use:
                    act.wait_ge(value_done, KT * (b - 1))
                act.activation(kv[j][:, :, :], kv_pair[:, :, 0, :], ACT.Copy).then_inc(kv_filled, 1)

            def shift_copy(b, j):
                for c in range(2):
                    act.wait_ge(shift_ready, 2 * b + c + 1)
                    act.activation(q_shift[j][DC:DC + 2, 8 * c:8 * c + 8, :].rearrange("p h s -> p (h s)"), w_bank[c][0:2, :], ACT.Copy).then_inc(shift_placed, 1)

            def first():
                act.wait_ge(consts_in, 16 * 9)
                query_copy(0)
                double(0, 0)
                fill_kv(0, 0, first_use=True)
                for n in range(4):
                    key_copy(0, 0, n)
                shift_copy(0, 0)

            def step(i, is_first, is_last):
                for j in range(2):
                    b = 2 * i + j
                    ahead = not (is_last and j == 1)
                    if ahead:
                        double(b + 1, 1 - j)
                    for u in range(UNITS):
                        k, half = divmod(u, 2)
                        act.wait_ge(score_ready, UNITS * b + u + 1)
                        if half == 0 and not (is_first and j == 0 and k < RING):
                            last = k - RING
                            batch = b
                            if last < 0:
                                last = max(t for t in range(k, KT, RING))
                                batch = b - 1
                            act.wait_ge(value_done, KT * batch + last + 1)
                            act.wait_ge(sum_added, (KT - 1) * batch + max(last, 1))
                        act.activation(probs[k % RING][:, half, :], s_bank[u % 2][:, :], ACT.Exp).then_inc(exp_done, 1)
                        if ahead:
                            if j == 1 and u == 1:
                                query_copy(i + 1)
                            if u == 1:
                                fill_kv(b + 1, 1 - j, first_use=is_first and j == 0)
                            if u == 24:
                                shift_copy(b + 1, 1 - j)
                            if 0 <= u - TURN_U[j] < 4:
                                key_copy(b + 1, 1 - j, u - TURN_U[j])
                    act.wait_ge(value_done, KT * (b + 1))
                    if not (is_first and j == 0):
                        act.wait_ge(norm_done, b)
                    act.activation(held[:, :], v_bank[:, :], ACT.Copy).then_inc(held_done, 1)

            walk(act, first, step)

        @block.vector
        def _(dve):
            def rope(b, j):
                dve.wait_ge(keys_in[j], 32 * ((b - j) // 2 + 1) if isinstance(b, int) else 16 * (b - j) + 32)
                if not (isinstance(b, int) and b == 0):
                    dve.wait_ge(turned_ready, 4 * b)
                    dve.wait_ge(kv_filled, b)
                dve.tensor_tensor(kv_pair[:, :, 0, :], raw[j][:, :, :], cos[:, :, :], ALU.mult).then_inc(rope_products, 1)
                dve.tensor_tensor(turned[:, :, 0:32], raw[j][:, :, 32:64], sin[:, :, 0:32], ALU.mult).then_inc(rope_products, 1)
                dve.tensor_tensor(turned[:, :, 32:64], raw[j][:, :, 0:32], sin[:, :, 32:64], ALU.mult).then_inc(rope_products, 1)
                dve.wait_ge(rope_products, 3 * b + 3)
                dve.tensor_tensor(kv_pair[:, :, 0, :], kv_pair[:, :, 0, :], turned[:, :, :], ALU.add).then_inc(rope_done, 1)

            def query_lows(tile):
                for piece in range(2):
                    dve.wait_ge(query_high, 2 * tile + piece + 1)
                    hi = q_hi[:, 4 * piece:4 * piece + 4, :].rearrange("p a t -> p (a t)")
                    lo = q_lo[:, 4 * piece:4 * piece + 4, :].rearrange("p a t -> p (a t)")
                    dve.tensor_tensor(lo, w_bank[piece][:, :], hi, ALU.subtract).then_inc(query_low, 1)

            def stack(b, j):
                if not (isinstance(b, int) and b < 2):
                    dve.wait_ge(score_ready, UNITS * (b - 1))
                dve.wait_ge(query_low, 2 * (b // 2) + 2 if isinstance(b, int) else b - j + 2)
                for e in range(2):
                    src = slice(DC * e, DC * e + DC)
                    dve.tensor_copy(q_both[j][0:DC, e::2, :], q_hi[src, :, S * j:S * j + S])
                    dve.tensor_copy(q_shift[j][0:DC, e::2, :], q_hi[src, :, S * j:S * j + S])
                    last = dve.tensor_copy(q_both[j][DC:P, e::2, :], q_lo[src, :, S * j:S * j + S])
                last.then_inc(stacked, 1)

            def key_lows(b, j):
                for n in range(4):
                    w = min(4 * P, KEYS - 512 * n)
                    dve.wait_ge(key_high, 4 * b + n + 1)
                    dve.tensor_tensor(k_low[j][0:DC, 512 * n:512 * n + w], w_bank[n % 2][0:DC, 0:w], k_high[j][0:DC, 512 * n:512 * n + w], ALU.subtract).then_inc(key_low, 1)

            def chunk(b, n):
                dve.wait_ge(chunk_ready, MAXES * b + n + 1)
                dve.tensor_reduce(maxes[:, n // NCH, n % NCH:n % NCH + 1], m_bank[n % MR][:, 0:CH], AX.X, ALU.max).then_inc(chunk_max, 1)

            def shift(b):
                dve.wait_ge(chunk_max, MAXES * (b + 1))
                dve.tensor_reduce(neg_max[:, :], maxes[:, :, :], AX.X, ALU.max, negate=True).then_inc(max_steps, 1)
                dve.wait_ge(max_steps, 2 * b + 1)
                dve.tensor_copy(neg_max2[:, :, 0], neg_max[:, :]).then_inc(max_steps, 1)
                dve.wait_ge(max_steps, 2 * b + 2)
                dve.tensor_tensor(neg_max2[:, :, 1], neg_max[:, :], neg_max2[:, :, 0], ALU.subtract).then_inc(shift_known, 1)

            def invert(b):
                dve.wait_ge(sum_ready, b + 1)
                dve.reciprocal(inv[0:QT, :], w_bank[0][0:QT, 0:P]).then_inc(inverted, 1)

            def normalise(b, j, tile):
                dve.wait_ge(spread_ready, b + 1)
                dve.wait_ge(held_done, b + 1)
                if j == 0 and not (isinstance(b, int) and b == 0):
                    dve.wait_ge(out_ready, tile)
                dve.tensor_tensor(mixed[:, :, j, :], held[:, :].rearrange("p (h s) -> p h s", h=HH),
                                  w_bank[1][:, :].rearrange("p (h s) -> p h s", h=HH), ALU.mult).then_inc(norm_done, 1)

            def add_out(tile):
                dve.wait_ge(out_ready, tile + 1)
                xt = x_res[:, bass.ds(tile, 1), :].rearrange("p a d -> p (a d)")
                dve.tensor_tensor(xt, w_bank[0][:, 0:D], xt, ALU.add).then_inc(x_added, 1)

            def first():
                dve.memset(inv[:, :], 0.0).then_inc(const_made, 1)
                dve.wait_ge(consts_in, 16 * 9)
                rope(0, 0)
                query_lows(0)
                stack(0, 0)
                key_lows(0, 0)
                for n in range(MAXES):
                    chunk(0, n)
                shift(0)
                rope(1, 1)

            def step(i, is_first, is_last):
                for j in range(2):
                    b = 2 * i + j
                    ahead = not (is_last and j == 1)
                    behind = not (is_first and j == 0)
                    if ahead:
                        if j == 1:
                            query_lows(i + 1)
                        stack(b + 1, 1 - j)
                        key_lows(b + 1, 1 - j)
                    for u in range(UNITS):
                        if ahead:
                            for n in chunks_in(j, u, 0) + chunks_in(j, u, 1):
                                chunk(b + 1, n)
                        if behind and u == SUMS_U:
                            invert(b - 1)
                        if behind and u == SPREAD_U:
                            normalise(b - 1, 1 - j, i)
                        if u == OUT_U and j == 0 and not is_first:
                            add_out(i - 1)
                    if ahead:
                        shift(b + 1)
                    if not is_last:
                        rope(b + 2, j)

            walk(dve, first, step)
            invert(B - 1)
            normalise(B - 1, 1, NT - 1)
            add_out(NT - 1)

        @block.tensor
        def _(pe):
            def queries(tile, after):
                for piece in range(2):
                    after(piece)
                    for pair in range(4):
                        for c in range(2):
                            h = 8 * piece + 2 * pair
                            last = pe.matmul(w_bank[piece][:, P * pair:P * pair + P],
                                             to_query[:, c, h:h + 2, :].rearrange("p h d -> p (h d)"),
                                             y_cols[:, c, bass.ds(tile * P, P)], start=(c == 0), stop=(c == 1))
                    last.then_inc(query_ready, 1)

            def turn_keys(b, j, n):
                for t in range(4 * n, min(4 * n + 4, KT)):
                    last = pe.transpose(w_bank[n % 2][:, P * (t % 4):P * (t % 4) + P],
                                        kv_pair[:, t, :, :].rearrange("p a d -> p (a d)"), ident[:, :])
                last.then_inc(turned_ready, 1)

            def chunk(b, j, n, first_batch=False):
                if n >= MR:
                    pe.wait_ge(chunk_max, MAXES * b + n - MR + 1)
                elif not first_batch:
                    pe.wait_ge(chunk_max, MAXES * b)
                g, c = divmod(n, NCH)
                pe.matmul(m_bank[n % MR][:, 0:CH], q_both[j][:, 2 * g:2 * g + 2, :].rearrange("p h s -> p (h s)"),
                          k_high[j][:, CH * c:CH * c + CH], start=True, stop=True).then_inc(chunk_ready, 1)

            def shift_rows(b, j):
                pe.wait_ge(shift_known, b + 1)
                for c in range(2):
                    for g in range(4 * c, 4 * c + 4):
                        last = pe.matmul(w_bank[c][0:2, P * (g % 4):P * (g % 4) + P], neg_max2[:, g, :], ident16[:, :], start=True, stop=True)
                    last.then_inc(shift_ready, 1)

            def score(b, j, u):
                t, half = divmod(u, 2)
                keys = slice(P * t, P * t + P)
                cols = slice(8 * half, 8 * half + 8)
                pe.matmul(s_bank[u % 2][:, :], k_high[j][:, keys], q_both[j][:, cols, :].rearrange("p h s -> p (h s)"), start=True, stop=False)
                pe.matmul(s_bank[u % 2][:, :], k_low[j][:, keys], q_shift[j][:, cols, :].rearrange("p h s -> p (h s)"), start=False, stop=True).then_inc(score_ready, 1)

            def values(b, j, t):
                for half in range(2):
                    last = pe.matmul(v_bank[DC * half:DC * half + DC, :], kv[j][:, t, :], probs[t % RING][:, half, :],
                                     start=(t == 0), stop=(t == KT - 1))
                last.then_inc(value_done, 1)

            def add_keys(b, j):
                pe.wait_ge(sum_added, (KT - 1) * (b + 1))
                for g in range(QT):
                    last = pe.matmul(w_bank[0][0:QT, 0:P], pick[:, g, :], sums[j][:, g // 4, P * (g % 4):P * (g % 4) + P], start=(g == 0), stop=(g == QT - 1))
                last.then_inc(sum_ready, 1)

            def spread_inverse(b):
                pe.wait_ge(inverted, b + 1)
                for g in range(QT // 2):
                    last = pe.matmul(w_bank[1][:, P * g:P * g + P], unpick[:, g, :], inv[:, :], start=True, stop=True)
                last.then_inc(spread_ready, 1)

            def project(tile):
                pe.wait_ge(norm_done, 2 * tile + 2)
                for h in range(HH):
                    last = pe.matmul(w_bank[0][:, 0:D], mixed[:, h, :, :].rearrange("p j s -> p (j s)"), to_out[:, h, :], start=(h == 0), stop=(h == HH - 1))
                last.then_inc(out_ready, 1)

            def first():
                pe.wait_ge(consts_in, 16 * 9)
                queries(0, lambda piece: None)
                pe.wait_ge(doubled, 1)
                for n in range(4):
                    if n < 2:
                        pe.wait_ge(query_low, n + 1)
                    else:
                        pe.wait_ge(key_low, n - 1)
                    turn_keys(0, 0, n)
                pe.wait_ge(key_high, 4)
                pe.wait_ge(stacked, 1)
                for n in range(MAXES):
                    chunk(0, 0, n, first_batch=True)
                pe.wait_ge(key_low, 4)
                shift_rows(0, 0)
                pe.wait_ge(const_made, 1)

            def step(i, is_first, is_last):
                for j in range(2):
                    b = 2 * i + j
                    nb = b + 1
                    ahead = not (is_last and j == 1)
                    behind = not (is_first and j == 0)
                    pe.wait_ge(shift_placed, 2 * b + 2)
                    for u in range(UNITS):
                        if not (is_first and j == 0 and u < 2):
                            pe.wait_ge(exp_done, UNITS * b + u - 1)
                        score(b, j, u)
                        if ahead and j == 1 and u == 0:
                            queries(i + 1, lambda piece: None)
                        if ahead and 0 <= u - TURN_U[j] < 4:
                            n = u - TURN_U[j]
                            if n == 0:
                                pe.wait_ge(doubled, nb + 1)
                            if n < 2:
                                if j == 1:
                                    pe.wait_ge(query_low, 2 * (i + 1) + n + 1)
                            else:
                                pe.wait_ge(key_low, 4 * nb + n - 1)
                            turn_keys(nb, 1 - j, n)
                        if ahead:
                            for n in chunks_in(j, u, 0):
                                if n == 0:
                                    pe.wait_ge(stacked, nb + 1)
                                if n < NCH:
                                    pe.wait_ge(key_high, 4 * nb + (CH * (n + 1) - 1) // 512 + 1)
                                chunk(nb, 1 - j, n)
                        t = u // 2
                        if u % 2 == 1 and t >= 1:
                            pe.wait_ge(exp_done, UNITS * b + 2 * t)
                            if t == 1:
                                if behind:
                                    pe.wait_ge(held_done, b)
                                pe.wait_ge(kv_filled, b + 1)
                            values(b, j, t - 1)
                        if behind and u == SUMS_U:
                            if ahead:
                                pe.wait_ge(key_low, 4 * nb + 3)
                            add_keys(b - 1, 1 - j)
                        if behind and u == SPREAD_U:
                            if ahead:
                                pe.wait_ge(key_low, 4 * nb + 4)
                            spread_inverse(b - 1)
                        if ahead:
                            for n in chunks_in(j, u, 1):
                                if n < NCH:
                                    pe.wait_ge(key_high, 4 * nb + (CH * (n + 1) - 1) // 512 + 1)
                                chunk(nb, 1 - j, n)
                        if u == OUT_U and j == 0 and not is_first:
                            project(i - 1)
                        if ahead and u == 24:
                            if j == 0 and not is_first:
                                pe.wait_ge(x_added, i)
                            elif behind:
                                pe.wait_ge(norm_done, b)
                            shift_rows(nb, 1 - j)
                    pe.wait_ge(exp_done, UNITS * (b + 1))
                    values(b, j, KT - 1)

            walk(pe, first, step)
            pe.wait_ge(norm_done, B - 1)
            add_keys(B - 1, 1)
            spread_inverse(B - 1)
            project(NT - 1)


def fold(nc, a, x_res, ident, to_query, to_out, y_cols):
    HG = 8
    with ExitStack() as ctx:
        def sb(name, shape, dt=F32):
            return ctx.enter_context(nc.sbuf_tensor(name, shape, dt))

        def sem(name):
            return ctx.enter_context(nc.semaphore(name))

        wq = sb("wq", [P, H, D])
        wkc = sb("wkc", [96, 2, H, P])
        wqr = sb("wqr", [DC, H, 192])
        wkr = sb("wkr", [DC, H, DC])
        wkv = sb("wkv", [P, H, DC])
        wo = sb("wo", [P, H, D])
        qr_kr = sb("qr_kr", [96, 2, H, DC])
        kc_kr = sb("kc_kr", [P, H, DC])
        y = sb("y", [P, 2, GT, D])
        stats = sb("stats", [P, GT, 6])
        mv = sb("mv", [P, GT, 2])
        half_var = sb("half_var", [P, GT])
        root = sb("root", [P, GT])
        work = sb("work", [P, GT])
        bank = [ctx.enter_context(nc.psum_tensor(f"fold_bank{k}", [P, 512], F32)) for k in range(8)]

        x_in = sem("x_in")
        weights_in = sem("weights_in")
        job_ready = sem("job_ready")
        job_copied = sem("job_copied")
        ln_steps = sem("ln_steps")
        rows_ready = sem("rows_ready")
        cols_ready = sem("cols_ready")
        cols_copied = sem("cols_copied")
        block = ctx.enter_context(nc.Block())

        dests = [qr_kr[:, c, HG * g:HG * g + HG, :] for c in range(2) for g in range(2)]
        dests += [kc_kr[:, HG * g:HG * g + HG, :] for g in range(2)]
        dests += [to_query[:, c, HG * g:HG * g + HG, :] for c in range(2) for g in range(2)]
        dests += [to_out[:, 2 * g:2 * g + 2, :] for g in range(HH // 2)]
        FB = 4

        @block.sync
        def _(sp):
            sp.dma_start(ident[:, :], a["ident"]).then_inc(x_in, 16)
            sp.dma_start(x_res[:, :, :], a["x"].rearrange("(t p) d -> p t d", p=P)).then_inc(x_in, 16)
            for dst, name in ((wqr[:, :, :], "wqr"), (wkr[:, :, :], "wkr"), (wkc[:, :, :, :], "wkc"), (wq[:, :, :], "wq"),
                              (wkv[:, :, :], "wkv"), (wo[:, :, :], "wo")):
                sp.dma_start(dst, a[name]).then_inc(weights_in, 16)

        @block.tensor
        def _(pe):
            pe.wait_ge(weights_in, 16 * 6)
            n = 0

            def begin():
                if n >= FB:
                    pe.wait_ge(job_copied, n - FB + 1)
                return bank[n % FB]

            for c in range(2):
                for g in range(2):
                    out = begin()
                    for h in range(HG):
                        last = pe.matmul(out[0:96, DC * h:DC * h + DC], wqr[:, HG * g + h, 96 * c:96 * c + 96], wkr[:, HG * g + h, :], start=True, stop=True)
                    last.then_inc(job_ready, 1)
                    n += 1
            for g in range(2):
                out = begin()
                pe.wait_ge(job_copied, 4)
                for h in range(HG):
                    for c in range(2):
                        last = pe.matmul(out[:, DC * h:DC * h + DC], wkc[:, c, HG * g + h, :], qr_kr[:, c, HG * g + h, :], start=(c == 0), stop=(c == 1))
                last.then_inc(job_ready, 1)
                n += 1
            for c in range(2):
                for g in range(2):
                    out = begin()
                    pe.wait_ge(job_copied, 6)
                    for h in range(HG):
                        last = pe.matmul(out[:, DC * h:DC * h + DC], wq[:, HG * g + h, P * c:P * c + P], kc_kr[:, HG * g + h, :], start=True, stop=True)
                    last.then_inc(job_ready, 1)
                    n += 1
            for g in range(HH // 2):
                out = begin()
                for h in range(2 * g, 2 * g + 2):
                    for half in range(2):
                        last = pe.matmul(out[DC * half:DC * half + DC, D * (h - 2 * g):D * (h - 2 * g) + D],
                                         wkv[:, HH * half + h, :], wo[:, HH * half + h, :], start=True, stop=True)
                last.then_inc(job_ready, 1)
                n += 1
            pe.wait_ge(x_in, 32)
            for g in range(NG):
                pe.wait_ge(rows_ready, g + 1)
                for c in range(2):
                    if g >= 2:
                        pe.wait_ge(cols_copied, 2 * (g - 2) + c + 1)
                    out = bank[FB + (2 * g + c) % 4]
                    for t in range(GT):
                        last = pe.transpose(out[:, P * t:P * t + P], y[:, g % 2, t, P * c:P * c + P], ident[:, :])
                    last.then_inc(cols_ready, 1)

        @block.scalar
        def _(act):
            for n, dst in enumerate(dests):
                act.wait_ge(job_ready, n + 1)
                src = bank[n % FB][0:dst.shape[0], :]
                act.activation(dst, src.rearrange("p (h d) -> p h d", d=dst.shape[-1]), ACT.Copy).then_inc(job_copied, 1)
            for g in range(NG):
                for c in range(2):
                    act.wait_ge(cols_ready, 2 * g + c + 1)
                    act.activation(y_cols[:, c, GTOK * g:GTOK * g + GTOK], bank[FB + (2 * g + c) % 4][:, :], ACT.Copy).then_inc(cols_copied, 1)

        @block.vector
        def _(dve):
            dve.wait_ge(x_in, 32)
            for g in range(NG):
                if g >= 2:
                    dve.wait_ge(cols_ready, 2 * (g - 1))
                steps = Steps(dve, ln_steps, LN_STEPS * g)
                last = layernorm_rows(dve, steps, [x_res[:, GT * g + t, :] for t in range(GT)], [y[:, g % 2, t, :] for t in range(GT)],
                                      stats, mv, half_var, root, work)
                assert steps.n == LN_STEPS
                last.then_inc(rows_ready, 1)


PARTS = 5
NB0, TOP0 = 16, 4
NE, TOP1 = 8, 2
HF = 1024
HC = HF // P
HD = D // H
HPC = P // HD
PV = 2 * HD + 2
SM = GT * 2
RANK_STEPS = 5
ATT_STEPS = 4
GATE_STEPS = 6


def rank_below(dve, steps, logits, n, tri, diff, order, rank, keep, top):
    shape = [P, GT, n, n]
    flat = [t.rearrange("p t i j -> p (t i j)") for t in (diff, order)]
    steps.then(dve.tensor_tensor(diff, logits.unsqueeze(2).broadcast_to(shape), logits.unsqueeze(3).broadcast_to(shape), ALU.subtract))
    steps.then(dve.scalar_tensor_tensor(out=order.rearrange("p t i j -> p t (i j)"), in0=diff.rearrange("p t i j -> p t (i j)"), scalar=0.0,
                                        in1=tri.unsqueeze(1).broadcast_to([P, GT, n * n]), op0=ALU.is_equal, op1=ALU.mult))
    steps.then(dve.scalar_tensor_tensor(out=flat[1], in0=flat[0], scalar=0.0, in1=flat[1], op0=ALU.is_gt, op1=ALU.add))
    steps.then(dve.tensor_reduce(rank, order, AX.X, ALU.add))
    steps.then(dve.tensor_scalar(keep, rank, top - 0.5, None, ALU.is_lt))


def part_two(nc, a, out_dram, x_res, ident):
    with ExitStack() as ctx:
        def sb(name, shape, dt=F32):
            return ctx.enter_context(nc.sbuf_tensor(name, shape, dt))

        def sem(name):
            return ctx.enter_context(nc.semaphore(name))

        att_w = [sb("att0_w", [P, 2, 4, P]), sb("att1_w", [P, 2, 2, P])]
        att_b = [sb("att0_b", [P, 4]), sb("att1_b", [P, 2])]
        router0 = sb("router0", [P, 2, NB0])
        router0_b = sb("router0_b", [P, NB0])
        w1 = sb("w1", [P, 2, HF])
        w2 = sb("w2", [P, HC, D])
        x_wq = sb("x_wq", [P, 2, D])
        x_wk = sb("x_wk", [DC, D])
        x_wv = sb("x_wv", [DC, D])
        x_wo = sb("x_wo", [P, 2, D])
        router1 = sb("router1", [P, 2, NE])
        experts = sb("experts", [P, 2, NE, D])
        expert_b = sb("expert_b", [NE, D])
        block_mask = sb("block_mask", [P, P])
        causal = sb("causal", [P, S])
        head_mask = sb("head_mask", [P, HPC])
        pair_mask = sb("pair_mask", [P, D])
        tri0 = sb("tri0", [P, NB0 * NB0])
        tri1 = sb("tri1", [P, NE * NE])
        spread = sb("spread", [NB0, HC, P], F16)
        att_vo = [sb(f"att{s}_vo", [P, 2, D]) for s in range(2)]
        att_row = [sb(f"att{s}_row", [P, D]) for s in range(2)]

        bank = [ctx.enter_context(nc.psum_tensor(f"bank{k}", [P, 512], F32)) for k in range(8)]
        loads = [(att_w[0][:, :, :, :], "att0_w"), (att_w[1][:, :, :, :], "att1_w"), (att_b[0][:, :], "att0_b"), (att_b[1][:, :], "att1_b"),
                 (router0[:, :, :], "router0"), (router0_b[:, :], "router0_b"), (w1[:, :, :], "w1"), (w2[:, :, :], "w2"),
                 (x_wq[:, :, :], "x_wq"), (x_wk[:, :], "x_wk"), (x_wv[:, :], "x_wv"), (x_wo[:, :, :], "x_wo"),
                 (router1[:, :, :], "router1"), (experts[:, :, :, :], "experts"), (expert_b[:, :], "expert_b"),
                 (block_mask[:, :], "block_mask"), (causal[:, :], "causal"), (head_mask[:, :], "head_mask"), (pair_mask[:, :], "pair_mask"),
                 (tri0[:, :], "tri0"), (tri1[:, :], "tri1"), (spread[:, :, :], "spread")]
        fold_values(nc, a, bank, att_vo, att_row, loads)

        y = [sb(f"y2_{r}", [P, GT, D]) for r in range(2)]
        yt = sb("yt", [P, 2, GTOK])
        stats = sb("stats2", [P, GT, 6])
        mv = sb("mv2", [P, GT, 2])
        half_var = sb("half_var2", [P, GT])
        root = sb("root2", [P, GT])
        work = sb("work2", [P, GT])
        lin = sb("lin", [P, 4, GTOK])
        vals = sb("vals", [P, GT, D])
        masked = sb("masked", [P, GT, P])
        att_shift = sb("att_shift", [P, GT])
        att_sum = sb("att_sum", [P, GT])
        att_inv = sb("att_inv", [P, GT])
        att_p = sb("att_p", [P, GT, P])
        att_pt = sb("att_pt", [P, GTOK])
        logits = sb("logits", [P, GT, NB0])
        diff = sb("diff", [P, GT * NB0 * NB0])
        order = sb("order", [P, GT * NB0 * NB0])
        rank = sb("rank", [P, GT, NB0])
        keep = sb("keep", [P, GT, NB0])
        keep_t = sb("keep_t", [NB0, GTOK], F16)
        hidden = sb("hidden", [P, HC, GTOK])
        ctx_first = sb("ctx_first", [DC, 2 * GT, 2, S])
        xq = sb("xq", [P, 2, GTOK])
        xk1 = sb("xk1", [P, GTOK])
        wide_k = [sb(f"wide_k{c}", [P, 2 * GT, HPC, S]) for c in range(2)]
        pair_v = sb("pair_v", [P, 2 * GT, HPC, PV])
        xs = [sb(f"xs{k}", [P, HPC, S]) for k in range(2)]
        xmax = sb("xmax", [P, 2, HPC])
        xp = [sb(f"xp{k}", [P, HPC * S]) for k in range(2)]
        xpt = [sb(f"xpt{k}", [P, 4, P]) for k in range(2)]
        xinv = sb("xinv", [P, GT, H])
        xo = sb("xo", [P, GT, D])
        xot = sb("xot", [P, 2, GTOK])
        top = sb("top", [P, GT])
        gate = sb("gate", [P, GT, NE])
        gsum = sb("gsum", [P, GT])
        ginv = sb("ginv", [P, GT])
        gate_t = sb("gate_t", [NE, GTOK])

        ln_steps = sem("ln2_steps")
        dve_passed = sem("dve_passed")
        pool_passed = sem("pool_passed")
        rows_ready = sem("rows2_ready")
        cols_ready = sem("cols2_ready")
        cols_copied = sem("cols2_copied")
        bias_added = sem("bias_added")
        lin_ready = sem("lin_ready")
        lin_copied = sem("lin_copied")
        vals_ready = sem("vals_ready")
        vals_copied = sem("vals_copied")
        att_ready = sem("att_ready")
        att_steps = sem("att_steps")
        att_exp = sem("att_exp")
        att_turned = sem("att_turned")
        att_turned_copied = sem("att_turned_copied")
        att_mixed = sem("att_mixed")
        att_x = sem("att_x")
        x_new = sem("x_new")
        logits0_ready = sem("logits0_ready")
        logits_steps = sem("logits_steps")
        rank_steps = sem("rank_steps")
        hidden_ready = sem("hidden_ready")
        gelu_done = sem("gelu_done")
        keep_turned = sem("keep_turned")
        keep_copied = sem("keep_copied")
        spread_ready = sem("spread_ready")
        hidden_masked = sem("hidden_masked")
        ffn_ready = sem("ffn_ready")
        first_in = sem("first_in")
        pair_v_const = sem("pair_v_const")
        xq_ready = sem("xq_ready")
        xk_ready = sem("xk_ready")
        xv_ready = sem("xv_ready")
        xq_copied = sem("xq_copied")
        xk1_copied = sem("xk1_copied")
        wide0_done = sem("wide0_done")
        wide1_done = sem("wide1_done")
        pair_v_done = sem("pair_v_done")
        xs_ready = sem("xs_ready")
        xs_masked = sem("xs_masked")
        xs_max = sem("xs_max")
        xs_shifted = sem("xs_shifted")
        xp_done = sem("xp_done")
        xpt_ready = sem("xpt_ready")
        xpt_copied = sem("xpt_copied")
        xo_ready = sem("xo_ready")
        xinv_done = sem("xinv_done")
        xo_done = sem("xo_done")
        xot_ready = sem("xot_ready")
        xot_by_act = sem("xot_by_act")
        xot_by_dve = sem("xot_by_dve")
        xout_ready = sem("xout_ready")
        logits1_ready = sem("logits1_ready")
        gate_steps = sem("gate_steps")
        gate_shifted = sem("gate_shifted")
        gate_exp = sem("gate_exp")
        gate_turned = sem("gate_turned")
        gate_copied = sem("gate_copied")
        gate_bias_ready = sem("gate_bias_ready")
        expert_ready = sem("expert_ready")
        expert_added = sem("expert_added")
        stored = sem("stored")

        block = ctx.enter_context(nc.Block())
        SCALE = [float(D) ** -0.5, 1.0 / P]

        def x_tile(g, t):
            return x_res[:, bass.ds(g * GT + t, 1), :].rearrange("p a d -> p (a d)")

        def x_tiles(g, t, n):
            return x_res[:, bass.ds(g * GT + t, n), :].rearrange("p a d -> p (a d)")

        @block.sync
        def _(sp):
            def load(g):
                sp.dma_start(ctx_first[:, :, :, :], a["ctx_first"][:, bass.ds(g * 2 * GT, 2 * GT), :, :]).then_inc(first_in, 16)

            def step(i, ahead):
                for r in range(2):
                    if ahead or r == 0:
                        sp.wait_ge(xv_ready, 4 * (2 * i + r) + 4)
                        load(2 * i + r + 1)
                for r in range(2):
                    g = 2 * i + r
                    sp.wait_ge(x_new, 2 * PARTS * i + 2 * PARTS - 1 + r)
                    sp.dma_start(out_dram[bass.ds(g * GTOK, GTOK), :].rearrange("(t p) d -> p t d", p=P), x_res[:, bass.ds(g * GT, GT), :]).then_inc(stored, 16)

            sp.dma_start(pair_v[:, :, :, :], a["pair_v"]).then_inc(pair_v_const, 16)
            load(0)
            with sp.Fori(0, NG // 2 - 1) as i:
                step(i, True)
            step(NG // 2 - 1, False)
            sp.wait_ge(stored, 16 * NG)

        @block.gpsimd
        def _(pool):
            with pool.Fori(0, NG // 2) as i:
                def add_row(s, r):
                    pool.wait_ge(rows_ready, 2 * PARTS * i + 6 * s + r + 1)
                    pool.sem_inc(pool_passed, 1)
                    rows = x_res[:, bass.ds((2 * i + r) * GT, GT), :]
                    pool.tensor_tensor(rows, rows, att_row[s][:, :].unsqueeze(1).broadcast_to([P, GT, D]), ALU.add).then_inc(bias_added, 1)

                def cross_attention(g):
                    pool.wait_ge(xk1_copied, g + 1)
                    pool.tensor_tensor(wide_k[1][:, :, :, :], xk1[:, :].rearrange("p (b s) -> p b s", s=S).unsqueeze(2).broadcast_to([P, 2 * GT, HPC, S]),
                                       head_mask[:, :].unsqueeze(1).unsqueeze(3).broadcast_to([P, 2 * GT, HPC, S]), ALU.mult).then_inc(wide1_done, 1)
                    for n in range(SM):
                        pool.wait_ge(xs_max, SM * g + n + 1)
                        pool.tensor_tensor(xs[n % 2][:, :, :], xs[n % 2][:, :, :], xmax[:, n % 2, :].unsqueeze(2).broadcast_to([P, HPC, S]), ALU.subtract).then_inc(xs_shifted, 1)

                for r in range(2):
                    add_row(0, r)
                for r in range(2):
                    cross_attention(2 * i + r)
                for r in range(2):
                    add_row(1, r)

        @block.scalar
        def _(act):
            with act.Fori(0, NG // 2) as i:
                def cols(n):
                    for c in range(2):
                        act.wait_ge(cols_ready, 2 * n + c + 1)
                        act.activation(yt[:, c, :], bank[c][:, :], ACT.Copy).then_inc(cols_copied, 1)

                def attention(s, r):
                    n = 4 * i + 2 * s + r
                    cols(2 * PARTS * i + 6 * s + r)
                    lins = 4 - 2 * s
                    before = 12 * i + (8 + 2 * r if s else 4 * r)
                    for c in range(lins):
                        act.wait_ge(lin_ready, before + c + 1)
                        act.activation(lin[:, c, :], bank[2 + c][:, :], ACT.Identity, bias=att_b[s][:, c:c + 1]).then_inc(lin_copied, 1)
                    for k in range(2):
                        act.wait_ge(vals_ready, 2 * n + k + 1)
                        act.activation(vals[:, 2 * k:2 * k + 2, :].rearrange("p t d -> p (t d)"), bank[6 + k][:, :], ACT.Copy).then_inc(vals_copied, 1)
                    act.wait_ge(att_steps, ATT_STEPS * n + 3)
                    for t in range(GT):
                        last = act.activation(att_p[:, t, :], masked[:, t, :], ACT.Exp, bias=att_shift[:, t:t + 1], scale=SCALE[s], accum_out=att_sum[:, t:t + 1])
                    last.then_inc(att_exp, 1)
                    act.wait_ge(att_turned, n + 1)
                    act.activation(att_pt[:, :], bank[1][:, :], ACT.Copy).then_inc(att_turned_copied, 1)

                def feed_forward(r):
                    g = 2 * i + r
                    cols(2 * PARTS * i + 2 + r)
                    for c in range(HC):
                        act.wait_ge(hidden_ready, HC * g + c + 1)
                        act.activation(hidden[:, c, :], bank[3 + c % 2][:, :], ACT.Gelu).then_inc(gelu_done, 1)
                        if c == HC - 1:
                            act.wait_ge(keep_turned, g + 1)
                            act.activation(keep_t[:, :], bank[7][0:NB0, :], ACT.Copy).then_inc(keep_copied, 1)

                def cross_attention(r):
                    g = 2 * i + r
                    cols(2 * PARTS * i + 4 + r)
                    for c in range(2):
                        act.wait_ge(xq_ready, 2 * g + c + 1)
                        act.activation(xq[:, c, :], bank[2 + c][:, :], ACT.Copy).then_inc(xq_copied, 1)
                    act.wait_ge(xk_ready, 2 * g + 2)
                    act.activation(xk1[:, :], bank[5][:, :], ACT.Copy).then_inc(xk1_copied, 1)
                    for n in range(SM + 1):
                        if n < SM:
                            act.wait_ge(xs_shifted, SM * g + n + 1)
                            act.activation(xp[n % 2][:, :], xs[n % 2][:, :, :].rearrange("p h s -> p (h s)"), ACT.Exp, scale=float(HD) ** -0.5).then_inc(xp_done, 1)
                        if n >= 1:
                            act.wait_ge(xpt_ready, SM * g + n)
                            act.activation(xpt[(n - 1) % 2][:, :, :].rearrange("p a q -> p (a q)"), bank[4 + (n - 1) % 2][:, :], ACT.Copy).then_inc(xpt_copied, 1)
                    act.wait_ge(xot_ready, 2 * g + 1)
                    act.activation(xot[:, 0, :], bank[0][:, :], ACT.Copy).then_inc(xot_by_act, 1)

                def mix_experts(r):
                    g = 2 * i + r
                    cols(2 * PARTS * i + 8 + r)
                    act.wait_ge(gate_shifted, g + 1)
                    act.activation(gate[:, :, :], gate[:, :, :], ACT.Exp).then_inc(gate_exp, 1)
                    act.wait_ge(gate_turned, g + 1)
                    act.activation(gate_t[:, :], bank[7][0:NE, :], ACT.Copy).then_inc(gate_copied, 1)

                for r in range(2):
                    attention(0, r)
                for r in range(2):
                    feed_forward(r)
                for r in range(2):
                    cross_attention(r)
                for r in range(2):
                    attention(1, r)
                for r in range(2):
                    mix_experts(r)

        @block.vector
        def _(dve):
            square = "p (t i j) -> p t i j"
            with dve.Fori(0, NG // 2) as i:
                def normalised(part, r):
                    n = 2 * PARTS * i + 2 * part + r
                    g = 2 * i + r
                    if part > 0:
                        dve.wait_ge(x_new, n - 1)
                    dve.sem_inc(dve_passed, 1)
                    last = layernorm_rows(dve, Steps(dve, ln_steps, LN_STEPS * n), [x_tile(g, t) for t in range(GT)], [y[r][:, t, :] for t in range(GT)],
                                          stats, mv, half_var, root, work, passed=dve_passed)
                    last.then_inc(rows_ready, 1)

                def normalise_other(part, r):
                    if r == 0:
                        normalised(part, 1)
                    elif part + 1 < PARTS:
                        normalised(part + 1, 0)

                def attention(s, r):
                    n = 4 * i + 2 * s + r
                    g = 2 * i + r
                    normalise_other(3 * s, r)
                    dve.wait_ge(att_ready, n + 1)
                    steps = Steps(dve, att_steps, ATT_STEPS * n)
                    steps.then(dve.tensor_tensor(masked[:, :, :], bank[0][:, :].rearrange("p (t k) -> p t k", t=GT),
                                                 block_mask[:, :].unsqueeze(1).broadcast_to([P, GT, P]), ALU.add))
                    steps.then(dve.tensor_reduce(att_shift[:, :], masked[:, :, :], AX.X, ALU.max, negate=True))
                    steps.then(dve.tensor_scalar(att_shift[:, :], att_shift[:, :], SCALE[s], None, ALU.mult))
                    dve.wait_ge(att_exp, n + 1)
                    steps.then(dve.reciprocal(att_inv[:, :], att_sum[:, :]))
                    dve.wait_ge(bias_added, n + 1)
                    for t in range(GT):
                        if t % 2 == 0:
                            dve.wait_ge(att_mixed, 2 * n + t // 2 + 1)
                        last = dve.scalar_tensor_tensor(out=x_tile(g, t), in0=bank[2 + t // 2][:, D * (t % 2):D * (t % 2) + D], scalar=att_inv[:, t:t + 1],
                                                        in1=x_tile(g, t), op0=ALU.mult, op1=ALU.add)
                    last.then_inc(x_new, 1)

                def feed_forward(r):
                    g = 2 * i + r
                    normalise_other(1, r)
                    dve.wait_ge(logits0_ready, g + 1)
                    lsteps = Steps(dve, logits_steps, g)
                    lsteps.then(dve.tensor_tensor(logits[:, :, :], bank[2][:, 0:GT * NB0].rearrange("p (t n) -> p t n", n=NB0),
                                                  router0_b[:, :].unsqueeze(1).broadcast_to([P, GT, NB0]), ALU.add))
                    rank_below(dve, Steps(dve, rank_steps, RANK_STEPS * (4 * i + r)), logits[:, :, :], NB0, tri0[:, :],
                               diff[:, :].rearrange(square, t=GT, i=NB0), order[:, :].rearrange(square, t=GT, i=NB0),
                               rank[:, :, :], keep[:, :, :], TOP0)
                    for c in range(HC):
                        dve.wait_ge(spread_ready, HC * g + c + 1)
                        dve.wait_ge(gelu_done, HC * g + c + 1)
                        dve.tensor_tensor(hidden[:, c, :], bank[5 + c % 2][:, :], hidden[:, c, :], ALU.mult).then_inc(hidden_masked, 1)
                    dve.wait_ge(ffn_ready, g + 1)
                    for t, k in enumerate((0, 1, 2, 7)):
                        last = dve.tensor_tensor(x_tile(g, t), bank[k][:, 0:D], x_tile(g, t), ALU.add)
                    last.then_inc(x_new, 1)

                def cross_attention(r):
                    g = 2 * i + r
                    normalise_other(2, r)
                    dve.wait_ge(xk_ready, 2 * g + 1)
                    dve.tensor_tensor(wide_k[0][:, :, :, :], bank[4][:, :].rearrange("p (b s) -> p b s", s=S).unsqueeze(2).broadcast_to([P, 2 * GT, HPC, S]),
                                      head_mask[:, :].unsqueeze(1).unsqueeze(3).broadcast_to([P, 2 * GT, HPC, S]), ALU.mult).then_inc(wide0_done, 1)
                    for k in range(4):
                        dve.wait_ge(xv_ready, 4 * g + k + 1)
                        for b2 in range(2):
                            last = dve.tensor_tensor(pair_v[:, 2 * k + b2, :, 0:2 * HD], bank[(6 + k) % 8][:, D * b2:D * b2 + D].rearrange("p (a d) -> p a d", a=HPC),
                                                     pair_mask[:, :].rearrange("p (a d) -> p a d", a=HPC), ALU.mult)
                        last.then_inc(pair_v_done, 1)

                    def finish(t):
                        dve.wait_ge(xo_ready, 2 * GT * g + 2 * t + 2)
                        pv = bank[6 + t % 2][:, 0:HPC * PV].rearrange("p (a v) -> p a v", v=PV)
                        dve.reciprocal(xinv[:, t, :].rearrange("p (a e) -> p a e", e=2), pv[:, :, 2 * HD:PV]).then_inc(xinv_done, 1)
                        dve.wait_ge(xinv_done, GT * g + t + 1)
                        for e in range(2):
                            last = dve.tensor_tensor(xo[:, t, :].rearrange("p (a e d) -> p a e d", e=2, d=HD)[:, :, e, :], pv[:, :, HD * e:HD * e + HD],
                                                     xinv[:, t, e::2].unsqueeze(2).broadcast_to([P, HPC, HD]), ALU.mult)
                        last.then_inc(xo_done, 1)

                    for n in range(SM):
                        dve.wait_ge(xs_ready, SM * g + n + 1)
                        if n >= 2:
                            dve.wait_ge(xp_done, SM * g + n - 1)
                        dve.tensor_tensor(xs[n % 2][:, :, :], bank[2 + n % 2][:, :].rearrange("p (h s) -> p h s", s=S),
                                          causal[:, :].unsqueeze(1).broadcast_to([P, HPC, S]), ALU.add).then_inc(xs_masked, 1)
                        dve.wait_ge(xs_masked, SM * g + n + 1)
                        dve.tensor_reduce(xmax[:, n % 2, :], xs[n % 2][:, :, :], AX.X, ALU.max).then_inc(xs_max, 1)
                        if n >= 4 and n % 2 == 0:
                            finish(n // 2 - 2)
                    finish(GT - 2)
                    finish(GT - 1)
                    dve.wait_ge(xot_ready, 2 * g + 2)
                    dve.tensor_copy(xot[:, 1, :], bank[1][:, :]).then_inc(xot_by_dve, 1)
                    for k in range(2):
                        dve.wait_ge(xout_ready, 2 * g + k + 1)
                        last = dve.tensor_tensor(x_tiles(g, 2 * k, 2), bank[2 + k][:, :], x_tiles(g, 2 * k, 2), ALU.add)
                    last.then_inc(x_new, 1)

                def mix_experts(r):
                    g = 2 * i + r
                    normalise_other(4, r)
                    dve.wait_ge(logits1_ready, g + 1)
                    steps = Steps(dve, gate_steps, GATE_STEPS * g)
                    lg = logits[:, :, 0:NE]
                    steps.then(dve.tensor_copy(lg, bank[2][:, 0:GT * NE].rearrange("p (t n) -> p t n", n=NE)))
                    steps.then(dve.tensor_reduce(top[:, :], lg, AX.X, ALU.max))
                    dve.tensor_tensor(gate[:, :, :], lg, top[:, :].unsqueeze(2).broadcast_to([P, GT, NE]), ALU.subtract).then_inc(gate_shifted, 1)
                    n2 = GT * NE * NE
                    rank_below(dve, Steps(dve, rank_steps, RANK_STEPS * (4 * i + 2 + r)), lg, NE, tri1[:, :],
                               diff[:, 0:n2].rearrange(square, t=GT, i=NE), order[:, 0:n2].rearrange(square, t=GT, i=NE),
                               rank[:, :, 0:NE], keep[:, :, 0:NE], TOP1)
                    dve.wait_ge(gate_exp, g + 1)
                    steps.then(dve.tensor_tensor(gate[:, :, :], gate[:, :, :], keep[:, :, 0:NE], ALU.mult))
                    steps.then(dve.tensor_reduce(gsum[:, :], gate[:, :, :], AX.X, ALU.add))
                    steps.then(dve.reciprocal(ginv[:, :], gsum[:, :]))
                    steps.then(dve.tensor_tensor(gate[:, :, :], gate[:, :, :], ginv[:, :].unsqueeze(2).broadcast_to([P, GT, NE]), ALU.mult))
                    for t in range(GT):
                        for e in range(NE):
                            m = NE * t + e
                            if e % 2 == 0:
                                dve.wait_ge(expert_ready, GT * NE // 2 * g + m // 2 + 1)
                            if e > 0:
                                dve.wait_ge(expert_added, GT * NE * g + m)
                            dve.scalar_tensor_tensor(out=x_tile(g, t), in0=bank[3 + e // 2][:, D * (e % 2):D * (e % 2) + D], scalar=gate[:, t, e:e + 1],
                                                     in1=x_tile(g, t), op0=ALU.mult, op1=ALU.add).then_inc(expert_added, 1)
                    dve.wait_ge(expert_added, GT * NE * (g + 1))
                    dve.wait_ge(gate_bias_ready, g + 1)
                    for k in range(2):
                        last = dve.tensor_tensor(x_tiles(g, 2 * k, 2), bank[k][:, :], x_tiles(g, 2 * k, 2), ALU.add)
                    last.then_inc(x_new, 1)

                normalised(0, 0)
                for r in range(2):
                    attention(0, r)
                for r in range(2):
                    feed_forward(r)
                for r in range(2):
                    cross_attention(r)
                for r in range(2):
                    attention(1, r)
                for r in range(2):
                    mix_experts(r)

        @block.tensor
        def _(pe):
            with pe.Fori(0, NG // 2) as i:
                def tile(t):
                    return slice(P * t, P * t + P)

                def cols(part, r):
                    n = 2 * PARTS * i + 2 * part + r
                    pe.wait_ge(rows_ready, n + 1)
                    if part + r > 0:
                        pe.wait_ge(x_new, n)
                    for c in range(2):
                        for t in range(GT):
                            last = pe.transpose(bank[c][:, tile(t)], y[r][:, t, P * c:P * c + P], ident[:, :])
                        last.then_inc(cols_ready, 1)
                    pe.wait_ge(cols_copied, 2 * n + 2)

                def attention(s, r):
                    n = 4 * i + 2 * s + r
                    cols(3 * s, r)
                    lins = 4 - 2 * s
                    for c in range(lins):
                        for k in range(2):
                            last = pe.matmul(bank[2 + c][:, :], att_w[s][:, k, c, :], yt[:, k, :], start=(k == 0), stop=(k == 1))
                        last.then_inc(lin_ready, 1)
                    for t in range(GT):
                        for k in range(2):
                            last = pe.matmul(bank[6 + t // 2][:, D * (t % 2):D * (t % 2) + D], yt[:, k, tile(t)], att_vo[s][:, k, :], start=(k == 0), stop=(k == 1))
                        if t % 2:
                            last.then_inc(vals_ready, 1)
                    pe.wait_ge(lin_copied, 12 * i + (8 + 2 * r if s else 4 * r) + lins)
                    parts = lins // 2
                    for t in range(GT):
                        for k in range(parts):
                            last = pe.matmul(bank[0][:, tile(t)], lin[:, k, tile(t)], lin[:, parts + k, tile(t)], start=(k == 0), stop=(k == parts - 1))
                    last.then_inc(att_ready, 1)
                    pe.wait_ge(att_exp, n + 1)
                    for t in range(GT):
                        last = pe.transpose(bank[1][:, tile(t)], att_p[:, t, :], ident[:, :])
                    last.then_inc(att_turned, 1)
                    pe.wait_ge(att_turned_copied, n + 1)
                    pe.wait_ge(vals_copied, 2 * n + 2)
                    for t in range(GT):
                        last = pe.matmul(bank[2 + t // 2][:, D * (t % 2):D * (t % 2) + D], att_pt[:, tile(t)], vals[:, t, :], start=True, stop=True)
                        if t % 2:
                            last.then_inc(att_mixed, 1)

                def feed_forward(r):
                    g = 2 * i + r
                    cols(1, r)
                    for t in range(GT):
                        for k in range(2):
                            last = pe.matmul(bank[2][:, NB0 * t:NB0 * t + NB0], yt[:, k, tile(t)], router0[:, k, :], start=(k == 0), stop=(k == 1))
                    last.then_inc(logits0_ready, 1)

                    def hidden_chunk(c):
                        if c >= 2:
                            pe.wait_ge(gelu_done, HC * g + c - 1)
                        for k in range(2):
                            last = pe.matmul(bank[3 + c % 2][:, :], w1[:, k, P * c:P * c + P], yt[:, k, :], start=(k == 0), stop=(k == 1))
                        last.then_inc(hidden_ready, 1)

                    def hidden_out(c):
                        pe.wait_ge(hidden_masked, HC * g + c + 1)
                        for t, k in enumerate((0, 1, 2, 7)):
                            last = pe.matmul(bank[k][:, 0:D], hidden[:, c, tile(t)], w2[:, c, :], start=(c == 0), stop=(c == HC - 1))
                        if c == HC - 1:
                            last.then_inc(ffn_ready, 1)

                    for c in range(HC):
                        hidden_chunk(c)
                    pe.wait_ge(rank_steps, RANK_STEPS * (4 * i + r) + RANK_STEPS)
                    for t in range(GT):
                        last = pe.transpose(bank[7][0:NB0, tile(t)], keep[:, t, :], ident[:, :])
                    last.then_inc(keep_turned, 1)
                    pe.wait_ge(keep_copied, g + 1)
                    for c in range(HC):
                        if c >= 2:
                            pe.wait_ge(hidden_masked, HC * g + c - 1)
                        pe.matmul(bank[5 + c % 2][:, :], spread[:, c, :], keep_t[:, :], start=True, stop=True).then_inc(spread_ready, 1)
                        if c >= 1:
                            hidden_out(c - 1)
                    hidden_out(HC - 1)

                def cross_attention(r):
                    g = 2 * i + r
                    cols(2, r)
                    for c in range(2):
                        for k in range(2):
                            last = pe.matmul(bank[2 + c][:, :], x_wq[:, k, P * c:P * c + P], yt[:, k, :], start=(k == 0), stop=(k == 1))
                        last.then_inc(xq_ready, 1)
                    pe.wait_ge(first_in, 16 * g + 16)
                    for c in range(2):
                        pe.matmul(bank[4 + c][:, :], x_wk[:, P * c:P * c + P], ctx_first[:, :, 0, :], start=True, stop=True).then_inc(xk_ready, 1)
                    for k in range(4):
                        for b2 in range(2):
                            last = pe.matmul(bank[(6 + k) % 8][:, D * b2:D * b2 + D], ctx_first[:, 2 * k + b2, :, :].rearrange("p e s -> p (e s)"), x_wv[:, :],
                                             start=True, stop=True)
                        last.then_inc(xv_ready, 1)
                    pe.wait_ge(xq_copied, 2 * g + 2)
                    pe.wait_ge(wide0_done, g + 1)
                    pe.wait_ge(wide1_done, g + 1)
                    pe.wait_ge(pair_v_done, 4 * g + 4)
                    for n in range(SM + 2):
                        if n < SM:
                            t, c = divmod(n, 2)
                            if n >= 2:
                                pe.wait_ge(xs_masked, SM * g + n - 1)
                            for b2 in range(2):
                                last = pe.matmul(bank[2 + n % 2][S * b2:S * b2 + S, :], xq[:, c, P * t + S * b2:P * t + S * b2 + S],
                                                 wide_k[c][:, 2 * t + b2, :, :].rearrange("p h s -> p (h s)"), start=True, stop=True)
                            last.then_inc(xs_ready, 1)
                        if 1 <= n <= SM:
                            m = n - 1
                            pe.wait_ge(xp_done, SM * g + m + 1)
                            if m >= 2:
                                pe.wait_ge(xpt_copied, SM * g + m - 1)
                            for a2 in range(4):
                                last = pe.transpose(bank[4 + m % 2][:, tile(a2)], xp[m % 2][:, tile(a2)], ident[:, :])
                            last.then_inc(xpt_ready, 1)
                        if n >= 2:
                            m = n - 2
                            t, c = divmod(m, 2)
                            pe.wait_ge(xpt_copied, SM * g + m + 1)
                            if t >= 2 and c == 0:
                                pe.wait_ge(xo_done, GT * g + t - 1)
                            for a2 in range(4):
                                pair = 4 * c + a2
                                for b2 in range(2):
                                    last = pe.matmul(bank[6 + t % 2][S * b2:S * b2 + S, PV * pair:PV * pair + PV], xpt[m % 2][:, a2, S * b2:S * b2 + S],
                                                     pair_v[:, 2 * t + b2, pair, :], start=True, stop=True)
                            last.then_inc(xo_ready, 1)
                    pe.wait_ge(xo_done, GT * g + GT)
                    for c in range(2):
                        for t in range(GT):
                            last = pe.transpose(bank[c][:, tile(t)], xo[:, t, P * c:P * c + P], ident[:, :])
                        last.then_inc(xot_ready, 1)
                    pe.wait_ge(xot_by_act, g + 1)
                    pe.wait_ge(xot_by_dve, g + 1)
                    for t in range(GT):
                        for k in range(2):
                            last = pe.matmul(bank[2 + t // 2][:, D * (t % 2):D * (t % 2) + D], xot[:, k, tile(t)], x_wo[:, k, :], start=(k == 0), stop=(k == 1))
                        if t % 2:
                            last.then_inc(xout_ready, 1)

                def mix_experts(r):
                    g = 2 * i + r
                    cols(4, r)
                    for t in range(GT):
                        for k in range(2):
                            last = pe.matmul(bank[2][:, NE * t:NE * t + NE], yt[:, k, tile(t)], router1[:, k, :], start=(k == 0), stop=(k == 1))
                    last.then_inc(logits1_ready, 1)
                    for t in range(GT):
                        for e2 in range(NE // 2):
                            if t > 0:
                                pe.wait_ge(expert_added, GT * NE * g + NE * (t - 1) + 2 * e2 + 2)
                            for k in range(2):
                                last = pe.matmul(bank[3 + e2][:, :], yt[:, k, tile(t)], experts[:, k, 2 * e2:2 * e2 + 2, :].rearrange("p e d -> p (e d)"),
                                                 start=(k == 0), stop=(k == 1))
                            last.then_inc(expert_ready, 1)
                        if t == 0:
                            pe.wait_ge(gate_steps, GATE_STEPS * g + GATE_STEPS)
                            for t1 in range(GT):
                                last = pe.transpose(bank[7][0:NE, tile(t1)], gate[:, t1, :], ident[:, :])
                            last.then_inc(gate_turned, 1)
                            pe.wait_ge(gate_copied, g + 1)
                            for t1 in range(GT):
                                last = pe.matmul(bank[t1 // 2][:, D * (t1 % 2):D * (t1 % 2) + D], gate_t[:, tile(t1)], expert_b[:, :], start=True, stop=True)
                            last.then_inc(gate_bias_ready, 1)

                for r in range(2):
                    attention(0, r)
                for r in range(2):
                    feed_forward(r)
                for r in range(2):
                    cross_attention(r)
                for r in range(2):
                    attention(1, r)
                for r in range(2):
                    mix_experts(r)


def fold_values(nc, a, bank, att_vo, att_row, loads):
    with ExitStack() as ctx:
        def sb(name, shape, dt=F32):
            return ctx.enter_context(nc.sbuf_tensor(name, shape, dt))

        def sem(name):
            return ctx.enter_context(nc.semaphore(name))

        wv0 = sb("wv0", [P, 2, D])
        wo0 = sb("wo0", [P, 2, D])
        bv0 = sb("bv0", [P, 2, P])
        bo0 = sb("bo0", [P, D])
        wv1 = sb("wv1", [P, D])
        wo1 = sb("wo1", [P, H, D])
        bv1 = sb("bv1", [P, P])
        bo1 = sb("bo1", [P, D])
        wo1_sum = sb("wo1_sum", [P, D])
        own_in = sem("own_in")
        weights_in = sem("weights2_in")
        heads_summed = sem("heads_summed")
        joined = sem("joined")
        joined_copied = sem("joined_copied")
        rows_made = sem("rows_made")
        block = ctx.enter_context(nc.Block())
        own = [(wv0[:, :, :], "wv0"), (wo0[:, :, :], "wo0"), (bv0[:, :, :], "bv0"), (bo0[:, :], "bo0"),
               (wv1[:, :], "wv1"), (wo1[:, :, :], "wo1"), (bv1[:, :], "bv1"), (bo1[:, :], "bo1")]

        @block.sync
        def _(sp):
            for dst, name in own:
                sp.dma_start(dst, a[name]).then_inc(own_in, 16)
            for dst, name in loads:
                sp.dma_start(dst, a[name]).then_inc(weights_in, 16)
            sp.wait_ge(weights_in, 16 * len(loads))

        @block.tensor
        def _(pe):
            pe.wait_ge(own_in, 16 * len(own))
            for c in range(2):
                for k in range(2):
                    last = pe.matmul(bank[0][:, D * c:D * c + D], wv0[:, k, P * c:P * c + P], wo0[:, k, :], start=(k == 0), stop=(k == 1))
            last.then_inc(joined, 1)
            for k in range(2):
                last = pe.matmul(bank[1][:, 0:D], bv0[:, k, :], wo0[:, k, :], start=(k == 0), stop=(k == 1))
            last.then_inc(joined, 1)
            pe.wait_ge(heads_summed, 1)
            for c in range(2):
                last = pe.matmul(bank[2][:, D * c:D * c + D], wv1[:, P * c:P * c + P], wo1_sum[:, :], start=True, stop=True)
            last.then_inc(joined, 1)
            pe.matmul(bank[3][:, 0:D], bv1[:, :], wo1_sum[:, :], start=True, stop=True).then_inc(joined, 1)

        @block.scalar
        def _(act):
            for s in range(2):
                act.wait_ge(joined, 2 * s + 1)
                act.activation(att_vo[s][:, :, :].rearrange("p k d -> p (k d)"), bank[2 * s][:, :], ACT.Copy).then_inc(joined_copied, 1)

        @block.vector
        def _(dve):
            dve.wait_ge(own_in, 16 * len(own))
            dve.tensor_reduce(wo1_sum[:, :], wo1[:, :, :].rearrange("p h d -> p d h"), AX.X, ALU.add).then_inc(heads_summed, 1)
            for s, bo in enumerate((bo0, bo1)):
                dve.wait_ge(joined, 2 * s + 2)
                dve.tensor_tensor(att_row[s][:, :], bank[2 * s + 1][:, 0:D], bo[:, :], ALU.add).then_inc(rows_made, 1)


def bass_perceiver_two_layers(nc, a, out):
    with ExitStack() as ctx:
        x_res = ctx.enter_context(nc.sbuf_tensor("x_res", [P, NT, D], F32))
        ident = ctx.enter_context(nc.sbuf_tensor("ident", [P, P], F32))
        part_one(nc, a, x_res, ident)
        part_two(nc, a, out, x_res, ident)


def _layouts(i):
    import numpy as np

    c = np.ascontiguousarray
    f = np.float32
    pos = np.concatenate([np.arange(FULL_P * KT).reshape(FULL_P, KT),
                          np.arange(L - (P - FULL_P) * KT, L).reshape(P - FULL_P, KT)])
    inv = (f(1.0) / (f(10000.0) ** (np.arange(0, DC, 2, dtype=f) / f(DC)))).astype(f)
    freqs = (pos[:, :, None].astype(f) * inv).astype(f)
    sin = np.repeat(np.sin(freqs), 2, axis=-1).astype(f)
    cos = np.repeat(np.cos(freqs), 2, axis=-1).astype(f)
    sin[:, :, :DC // 2] *= -1
    repeated = np.zeros((P, KT), bool)
    repeated[FULL_P:] = pos[FULL_P:] < FULL_P * KT
    k_rows = np.zeros((P - DC, KT, P), np.float16)
    k_rows[0:2] = 1
    k_rows[2] = np.where(repeated.T, -30000.0, 0.0)
    q_rows = np.zeros((P - DC, H, S), np.float16)
    q_rows[2] = 1
    out = {
        "x": i["x"].reshape(TOK, D), "ctx": i["ctx_512"],
        "cos": cos, "sin": sin, "k_rows": k_rows.reshape(P - DC, KEYS), "q_rows": q_rows,
        "pick": np.broadcast_to(np.eye(QT, dtype=f)[None], (P, QT, QT)),
        "unpick": np.concatenate([np.repeat(np.eye(QT, dtype=f).reshape(QT, 2, QT // 2).transpose(0, 2, 1), DC, axis=2), np.zeros((P - QT, QT // 2, P), f)]),
        "ident": np.eye(P, dtype=f), "ident16": np.eye(P, dtype=np.float16),
        "wq": i["L0_xattn_Wq"].reshape(H, P, D).transpose(1, 0, 2),
        "wkc": i["L0_xattn_w_kc_q"].reshape(H, P, 2, 96).transpose(3, 2, 0, 1),
        "wqr": i["L0_xattn_W_qr"].transpose(2, 0, 1), "wkr": i["L0_xattn_W_kr"].transpose(2, 0, 1),
        "wkv": i["L0_xattn_w_kc_kv"].transpose(1, 0, 2),
        "wo": i["L0_xattn_Wo"].reshape(D, H, P).transpose(2, 1, 0),
    }
    tok = np.arange(P)
    tri = lambda n: np.broadcast_to((np.arange(n)[None, :] < np.arange(n)[:, None]).astype(f).reshape(1, n * n), (P, n * n))
    rows = lambda v: np.broadcast_to(v[None, :], (P, v.shape[0]))
    chunks = lambda w: w.reshape(2, P, -1).transpose(1, 0, 2)
    spread = np.zeros((NB0, HC, P), np.float16)
    spread[(np.arange(HF) // (HF // NB0)), np.arange(HF) // P, np.arange(HF) % P] = 1
    pair_v = np.zeros((P, 2 * GT, HPC, PV), f)
    pair_v[:S, :, :, 2 * HD] = 1
    pair_v[S:, :, :, 2 * HD + 1] = 1
    w_qkv, b_qkv = i["L0_attn_w_qkv"], i["L0_attn_b_qkv"]
    first = i["ctx_512"][:, :S, :].transpose(2, 0, 1)
    out |= {
        "att0_w": w_qkv[:2 * D].reshape(4, P, 2, P).transpose(3, 2, 0, 1), "att0_b": b_qkv[:2 * D].reshape(4, P).T,
        "att1_w": np.stack([i["L1_attn_Wv"], i["L1_attn_Wk"]]).reshape(2, 2, P, P).transpose(2, 1, 0, 3),
        "att1_b": np.stack([i["L1_attn_bv"], i["L1_attn_bk"]], axis=1),
        "wv0": w_qkv[2 * D:].reshape(2, P, D).transpose(1, 0, 2), "wo0": chunks(i["L0_attn_w_out"].T),
        "bv0": np.broadcast_to(b_qkv[2 * D:].reshape(2, P).T[:, :, None], (P, 2, P)), "bo0": rows(i["L0_attn_b_out"]),
        "wv1": i["L1_attn_Wv"].T, "wo1": i["L1_attn_Wo"].reshape(H, P, D).transpose(1, 0, 2),
        "bv1": np.broadcast_to(i["L1_attn_bv"][:, None], (P, P)), "bo1": rows(i["L1_attn_bo"]),
        "router0": chunks(i["L0_ffn_Wr"].T), "router0_b": rows(i["L0_ffn_br"]),
        "w1": chunks(i["L0_ffn_W1"].T), "w2": i["L0_ffn_W2"].T.reshape(HC, P, D).transpose(1, 0, 2),
        "x_wq": chunks(i["L1_xattn_Wq"].T), "x_wk": i["L1_xattn_Wkv_expand"][:D].T, "x_wv": i["L1_xattn_Wkv_expand"][D:].T,
        "x_wo": chunks(i["L1_xattn_Wout"].T),
        "router1": chunks(i["L1_ffn_Wr"]), "experts": i["L1_ffn_We"].reshape(NE, 2, P, D).transpose(2, 1, 0, 3), "expert_b": i["L1_ffn_be"],
        "block_mask": np.where((tok[:, None] // S) == (tok[None, :] // S), 0.0, -1e30).astype(f),
        "causal": np.where(np.arange(S)[None, :] <= (tok % S)[:, None], 0.0, -1e30).astype(f),
        "head_mask": ((tok[:, None] // HD) == np.arange(HPC)[None, :]).astype(f),
        "pair_mask": ((np.arange(D)[None, :] // HD % 2) == (tok[:, None] // S)).astype(f),
        "tri0": tri(NB0), "tri1": tri(NE), "spread": spread, "pair_v": pair_v,
        "ctx_first": np.stack([first, first], axis=2),
    }
    return {k: c(v) for k, v in out.items()}


def kernel(**inputs):
    import numpy as _np
    import concourse.bacc as _bacc
    from concourse import mybir as _mybir
    from concourse.bass_utils import run_bass_kernel_spmd as _run

    nc = _bacc.Bacc("TRN2", target_bir_lowering=False, num_devices=1)
    arrays, args = {}, {}
    for name, v in _layouts({k: _np.asarray(v) for k, v in inputs.items()}).items():
        arrays[f"in_{name}"] = v
        args[name] = nc.dram_tensor(f"in_{name}", v.shape, _mybir.dt.from_np(v.dtype), kind="ExternalInput").ap()
    out = nc.dram_tensor("out", (TOK, D), _mybir.dt.float32, kind="ExternalOutput").ap()
    bass_perceiver_two_layers(nc, args, out)
    r = _run(nc, [arrays], core_ids=[0])
    return r.results[0]["out"].reshape(B, S, D)
```

```python
from contextlib import ExitStack

import concourse.bass as bass
from concourse import mybir

ALU = mybir.AluOpType
ACT = mybir.ActivationFunctionType
AX = mybir.AxisListType
F32 = mybir.dt.float32
F16 = mybir.dt.float16
I32 = mybir.dt.int32

P = 128
B, S, D = 32, 64, 256
L, DC = 1601, 64
H = 16
TOK = B * S
NT = TOK // P
KT = -(-L // P)
KEYS = KT * P
FULL_P = L // KT
QC = H * S
HH = H // 2
UNITS = 2 * KT
CH = 416
NCH = KEYS // CH
QT = QC // P
MAXES = QT * NCH
MR = 3
RING = 7
GT = 4
NG = NT // GT
GTOK = GT * P
EPS = 1e-5


FIRST_U = (6, 7)
LAST_U = 20
TURN_U = (2, 3)
SUMS_U, SPREAD_U, OUT_U = 8, 12, 16
SHIFT_U = 22
SHIFT_BY_DVE = 1


SLOTS = [[(u, place) for u in range(FIRST_U[j], LAST_U + 1) for place in range(2) if place == 0 or u % 2 == 1] for j in range(2)]


def chunks_in(j, u, place):
    return [n for n in range(MAXES) if SLOTS[j][n * len(SLOTS[j]) // MAXES] == (u, place)]


class Steps:

    def __init__(self, engine, sem, base=0):
        self.engine, self.sem, self.base, self.n = engine, sem, base, 0

    def then(self, instruction, passed=None):
        instruction.then_inc(self.sem, 1)
        self.n += 1
        self.engine.wait_ge(self.sem, self.base + self.n)
        if passed:
            self.engine.sem_inc(passed, 1)


LN_STEPS = 14


def layernorm_rows(dve, steps, x_tiles, out_tiles, stats, mv, half_var, root, work, passed=None):
    n = len(x_tiles)
    for t in range(n - 1):
        dve.bn_stats(stats[:, t, :], x_tiles[t])
    steps.then(dve.bn_stats(stats[:, n - 1, :], x_tiles[n - 1]), passed)
    for t in range(n - 1):
        dve.bn_aggr(mv[:, t, :], stats[:, t, :])
    steps.then(dve.bn_aggr(mv[:, n - 1, :], stats[:, n - 1, :]))
    v = mv[:, 0:n, 1]
    dve.tensor_scalar(half_var[:, 0:n], v, EPS, -0.5, ALU.add, ALU.mult)
    steps.then(dve.tensor_scalar(work[:, 0:n], v, EPS, None, ALU.add))
    steps.then(dve.tensor_scalar(root[:, 0:n].bitcast(I32), work[:, 0:n].bitcast(I32), 1, None, ALU.logical_shift_right))
    steps.then(dve.tensor_scalar(root[:, 0:n].bitcast(I32), root[:, 0:n].bitcast(I32), -1.0, float(0x5F3759DF), ALU.mult, ALU.add))
    for _ in range(3):
        steps.then(dve.tensor_tensor(work[:, 0:n], root[:, 0:n], root[:, 0:n], ALU.mult))
        steps.then(dve.tensor_tensor(work[:, 0:n], work[:, 0:n], half_var[:, 0:n], ALU.mult))
        steps.then(dve.scalar_tensor_tensor(out=root[:, 0:n], in0=work[:, 0:n], scalar=1.5, in1=root[:, 0:n], op0=ALU.add, op1=ALU.mult))
    for t in range(n):
        last = dve.tensor_scalar(out_tiles[t], x_tiles[t], mv[:, t, 0:1], root[:, t:t + 1], ALU.subtract, ALU.mult)
    return last


def part_one(nc, a, x_res, ident, own, own_in):
    with ExitStack() as ctx:
        def sb(name, shape, dt=F32):
            return ctx.enter_context(nc.sbuf_tensor(name, shape, dt))

        def sem(name):
            return ctx.enter_context(nc.semaphore(name))

        to_query = sb("to_query", [P, 2, H, DC])
        to_out = sb("to_out", [P, HH, D])
        y_cols = sb("y_cols", [P, 2, TOK])
        cos = sb("cos", [P, KT, DC])
        sin = sb("sin", [P, KT, DC])
        raw = [sb(f"raw{j}", [P, KT, DC]) for j in range(2)]
        k_low = [sb(f"k_low{j}", [P, KEYS], F16) for j in range(2)]
        q_shift = [sb(f"q_shift{j}", [P, H, S], F16) for j in range(2)]
        ident16 = sb("ident16", [P, P], F16)
        pick = sb("pick", [P, QT, QT])
        unpick = sb("unpick", [P, QT // 2, P])
        consts_in = sem("consts_in")
        keys_in = [sem(f"keys_in{j}") for j in range(2)]

        def load(sp, b, j):
            src = a["ctx"][bass.ds(b, 1), :, :].rearrange("a l d -> (a l) d")
            sp.dma_start(raw[j][0:FULL_P, :, :], src[0:FULL_P * KT, :].rearrange("(p t) d -> p t d", t=KT)).then_inc(keys_in[j], 16)
            sp.dma_start(raw[j][FULL_P:P, :, :], src[L - (P - FULL_P) * KT:L, :].rearrange("(p t) d -> p t d", t=KT)).then_inc(keys_in[j], 16)

        def load_ahead(sp):
            sp.dma_start(cos[:, :, :], a["cos"]).then_inc(consts_in, 16)
            sp.dma_start(sin[:, :, :], a["sin"]).then_inc(consts_in, 16)
            sp.dma_start(ident16[:, :], a["ident16"]).then_inc(consts_in, 16)
            sp.dma_start(pick[:, :, :], a["pick"]).then_inc(consts_in, 16)
            sp.dma_start(unpick[:, :, :], a["unpick"]).then_inc(consts_in, 16)
            for j in range(2):
                sp.dma_start(k_low[j][DC:P, :], a["k_rows"]).then_inc(consts_in, 16)
                sp.dma_start(q_shift[j][DC:P, :, :], a["q_rows"]).then_inc(consts_in, 16)
            for b in range(2):
                load(sp, b, b)

        fold(nc, a, x_res, ident, to_query, to_out, y_cols, load_ahead)
        turned = sb("turned", [P, KT, DC])
        kv_pair = sb("kv_pair", [P, KT, 2, DC])
        kv = [sb(f"kv{j}", [P, KT, DC]) for j in range(2)]
        k_high = [sb(f"k_high{j}", [P, KEYS], F16) for j in range(2)]
        q_both = [sb(f"q_both{j}", [P, H, S], F16) for j in range(2)]
        q_hi = sb("q_hi", [P, H // 2, P], F16)
        q_lo = sb("q_lo", [P, H // 2, P], F16)
        maxes = sb("maxes", [P, QT, NCH])
        neg_max = sb("neg_max", [P, QT])
        neg_max2 = sb("neg_max2", [P, QT, 2], F16)
        probs = [sb(f"probs{r}", [P, 2, 512]) for r in range(RING)]
        sums = [sb(f"sums{j}", [P, 2, 512]) for j in range(2)]
        held = sb("held", [P, 512])
        inv = sb("inv", [P, P])
        mixed = sb("mixed", [P, HH, 2, S])

        s_bank = [ctx.enter_context(nc.psum_tensor(f"s_bank{k}", [P, 512], F32)) for k in range(2)]
        m_bank = [ctx.enter_context(nc.psum_tensor(f"m_bank{k}", [P, 512], F32)) for k in range(MR)]
        v_bank = ctx.enter_context(nc.psum_tensor("v_bank", [P, 512], F32))
        w_bank = [ctx.enter_context(nc.psum_tensor(f"w_bank{k}", [P, 512], F32)) for k in range(2)]

        rope_products = sem("rope_products")
        rope_done = sem("rope_done")
        const_made = sem("const_made")
        query_ready = sem("query_ready")
        query_high = sem("query_high")
        query_low = sem("query_low")
        stacked = sem("stacked")
        turned_ready = sem("turned_ready")
        key_high = sem("key_high")
        key_low = sem("key_low")
        chunk_ready = sem("chunk_ready")
        chunk_max = sem("chunk_max")
        max_steps = sem("max_steps")
        shift_known = sem("shift_known")
        shift_ready = sem("shift_ready")
        shift_placed = [sem(f"shift_placed{c}") for c in range(2)]
        score_ready = sem("score_ready")
        exp_done = sem("exp_done")
        value_done = sem("value_done")
        held_done = sem("held_done")
        sum_added = sem("sum_added")
        sum_ready = sem("sum_ready")
        inverted = sem("inverted")
        spread_ready = sem("spread_ready")
        doubled = sem("doubled")
        kv_filled = sem("kv_filled")
        norm_done = sem("norm_done")
        out_ready = sem("out_ready")
        x_added = sem("x_added")
        heads_summed = sem("heads_summed")

        block = ctx.enter_context(nc.Block())

        def walk(engine, first, step):
            first()
            step(0, True, False)
            with engine.Fori(1, NT - 1) as i:
                step(i, False, False)
            step(NT - 1, False, True)

        @block.sync
        def _(sp):
            def step(i, is_first, is_last):
                for j in range(2):
                    if not is_last:
                        sp.wait_ge(rope_done, 2 * i + j + 1)
                        load(sp, 2 * i + j + 2, j)

            load_own(sp, a, own, own_in)
            walk(sp, lambda: None, step)
            sp.wait_ge(own_in, 16 * len(OWN))

        @block.gpsimd
        def _(pool):
            def step(i, is_first, is_last):
                for j in range(2):
                    b = 2 * i + j
                    for k in range(1, KT):
                        pool.wait_ge(exp_done, UNITS * b + 2 * k + 2)
                        if k == 1:
                            if not is_first:
                                pool.wait_ge(sum_ready, b - 1)
                            before = probs[0]
                        else:
                            pool.wait_ge(sum_added, (KT - 1) * b + k - 1)
                            before = sums[j]
                        pool.tensor_tensor(sums[j][:, :, :], before[:, :, :], probs[k % RING][:, :, :], ALU.add).then_inc(sum_added, 1)

            walk(pool, lambda: None, step)

        def shift_copy(engine, b, j, c):
            engine.wait_ge(shift_ready, 2 * b + c + 1)
            dst, src = q_shift[j][DC:DC + 2, 8 * c:8 * c + 8, :].rearrange("p h s -> p (h s)"), w_bank[c][0:2, :]
            op = engine.activation(dst, src, ACT.Copy) if c < 2 - SHIFT_BY_DVE else engine.tensor_copy(dst, src)
            op.then_inc(shift_placed[c], 1)

        @block.scalar
        def _(act):
            def query_copy(tile):
                for piece in range(2):
                    act.wait_ge(query_ready, 2 * tile + piece + 1)
                    if not (isinstance(tile, int) and tile == 0):
                        act.wait_ge(stacked, 2 * tile)
                    act.activation(q_hi[:, 4 * piece:4 * piece + 4, :].rearrange("p a t -> p (a t)"), w_bank[piece][:, :], ACT.Copy).then_inc(query_high, 1)

            def key_copy(b, j, n):
                w = min(4 * P, KEYS - 512 * n)
                act.wait_ge(turned_ready, 4 * b + n + 1)
                act.activation(k_high[j][:, 512 * n:512 * n + w], w_bank[n % 2][:, 0:w], ACT.Copy).then_inc(key_high, 1)

            def double(b, j):
                act.wait_ge(rope_done, b + 1)
                act.activation(kv_pair[:, :, 1, :], kv_pair[:, :, 0, :], ACT.Copy).then_inc(doubled, 1)

            def fill_kv(b, j, first_use=False):
                if not first_use:
                    act.wait_ge(value_done, KT * (b - 1))
                act.activation(kv[j][:, :, :], kv_pair[:, :, 0, :], ACT.Copy).then_inc(kv_filled, 1)

            def hold(b, first_use=False):
                act.wait_ge(value_done, KT * (b + 1))
                if not first_use:
                    act.wait_ge(norm_done, b)
                act.activation(held[:, :], v_bank[:, :], ACT.Copy).then_inc(held_done, 1)

            def first():
                act.wait_ge(consts_in, 16 * 9)
                query_copy(0)
                double(0, 0)
                fill_kv(0, 0, first_use=True)
                for n in range(4):
                    key_copy(0, 0, n)
                for c in range(2 - SHIFT_BY_DVE):
                    shift_copy(act, 0, 0, c)

            def step(i, is_first, is_last):
                for j in range(2):
                    b = 2 * i + j
                    ahead = not (is_last and j == 1)
                    if ahead:
                        double(b + 1, 1 - j)
                    for u in range(UNITS):
                        k, half = divmod(u, 2)
                        act.wait_ge(score_ready, UNITS * b + u + 1)
                        if half == 0 and not (is_first and j == 0 and k < RING):
                            last = k - RING
                            batch = b
                            if last < 0:
                                last = max(t for t in range(k, KT, RING))
                                batch = b - 1
                            act.wait_ge(value_done, KT * batch + last + 1)
                            act.wait_ge(sum_added, (KT - 1) * batch + max(last, 1))
                        act.activation(probs[k % RING][:, half, :], s_bank[u % 2][:, :], ACT.Exp).then_inc(exp_done, 1)
                        if u == 0 and not (is_first and j == 0):
                            hold(b - 1, first_use=is_first and j == 1)
                        if ahead:
                            if j == 1 and u == 1:
                                query_copy(i + 1)
                            if u == 1:
                                fill_kv(b + 1, 1 - j, first_use=is_first and j == 0)
                            if u == SHIFT_U:
                                for c in range(2 - SHIFT_BY_DVE):
                                    shift_copy(act, b + 1, 1 - j, c)
                            if 0 <= u - TURN_U[j] < 4:
                                key_copy(b + 1, 1 - j, u - TURN_U[j])

            walk(act, first, step)
            hold(B - 1)

        @block.vector
        def _(dve):
            def rope(b, j):
                dve.wait_ge(keys_in[j], 32 * ((b - j) // 2 + 1) if isinstance(b, int) else 16 * (b - j) + 32)
                if not (isinstance(b, int) and b == 0):
                    dve.wait_ge(turned_ready, 4 * b)
                    dve.wait_ge(kv_filled, b)
                dve.tensor_tensor(kv_pair[:, :, 0, :], raw[j][:, :, :], cos[:, :, :], ALU.mult).then_inc(rope_products, 1)
                dve.tensor_tensor(turned[:, :, 0:32], raw[j][:, :, 32:64], sin[:, :, 0:32], ALU.mult).then_inc(rope_products, 1)
                dve.tensor_tensor(turned[:, :, 32:64], raw[j][:, :, 0:32], sin[:, :, 32:64], ALU.mult).then_inc(rope_products, 1)
                dve.wait_ge(rope_products, 3 * b + 3)
                dve.tensor_tensor(kv_pair[:, :, 0, :], kv_pair[:, :, 0, :], turned[:, :, :], ALU.add).then_inc(rope_done, 1)

            def query_lows(tile):
                for piece in range(2):
                    dve.wait_ge(query_high, 2 * tile + piece + 1)
                    hi = q_hi[:, 4 * piece:4 * piece + 4, :].rearrange("p a t -> p (a t)")
                    lo = q_lo[:, 4 * piece:4 * piece + 4, :].rearrange("p a t -> p (a t)")
                    dve.tensor_tensor(lo, w_bank[piece][:, :], hi, ALU.subtract).then_inc(query_low, 1)

            def stack(b, j):
                if not (isinstance(b, int) and b < 2):
                    dve.wait_ge(score_ready, UNITS * (b - 1))
                dve.wait_ge(query_low, 2 * (b // 2) + 2 if isinstance(b, int) else b - j + 2)
                for e in range(2):
                    src = slice(DC * e, DC * e + DC)
                    dve.tensor_copy(q_both[j][0:DC, e::2, :], q_hi[src, :, S * j:S * j + S])
                    dve.tensor_copy(q_shift[j][0:DC, e::2, :], q_hi[src, :, S * j:S * j + S])
                    last = dve.tensor_copy(q_both[j][DC:P, e::2, :], q_lo[src, :, S * j:S * j + S])
                last.then_inc(stacked, 1)

            def key_lows(b, j):
                for n in range(4):
                    w = min(4 * P, KEYS - 512 * n)
                    dve.wait_ge(key_high, 4 * b + n + 1)
                    dve.tensor_tensor(k_low[j][0:DC, 512 * n:512 * n + w], w_bank[n % 2][0:DC, 0:w], k_high[j][0:DC, 512 * n:512 * n + w], ALU.subtract).then_inc(key_low, 1)

            def chunk(b, n):
                dve.wait_ge(chunk_ready, MAXES * b + n + 1)
                dve.tensor_reduce(maxes[:, n // NCH, n % NCH:n % NCH + 1], m_bank[n % MR][:, 0:CH], AX.X, ALU.max).then_inc(chunk_max, 1)

            def shift(b):
                dve.wait_ge(chunk_max, MAXES * (b + 1))
                dve.tensor_reduce(neg_max[:, :], maxes[:, :, :], AX.X, ALU.max, negate=True).then_inc(max_steps, 1)
                dve.wait_ge(max_steps, 2 * b + 1)
                dve.tensor_copy(neg_max2[:, :, 0], neg_max[:, :]).then_inc(max_steps, 1)
                dve.wait_ge(max_steps, 2 * b + 2)
                dve.tensor_tensor(neg_max2[:, :, 1], neg_max[:, :], neg_max2[:, :, 0], ALU.subtract).then_inc(shift_known, 1)

            def invert(b):
                dve.wait_ge(sum_ready, b + 1)
                dve.reciprocal(inv[0:QT, :], w_bank[0][0:QT, 0:P]).then_inc(inverted, 1)

            def normalise(b, j, tile):
                dve.wait_ge(spread_ready, b + 1)
                dve.wait_ge(held_done, b + 1)
                if j == 0 and not (isinstance(b, int) and b == 0):
                    dve.wait_ge(out_ready, tile)
                dve.tensor_tensor(mixed[:, :, j, :], held[:, :].rearrange("p (h s) -> p h s", h=HH),
                                  w_bank[1][:, :].rearrange("p (h s) -> p h s", h=HH), ALU.mult).then_inc(norm_done, 1)

            def add_out(tile):
                dve.wait_ge(out_ready, tile + 1)
                xt = x_res[:, bass.ds(tile, 1), :].rearrange("p a d -> p (a d)")
                dve.tensor_tensor(xt, w_bank[0][:, 0:D], xt, ALU.add).then_inc(x_added, 1)

            def first():
                dve.memset(inv[:, :], 0.0).then_inc(const_made, 1)
                dve.wait_ge(consts_in, 16 * 9)
                rope(0, 0)
                query_lows(0)
                stack(0, 0)
                key_lows(0, 0)
                for n in range(MAXES):
                    chunk(0, n)
                shift(0)
                for c in range(2 - SHIFT_BY_DVE, 2):
                    shift_copy(dve, 0, 0, c)
                rope(1, 1)

            def step(i, is_first, is_last):
                for j in range(2):
                    b = 2 * i + j
                    ahead = not (is_last and j == 1)
                    behind = not (is_first and j == 0)
                    if ahead:
                        if j == 1:
                            query_lows(i + 1)
                        stack(b + 1, 1 - j)
                        key_lows(b + 1, 1 - j)
                    for u in range(UNITS):
                        if ahead:
                            for n in chunks_in(j, u, 0) + chunks_in(j, u, 1):
                                chunk(b + 1, n)
                        if behind and u == SUMS_U:
                            invert(b - 1)
                        if behind and u == SPREAD_U:
                            normalise(b - 1, 1 - j, i)
                        if u == OUT_U and j == 0 and not is_first:
                            add_out(i - 1)
                    if ahead:
                        shift(b + 1)
                        for c in range(2 - SHIFT_BY_DVE, 2):
                            shift_copy(dve, b + 1, 1 - j, c)
                    if not is_last:
                        rope(b + 2, j)

            walk(dve, first, step)
            dve.wait_ge(own_in, 16 * len(OWN))
            dve.tensor_reduce(own["wo1_sum"][:, :], own["wo1"][:, :, :].rearrange("p h d -> p d h"), AX.X, ALU.add).then_inc(heads_summed, 1)
            invert(B - 1)
            normalise(B - 1, 1, NT - 1)
            add_out(NT - 1)

        @block.tensor
        def _(pe):
            def queries(tile, after):
                for piece in range(2):
                    after(piece)
                    for pair in range(4):
                        for c in range(2):
                            h = 8 * piece + 2 * pair
                            last = pe.matmul(w_bank[piece][:, P * pair:P * pair + P],
                                             to_query[:, c, h:h + 2, :].rearrange("p h d -> p (h d)"),
                                             y_cols[:, c, bass.ds(tile * P, P)], start=(c == 0), stop=(c == 1))
                    last.then_inc(query_ready, 1)

            def turn_keys(b, j, n):
                for t in range(4 * n, min(4 * n + 4, KT)):
                    last = pe.transpose(w_bank[n % 2][:, P * (t % 4):P * (t % 4) + P],
                                        kv_pair[:, t, :, :].rearrange("p a d -> p (a d)"), ident[:, :])
                last.then_inc(turned_ready, 1)

            def chunk(b, j, n, first_batch=False):
                if n >= MR:
                    pe.wait_ge(chunk_max, MAXES * b + n - MR + 1)
                elif not first_batch:
                    pe.wait_ge(chunk_max, MAXES * b)
                g, c = divmod(n, NCH)
                pe.matmul(m_bank[n % MR][:, 0:CH], q_both[j][:, 2 * g:2 * g + 2, :].rearrange("p h s -> p (h s)"),
                          k_high[j][:, CH * c:CH * c + CH], start=True, stop=True).then_inc(chunk_ready, 1)

            def shift_rows(b, j):
                pe.wait_ge(shift_known, b + 1)
                for c in range(2):
                    for g in range(4 * c, 4 * c + 4):
                        last = pe.matmul(w_bank[c][0:2, P * (g % 4):P * (g % 4) + P], neg_max2[:, g, :], ident16[:, :], start=True, stop=True)
                    last.then_inc(shift_ready, 1)

            def score(b, j, u):
                t, half = divmod(u, 2)
                keys = slice(P * t, P * t + P)
                cols = slice(8 * half, 8 * half + 8)
                pe.matmul(s_bank[u % 2][:, :], k_high[j][:, keys], q_both[j][:, cols, :].rearrange("p h s -> p (h s)"), start=True, stop=False)
                pe.matmul(s_bank[u % 2][:, :], k_low[j][:, keys], q_shift[j][:, cols, :].rearrange("p h s -> p (h s)"), start=False, stop=True).then_inc(score_ready, 1)

            def values(b, j, t):
                for half in range(2):
                    last = pe.matmul(v_bank[DC * half:DC * half + DC, :], kv[j][:, t, :], probs[t % RING][:, half, :],
                                     start=(t == 0), stop=(t == KT - 1))
                last.then_inc(value_done, 1)

            def add_keys(b, j):
                pe.wait_ge(sum_added, (KT - 1) * (b + 1))
                for g in range(QT):
                    last = pe.matmul(w_bank[0][0:QT, 0:P], pick[:, g, :], sums[j][:, g // 4, P * (g % 4):P * (g % 4) + P], start=(g == 0), stop=(g == QT - 1))
                last.then_inc(sum_ready, 1)

            def spread_inverse(b):
                pe.wait_ge(inverted, b + 1)
                for g in range(QT // 2):
                    last = pe.matmul(w_bank[1][:, P * g:P * g + P], unpick[:, g, :], inv[:, :], start=True, stop=True)
                last.then_inc(spread_ready, 1)

            def project(tile):
                pe.wait_ge(norm_done, 2 * tile + 2)
                for h in range(HH):
                    last = pe.matmul(w_bank[0][:, 0:D], mixed[:, h, :, :].rearrange("p j s -> p (j s)"), to_out[:, h, :], start=(h == 0), stop=(h == HH - 1))
                last.then_inc(out_ready, 1)

            def first():
                pe.wait_ge(consts_in, 16 * 9)
                queries(0, lambda piece: None)
                pe.wait_ge(doubled, 1)
                for n in range(4):
                    if n < 2:
                        pe.wait_ge(query_low, n + 1)
                    else:
                        pe.wait_ge(key_low, n - 1)
                    turn_keys(0, 0, n)
                pe.wait_ge(key_high, 4)
                pe.wait_ge(stacked, 1)
                for n in range(MAXES):
                    chunk(0, 0, n, first_batch=True)
                pe.wait_ge(key_low, 4)
                shift_rows(0, 0)
                pe.wait_ge(const_made, 1)

            def step(i, is_first, is_last):
                for j in range(2):
                    b = 2 * i + j
                    nb = b + 1
                    ahead = not (is_last and j == 1)
                    behind = not (is_first and j == 0)
                    for u in range(UNITS):
                        if u < 2:
                            pe.wait_ge(shift_placed[u], b + 1)
                        if not (is_first and j == 0 and u < 2):
                            pe.wait_ge(exp_done, UNITS * b + u - 1)
                        score(b, j, u)
                        if u == 0 and behind:
                            pe.wait_ge(exp_done, UNITS * b)
                            values(b - 1, 1 - j, KT - 1)
                        if ahead and j == 1 and u == 0:
                            queries(i + 1, lambda piece: pe.wait_ge(shift_placed[piece], b + 1))
                        if ahead and 0 <= u - TURN_U[j] < 4:
                            n = u - TURN_U[j]
                            if n == 0:
                                pe.wait_ge(doubled, nb + 1)
                            if n < 2:
                                if j == 1:
                                    pe.wait_ge(query_low, 2 * (i + 1) + n + 1)
                            else:
                                pe.wait_ge(key_low, 4 * nb + n - 1)
                            turn_keys(nb, 1 - j, n)
                        if ahead:
                            for n in chunks_in(j, u, 0):
                                if n == 0:
                                    pe.wait_ge(stacked, nb + 1)
                                if n < NCH:
                                    pe.wait_ge(key_high, 4 * nb + (CH * (n + 1) - 1) // 512 + 1)
                                chunk(nb, 1 - j, n)
                        t = u // 2
                        if u % 2 == 1 and t >= 1:
                            pe.wait_ge(exp_done, UNITS * b + 2 * t)
                            if t == 1:
                                if behind:
                                    pe.wait_ge(held_done, b)
                                pe.wait_ge(kv_filled, b + 1)
                            values(b, j, t - 1)
                        if behind and u == SUMS_U:
                            if ahead:
                                pe.wait_ge(key_low, 4 * nb + 3)
                            add_keys(b - 1, 1 - j)
                        if behind and u == SPREAD_U:
                            if ahead:
                                pe.wait_ge(key_low, 4 * nb + 4)
                            spread_inverse(b - 1)
                        if ahead:
                            for n in chunks_in(j, u, 1):
                                if n < NCH:
                                    pe.wait_ge(key_high, 4 * nb + (CH * (n + 1) - 1) // 512 + 1)
                                chunk(nb, 1 - j, n)
                        if u == OUT_U and j == 0 and not is_first:
                            project(i - 1)
                        if ahead and u == SHIFT_U:
                            if j == 0 and not is_first:
                                pe.wait_ge(x_added, i)
                            elif behind:
                                pe.wait_ge(norm_done, b)
                            shift_rows(nb, 1 - j)

            walk(pe, first, step)
            pe.wait_ge(exp_done, UNITS * B)
            values(B - 1, 1, KT - 1)
            pe.wait_ge(norm_done, B - 1)
            add_keys(B - 1, 1)
            spread_inverse(B - 1)
            project(NT - 1)


def fold(nc, a, x_res, ident, to_query, to_out, y_cols, load_ahead):
    HG = 8
    with ExitStack() as ctx:
        def sb(name, shape, dt=F32):
            return ctx.enter_context(nc.sbuf_tensor(name, shape, dt))

        def sem(name):
            return ctx.enter_context(nc.semaphore(name))

        wq = sb("wq", [P, H, D])
        wkc = sb("wkc", [96, 2, H, P])
        wqr = sb("wqr", [DC, H, 192])
        wkr = sb("wkr", [DC, H, DC])
        wkv = sb("wkv", [P, H, DC])
        wo = sb("wo", [P, H, D])
        qr_kr = sb("qr_kr", [96, 2, H, DC])
        kc_kr = sb("kc_kr", [P, H, DC])
        y = sb("y", [P, NG, GT, D])
        stats = sb("stats", [P, GT, 6])
        mv = sb("mv", [P, GT, 2])
        half_var = sb("half_var", [P, GT])
        root = sb("root", [P, GT])
        work = sb("work", [P, GT])
        bank = [ctx.enter_context(nc.psum_tensor(f"fold_bank{k}", [P, 512], F32)) for k in range(8)]

        ident_in = sem("ident_in")
        x_in = [sem(f"x_in{g}") for g in range(NG)]
        key_weights_in = sem("key_weights_in")
        wkc_in = sem("wkc_in")
        wq_in = sem("wq_in")
        out_weights_in = sem("out_weights_in")
        job_ready = sem("job_ready")
        job_copied = sem("job_copied")
        ln_steps = sem("ln_steps")
        rows_ready = sem("rows_ready")
        cols_ready = sem("cols_ready")
        cols_copied = sem("cols_copied")
        block = ctx.enter_context(nc.Block())

        dests = [qr_kr[:, c, HG * g:HG * g + HG, :] for c in range(2) for g in range(2)]
        dests += [kc_kr[:, HG * g:HG * g + HG, :] for g in range(2)]
        dests += [to_query[:, c, HG * g:HG * g + HG, :] for c in range(2) for g in range(2)]
        dests += [to_out[:, 2 * g:2 * g + 2, :] for g in range(HH // 2)]
        FB = 4

        @block.sync
        def _(sp):
            def load_x(g):
                tiles = slice(GT * g, GT * g + GT)
                sp.dma_start(x_res[:, tiles, :], a["x"].rearrange("(t p) d -> p t d", p=P)[:, tiles, :]).then_inc(x_in[g], 16)

            sp.dma_start(wqr[:, :, :], a["wqr"]).then_inc(key_weights_in, 16)
            sp.dma_start(wkr[:, :, :], a["wkr"]).then_inc(key_weights_in, 16)
            sp.dma_start(ident[:, :], a["ident"]).then_inc(ident_in, 16)
            load_x(0)
            sp.dma_start(wkc[:, :, :, :], a["wkc"]).then_inc(wkc_in, 16)
            load_x(1)
            sp.dma_start(wq[:, :, :], a["wq"]).then_inc(wq_in, 16)
            load_x(2)
            load_x(3)
            sp.dma_start(wkv[:, :, :], a["wkv"]).then_inc(out_weights_in, 16)
            sp.dma_start(wo[:, :, :], a["wo"]).then_inc(out_weights_in, 16)
            load_ahead(sp)

        @block.tensor
        def _(pe):
            def turn_rows(g):
                pe.wait_ge(rows_ready, g + 1)
                for c in range(2):
                    if g >= 2:
                        pe.wait_ge(cols_copied, 2 * (g - 2) + c + 1)
                    out = bank[FB + (2 * g + c) % 4]
                    for t in range(GT):
                        last = pe.transpose(out[:, P * t:P * t + P], y[:, g, t, P * c:P * c + P], ident[:, :])
                    last.then_inc(cols_ready, 1)

            pe.wait_ge(key_weights_in, 32)
            n = 0

            def begin():
                if n >= FB:
                    pe.wait_ge(job_copied, n - FB + 1)
                return bank[n % FB]

            for c in range(2):
                for g in range(2):
                    out = begin()
                    for h in range(HG):
                        last = pe.matmul(out[0:96, DC * h:DC * h + DC], wqr[:, HG * g + h, 96 * c:96 * c + 96], wkr[:, HG * g + h, :], start=True, stop=True)
                    last.then_inc(job_ready, 1)
                    n += 1
            pe.wait_ge(wkc_in, 16)
            for g in range(2):
                out = begin()
                pe.wait_ge(job_copied, 4)
                for h in range(HG):
                    for c in range(2):
                        last = pe.matmul(out[:, DC * h:DC * h + DC], wkc[:, c, HG * g + h, :], qr_kr[:, c, HG * g + h, :], start=(c == 0), stop=(c == 1))
                last.then_inc(job_ready, 1)
                n += 1
            pe.wait_ge(ident_in, 16)
            turn_rows(0)
            pe.wait_ge(wq_in, 16)
            for c in range(2):
                for g in range(2):
                    out = begin()
                    pe.wait_ge(job_copied, 6)
                    for h in range(HG):
                        last = pe.matmul(out[:, DC * h:DC * h + DC], wq[:, HG * g + h, P * c:P * c + P], kc_kr[:, HG * g + h, :], start=True, stop=True)
                    last.then_inc(job_ready, 1)
                    n += 1
            turn_rows(1)
            turn_rows(2)
            turn_rows(3)
            pe.wait_ge(out_weights_in, 32)
            for g in range(HH // 2):
                out = begin()
                for h in range(2 * g, 2 * g + 2):
                    for half in range(2):
                        last = pe.matmul(out[DC * half:DC * half + DC, D * (h - 2 * g):D * (h - 2 * g) + D],
                                         wkv[:, HH * half + h, :], wo[:, HH * half + h, :], start=True, stop=True)
                last.then_inc(job_ready, 1)
                n += 1

        @block.scalar
        def _(act):
            def job(n):
                act.wait_ge(job_ready, n + 1)
                src = bank[n % FB][0:dests[n].shape[0], :]
                act.activation(dests[n], src.rearrange("p (h d) -> p h d", d=dests[n].shape[-1]), ACT.Copy).then_inc(job_copied, 1)

            def cols(g):
                for c in range(2):
                    act.wait_ge(cols_ready, 2 * g + c + 1)
                    act.activation(y_cols[:, c, GTOK * g:GTOK * g + GTOK], bank[FB + (2 * g + c) % 4][:, :], ACT.Copy).then_inc(cols_copied, 1)

            for n in range(6):
                job(n)
            cols(0)
            for n in range(6, 10):
                job(n)
            for g in range(1, NG):
                cols(g)
            for n in range(10, len(dests)):
                job(n)

        @block.vector
        def _(dve):
            for g in range(NG):
                dve.wait_ge(x_in[g], 16)
                steps = Steps(dve, ln_steps, LN_STEPS * g)
                last = layernorm_rows(dve, steps, [x_res[:, GT * g + t, :] for t in range(GT)], [y[:, g, t, :] for t in range(GT)],
                                      stats, mv, half_var, root, work)
                assert steps.n == LN_STEPS
                last.then_inc(rows_ready, 1)


PARTS = 5
NB0, TOP0 = 16, 4
NE, TOP1 = 8, 2
HF = 1024
HC = HF // P
HD = D // H
HPC = P // HD
PV = 2 * HD + 2
SM = GT * 2
RANK_STEPS = 5
ATT_STEPS = 4
GATE_STEPS = 6
FFN_BANKS = (2, 3, 4, 7)
XV_BANKS = (7, 2, 3, 4)
XR = 3


def rank_below(dve, steps, logits, n, tri, diff, order, rank, keep, top):
    shape = [P, GT, n, n]
    flat = [t.rearrange("p t i j -> p (t i j)") for t in (diff, order)]
    steps.then(dve.tensor_tensor(diff, logits.unsqueeze(2).broadcast_to(shape), logits.unsqueeze(3).broadcast_to(shape), ALU.subtract))
    steps.then(dve.scalar_tensor_tensor(out=order.rearrange("p t i j -> p t (i j)"), in0=diff.rearrange("p t i j -> p t (i j)"), scalar=0.0,
                                        in1=tri.unsqueeze(1).broadcast_to([P, GT, n * n]), op0=ALU.is_equal, op1=ALU.mult))
    steps.then(dve.scalar_tensor_tensor(out=flat[1], in0=flat[0], scalar=0.0, in1=flat[1], op0=ALU.is_gt, op1=ALU.add))
    steps.then(dve.tensor_reduce(rank, order, AX.X, ALU.add))
    steps.then(dve.tensor_scalar(keep, rank, top - 0.5, None, ALU.is_lt))


def part_two(nc, a, out_dram, x_res, ident, own):
    with ExitStack() as ctx:
        def sb(name, shape, dt=F32):
            return ctx.enter_context(nc.sbuf_tensor(name, shape, dt))

        def sem(name):
            return ctx.enter_context(nc.semaphore(name))

        att_w = [sb("att0_w", [P, 2, 4, P]), sb("att1_w", [P, 2, 2, P])]
        att_b = [sb("att0_b", [P, 4]), sb("att1_b", [P, 2])]
        router0 = sb("router0", [P, 2, NB0])
        router0_b = sb("router0_b", [P, NB0])
        w1 = sb("w1", [P, 2, HF])
        w2 = sb("w2", [P, HC, D])
        x_wq = sb("x_wq", [P, 2, D])
        x_wk = sb("x_wk", [DC, D])
        x_wv = sb("x_wv", [DC, D])
        x_wo = sb("x_wo", [P, 2, D])
        router1 = sb("router1", [P, 2, NE])
        experts = sb("experts", [P, 2, NE, D])
        expert_b = sb("expert_b", [NE, D])
        block_mask = sb("block_mask", [P, P])
        causal = sb("causal", [P, S])
        head_mask = sb("head_mask", [P, HPC])
        pair_mask = sb("pair_mask", [P, D])
        tri0 = sb("tri0", [P, NB0 * NB0])
        tri1 = sb("tri1", [P, NE * NE])
        spread = sb("spread", [NB0, HC, P], F16)
        att_vo = [sb(f"att{s}_vo", [P, 2, D]) for s in range(2)]
        att_row = [sb(f"att{s}_row", [P, D]) for s in range(2)]

        bank = [ctx.enter_context(nc.psum_tensor(f"bank{k}", [P, 512], F32)) for k in range(8)]
        loads = {
            "att0_in": [(att_w[0][:, :, :, :], "att0_w"), (att_b[0][:, :], "att0_b"), (block_mask[:, :], "block_mask")],
            "ffn_in": [(router0[:, :, :], "router0"), (router0_b[:, :], "router0_b"), (tri0[:, :], "tri0"), (w1[:, :, :], "w1"), (spread[:, :, :], "spread"), (w2[:, :, :], "w2")],
            "cross_in": [(x_wq[:, :, :], "x_wq"), (x_wk[:, :], "x_wk"), (x_wv[:, :], "x_wv"), (head_mask[:, :], "head_mask"), (pair_mask[:, :], "pair_mask"),
                         (causal[:, :], "causal"), (x_wo[:, :, :], "x_wo")],
            "att1_in": [(att_w[1][:, :, :, :], "att1_w"), (att_b[1][:, :], "att1_b")],
            "experts_in": [(router1[:, :, :], "router1"), (tri1[:, :], "tri1"), (experts[:, :, :, :], "experts"), (expert_b[:, :], "expert_b")],
        }
        arrived = {name: sem(name) for name in loads}

        def wait_in(engine, name):
            engine.wait_ge(arrived[name], 16 * len(loads[name]))

        def load_weights(sp):
            for name, pairs in loads.items():
                for dst, source in pairs:
                    sp.dma_start(dst, a[source]).then_inc(arrived[name], 16)

        y = [sb(f"y2_{r}", [P, GT, D]) for r in range(2)]
        stats = sb("stats2", [P, GT, 6])
        mv = sb("mv2", [P, GT, 2])
        half_var = sb("half_var2", [P, GT])
        root = sb("root2", [P, GT])
        work = sb("work2", [P, GT])
        ln_steps = sem("ln2_steps")
        rows_ready = sem("rows2_ready")

        def normalise_first(dve):
            layernorm_rows(dve, Steps(dve, ln_steps), [x_res[:, t, :] for t in range(GT)], [y[0][:, t, :] for t in range(GT)],
                           stats, mv, half_var, root, work).then_inc(rows_ready, 1)

        fold_values(nc, bank, own, att_vo, att_row, load_weights, normalise_first)

        yt = sb("yt", [P, 2, GTOK])
        lin = sb("lin", [P, 4, GTOK])
        vals = sb("vals", [P, GT, D])
        masked = sb("masked", [P, GT, P])
        att_shift = sb("att_shift", [P, GT])
        att_sum = sb("att_sum", [P, GT])
        att_inv = sb("att_inv", [P, GT])
        att_p = sb("att_p", [P, GT, P])
        att_pt = sb("att_pt", [P, GTOK])
        logits = sb("logits", [P, GT, NB0])
        diff = sb("diff", [P, GT * NB0 * NB0])
        order = sb("order", [P, GT * NB0 * NB0])
        rank = sb("rank", [P, GT, NB0])
        keep = sb("keep", [P, GT, NB0])
        keep_t = sb("keep_t", [NB0, GTOK], F16)
        hidden = own["wo1"][:, :, :].rearrange("p (c a) d -> p c (a d)", c=HC)
        ctx_first = sb("ctx_first", [DC, 2 * GT, 2, S])
        xq = sb("xq", [P, 2, GTOK])
        xk1 = sb("xk1", [P, GTOK])
        wide_k = [sb(f"wide_k{c}", [P, 2 * GT, HPC, S]) for c in range(2)]
        pair_v = sb("pair_v", [P, 2 * GT, HPC, PV])
        xs = [sb(f"xs{k}", [P, HPC, S]) for k in range(XR)]
        xmax = sb("xmax", [P, XR, HPC])
        xp = [sb(f"xp{k}", [P, HPC * S]) for k in range(2)]
        xpt = [sb(f"xpt{k}", [P, 4, P]) for k in range(2)]
        xinv = sb("xinv", [P, GT, H])
        xo = vals
        xot = xq
        top = sb("top", [P, GT])
        gate = sb("gate", [P, GT, NE])
        gsum = sb("gsum", [P, GT])
        ginv = sb("ginv", [P, GT])
        gate_t = sb("gate_t", [NE, GTOK])

        dve_passed = sem("dve_passed")
        pool_passed = sem("pool_passed")
        cols_ready = sem("cols2_ready")
        cols_copied = sem("cols2_copied")
        bias_added = sem("bias_added")
        lin_ready = sem("lin_ready")
        lin_copied = sem("lin_copied")
        vals_ready = sem("vals_ready")
        vals_copied = sem("vals_copied")
        vals_by_dve = sem("vals_by_dve")
        att_ready = sem("att_ready")
        att_steps = sem("att_steps")
        att_exp = sem("att_exp")
        att_turned = sem("att_turned")
        att_turned_copied = sem("att_turned_copied")
        att_mixed = sem("att_mixed")
        att_x = sem("att_x")
        x_new = sem("x_new")
        logits0_ready = sem("logits0_ready")
        logits_steps = sem("logits_steps")
        rank_steps = sem("rank_steps")
        hidden_ready = sem("hidden_ready")
        gelu_done = sem("gelu_done")
        keep_turned = sem("keep_turned")
        keep_copied = sem("keep_copied")
        spread_ready = sem("spread_ready")
        hidden_masked = sem("hidden_masked")
        ffn_ready = sem("ffn_ready")
        first_in = sem("first_in")
        pair_v_const = sem("pair_v_const")
        xq_ready = sem("xq_ready")
        xk_ready = sem("xk_ready")
        xv_ready = sem("xv_ready")
        xq_copied = sem("xq_copied")
        xk1_copied = sem("xk1_copied")
        wide0_done = sem("wide0_done")
        wide1_done = sem("wide1_done")
        pair_v_done = sem("pair_v_done")
        xs_ready = sem("xs_ready")
        xs_masked = sem("xs_masked")
        xs_max = sem("xs_max")
        xs_shifted = sem("xs_shifted")
        xp_done = sem("xp_done")
        xpt_ready = sem("xpt_ready")
        xpt_copied = sem("xpt_copied")
        xo_ready = sem("xo_ready")
        xinv_done = sem("xinv_done")
        xo_done = sem("xo_done")
        xot_ready = sem("xot_ready")
        xot_by_act = sem("xot_by_act")
        xot_by_dve = sem("xot_by_dve")
        xout_ready = sem("xout_ready")
        logits1_ready = sem("logits1_ready")
        gate_steps = sem("gate_steps")
        gate_shifted = sem("gate_shifted")
        gate_exp = sem("gate_exp")
        gate_turned = sem("gate_turned")
        gate_copied = sem("gate_copied")
        gate_bias_ready = sem("gate_bias_ready")
        gate_bias_added = sem("gate_bias_added")
        expert_ready = sem("expert_ready")
        expert_added = sem("expert_added")
        stored = sem("stored")

        block = ctx.enter_context(nc.Block())
        SCALE = [float(D) ** -0.5, 1.0 / P]

        def x_tile(g, t):
            return x_res[:, bass.ds(g * GT + t, 1), :].rearrange("p a d -> p (a d)")

        def x_tiles(g, t, n):
            return x_res[:, bass.ds(g * GT + t, n), :].rearrange("p a d -> p (a d)")

        @block.sync
        def _(sp):
            def load(g):
                sp.dma_start(ctx_first[:, :, :, :], a["ctx_first"][:, bass.ds(g * 2 * GT, 2 * GT), :, :]).then_inc(first_in, 16)

            def step(i, ahead):
                for r in range(2):
                    if ahead or r == 0:
                        sp.wait_ge(xv_ready, 4 * (2 * i + r) + 4)
                        load(2 * i + r + 1)
                for r in range(2):
                    g = 2 * i + r
                    sp.wait_ge(x_new, 2 * PARTS * i + 2 * PARTS - 1 + r)
                    sp.dma_start(out_dram[bass.ds(g * GTOK, GTOK), :].rearrange("(t p) d -> p t d", p=P), x_res[:, bass.ds(g * GT, GT), :]).then_inc(stored, 16)

            sp.dma_start(pair_v[:, :, :, :], a["pair_v"]).then_inc(pair_v_const, 16)
            load(0)
            with sp.Fori(0, NG // 2 - 1) as i:
                step(i, True)
            step(NG // 2 - 1, False)
            sp.wait_ge(stored, 16 * NG)

        @block.gpsimd
        def _(pool):
            def step(i, is_last):
                def add_row(s, r):
                    pool.wait_ge(rows_ready, 2 * PARTS * i + 6 * s + r + 1)
                    pool.sem_inc(pool_passed, 1)
                    rows = x_res[:, bass.ds((2 * i + r) * GT, GT), :]
                    pool.tensor_tensor(rows, rows, att_row[s][:, :].unsqueeze(1).broadcast_to([P, GT, D]), ALU.add).then_inc(bias_added, 1)

                def cross_attention(g):
                    wait_in(pool, "cross_in")
                    pool.wait_ge(xk1_copied, g + 1)
                    pool.tensor_tensor(wide_k[1][:, :, :, :], xk1[:, :].rearrange("p (b s) -> p b s", s=S).unsqueeze(2).broadcast_to([P, 2 * GT, HPC, S]),
                                       head_mask[:, :].unsqueeze(1).unsqueeze(3).broadcast_to([P, 2 * GT, HPC, S]), ALU.mult).then_inc(wide1_done, 1)
                    for n in range(SM):
                        pool.wait_ge(xs_max, SM * g + n + 1)
                        pool.tensor_tensor(xs[n % XR][:, :, :], xs[n % XR][:, :, :], xmax[:, n % XR, :].unsqueeze(2).broadcast_to([P, HPC, S]), ALU.subtract).then_inc(xs_shifted, 1)

                for r in range(2):
                    add_row(0, r)
                for r in range(2):
                    cross_attention(2 * i + r)
                for r in range(2):
                    add_row(1, r)

            with pool.Fori(0, NG // 2 - 1) as i:
                step(i, False)
            step(NG // 2 - 1, True)

        @block.scalar
        def _(act):
            def step(i, is_last):
                def cols(n):
                    for c in range(2):
                        act.wait_ge(cols_ready, 2 * n + c + 1)
                        act.activation(yt[:, c, :], bank[c][:, :], ACT.Copy).then_inc(cols_copied, 1)

                def attention(s, r):
                    n = 4 * i + 2 * s + r
                    cols(2 * PARTS * i + 6 * s + r)
                    lins = 4 - 2 * s
                    if r == 0:
                        wait_in(act, f"att{s}_in")
                    before = 12 * i + (8 + 2 * r if s else 4 * r)
                    for c in range(lins):
                        act.wait_ge(lin_ready, before + c + 1)
                        act.activation(lin[:, c, :], bank[2 + c][:, :], ACT.Identity, bias=att_b[s][:, c:c + 1]).then_inc(lin_copied, 1)
                    act.wait_ge(vals_ready, 2 * n + 1)
                    act.activation(vals[:, 0:2, :].rearrange("p t d -> p (t d)"), bank[6][:, :], ACT.Copy).then_inc(vals_copied, 1)
                    act.wait_ge(att_steps, ATT_STEPS * n + 3)
                    for t in range(GT):
                        last = act.activation(att_p[:, t, :], masked[:, t, :], ACT.Exp, bias=att_shift[:, t:t + 1], scale=SCALE[s], accum_out=att_sum[:, t:t + 1])
                    last.then_inc(att_exp, 1)
                    act.wait_ge(att_turned, n + 1)
                    act.activation(att_pt[:, :], bank[1][:, :], ACT.Copy).then_inc(att_turned_copied, 1)

                def feed_forward(r):
                    g = 2 * i + r
                    cols(2 * PARTS * i + 2 + r)
                    for c in range(HC):
                        act.wait_ge(hidden_ready, HC * g + c + 1)
                        act.activation(hidden[:, c, :], bank[3 + c % 2][:, :], ACT.Gelu).then_inc(gelu_done, 1)
                        if c == HC - 2:
                            act.wait_ge(keep_turned, g + 1)
                            act.activation(keep_t[:, :], bank[7][0:NB0, :], ACT.Copy).then_inc(keep_copied, 1)

                def cross_attention(r):
                    g = 2 * i + r
                    if r == 0:
                        wait_in(act, "cross_in")
                    act.wait_ge(xk_ready, 2 * g + 2)
                    act.activation(xk1[:, :], bank[6][:, :], ACT.Copy).then_inc(xk1_copied, 1)
                    for h in range(HPC):
                        last = act.activation(wide_k[0][:, :, h, :], bank[5][:, :].rearrange("p (b s) -> p b s", s=S), ACT.Copy, scale=head_mask[:, h:h + 1])
                    last.then_inc(wide0_done, 1)
                    cols(2 * PARTS * i + 4 + r)
                    for c in range(2):
                        act.wait_ge(xq_ready, 2 * g + c + 1)
                        act.activation(xq[:, c, :], bank[c][:, :], ACT.Copy).then_inc(xq_copied, 1)
                    for n in range(SM + 2):
                        if n >= 2:
                            act.wait_ge(xpt_ready, SM * g + n - 1)
                            act.activation(xpt[n % 2][:, :, :].rearrange("p a q -> p (a q)"), bank[4 + n % 2][:, :], ACT.Copy).then_inc(xpt_copied, 1)
                        if n < SM:
                            act.wait_ge(xs_shifted, SM * g + n + 1)
                            act.activation(xp[n % 2][:, :], xs[n % XR][:, :, :].rearrange("p h s -> p (h s)"), ACT.Exp, scale=float(HD) ** -0.5).then_inc(xp_done, 1)
                    act.wait_ge(xot_ready, 2 * g + 1)
                    act.activation(xot[:, 0, :], bank[0][:, :], ACT.Copy).then_inc(xot_by_act, 1)

                def mix_experts(r):
                    g = 2 * i + r
                    cols(2 * PARTS * i + 8 + r)
                    act.wait_ge(gate_shifted, g + 1)
                    act.activation(gate[:, :, :], gate[:, :, :], ACT.Exp).then_inc(gate_exp, 1)
                    act.wait_ge(gate_turned, g + 1)
                    act.activation(gate_t[:, :], bank[7][0:NE, :], ACT.Copy).then_inc(gate_copied, 1)

                for r in range(2):
                    attention(0, r)
                for r in range(2):
                    feed_forward(r)
                for r in range(2):
                    cross_attention(r)
                for r in range(2):
                    attention(1, r)
                for r in range(2):
                    mix_experts(r)

            with act.Fori(0, NG // 2 - 1) as i:
                step(i, False)
            step(NG // 2 - 1, True)

        @block.vector
        def _(dve):
            square = "p (t i j) -> p t i j"
            def step(i, is_last):
                def normalised(part, r):
                    n = 2 * PARTS * i + 2 * part + r
                    g = 2 * i + r + (2 if part == PARTS else 0)
                    if part > 0:
                        dve.wait_ge(x_new, n - 1)
                    dve.sem_inc(dve_passed, 1)
                    last = layernorm_rows(dve, Steps(dve, ln_steps, LN_STEPS * n), [x_tile(g, t) for t in range(GT)], [y[r][:, t, :] for t in range(GT)],
                                          stats, mv, half_var, root, work, passed=dve_passed)
                    last.then_inc(rows_ready, 1)

                def normalise_other(part, r):
                    if r == 0:
                        normalised(part, 1)
                    elif part + 1 < PARTS or not is_last:
                        normalised(part + 1, 0)

                def attention(s, r):
                    n = 4 * i + 2 * s + r
                    g = 2 * i + r
                    normalise_other(3 * s, r)
                    if s == 0 and r == 0:
                        wait_in(dve, "att0_in")
                    dve.wait_ge(att_ready, n + 1)
                    steps = Steps(dve, att_steps, ATT_STEPS * n)
                    steps.then(dve.tensor_tensor(masked[:, :, :], bank[0][:, :].rearrange("p (t k) -> p t k", t=GT),
                                                 block_mask[:, :].unsqueeze(1).broadcast_to([P, GT, P]), ALU.add))
                    steps.then(dve.tensor_reduce(att_shift[:, :], masked[:, :, :], AX.X, ALU.max, negate=True))
                    steps.then(dve.tensor_scalar(att_shift[:, :], att_shift[:, :], SCALE[s], None, ALU.mult))
                    dve.wait_ge(vals_ready, 2 * n + 2)
                    dve.tensor_copy(vals[:, 2:4, :].rearrange("p t d -> p (t d)"), bank[7][:, :]).then_inc(vals_by_dve, 1)
                    dve.wait_ge(att_exp, n + 1)
                    steps.then(dve.reciprocal(att_inv[:, :], att_sum[:, :]))
                    dve.wait_ge(bias_added, n + 1)
                    for t in range(GT):
                        if t % 2 == 0:
                            dve.wait_ge(att_mixed, 2 * n + t // 2 + 1)
                        last = dve.scalar_tensor_tensor(out=x_tile(g, t), in0=bank[2 + t // 2][:, D * (t % 2):D * (t % 2) + D], scalar=att_inv[:, t:t + 1],
                                                        in1=x_tile(g, t), op0=ALU.mult, op1=ALU.add)
                    last.then_inc(x_new, 1)

                def feed_forward(r):
                    g = 2 * i + r
                    normalise_other(1, r)
                    if r == 0:
                        wait_in(dve, "ffn_in")
                    dve.wait_ge(logits0_ready, g + 1)
                    lsteps = Steps(dve, logits_steps, g)
                    lsteps.then(dve.tensor_tensor(logits[:, :, :], bank[2][:, 0:GT * NB0].rearrange("p (t n) -> p t n", n=NB0),
                                                  router0_b[:, :].unsqueeze(1).broadcast_to([P, GT, NB0]), ALU.add))
                    rank_below(dve, Steps(dve, rank_steps, RANK_STEPS * (4 * i + r)), logits[:, :, :], NB0, tri0[:, :],
                               diff[:, :].rearrange(square, t=GT, i=NB0), order[:, :].rearrange(square, t=GT, i=NB0),
                               rank[:, :, :], keep[:, :, :], TOP0)
                    for c in range(HC):
                        dve.wait_ge(spread_ready, HC * g + c + 1)
                        dve.wait_ge(gelu_done, HC * g + c + 1)
                        dve.tensor_tensor(hidden[:, c, :], bank[5 + c % 2][:, :], hidden[:, c, :], ALU.mult).then_inc(hidden_masked, 1)
                    dve.wait_ge(ffn_ready, g + 1)
                    for t, k in enumerate(FFN_BANKS):
                        last = dve.tensor_tensor(x_tile(g, t), bank[k][:, 0:D], x_tile(g, t), ALU.add)
                    last.then_inc(x_new, 1)

                def cross_attention(r):
                    g = 2 * i + r
                    normalise_other(2, r)
                    if r == 0:
                        wait_in(dve, "cross_in")
                    for k in range(4):
                        dve.wait_ge(xv_ready, 4 * g + k + 1)
                        for b2 in range(2):
                            last = dve.tensor_tensor(pair_v[:, 2 * k + b2, :, 0:2 * HD], bank[XV_BANKS[k]][:, D * b2:D * b2 + D].rearrange("p (a d) -> p a d", a=HPC),
                                                     pair_mask[:, :].rearrange("p (a d) -> p a d", a=HPC), ALU.mult)
                        last.then_inc(pair_v_done, 1)

                    def finish(t):
                        dve.wait_ge(xo_ready, 2 * GT * g + 2 * t + 2)
                        pv = bank[6 + t % 2][:, 0:HPC * PV].rearrange("p (a v) -> p a v", v=PV)
                        dve.reciprocal(xinv[:, t, :].rearrange("p (a e) -> p a e", e=2), pv[:, :, 2 * HD:PV]).then_inc(xinv_done, 1)
                        dve.wait_ge(xinv_done, GT * g + t + 1)
                        for e in range(2):
                            last = dve.tensor_tensor(xo[:, t, :].rearrange("p (a e d) -> p a e d", e=2, d=HD)[:, :, e, :], pv[:, :, HD * e:HD * e + HD],
                                                     xinv[:, t, e::2].unsqueeze(2).broadcast_to([P, HPC, HD]), ALU.mult)
                        last.then_inc(xo_done, 1)

                    for n in range(SM):
                        dve.wait_ge(xs_ready, SM * g + n + 1)
                        if n >= XR:
                            dve.wait_ge(xp_done, SM * g + n - XR + 1)
                        dve.tensor_tensor(xs[n % XR][:, :, :], bank[2 + n % 2][:, :].rearrange("p (h s) -> p h s", s=S),
                                          causal[:, :].unsqueeze(1).broadcast_to([P, HPC, S]), ALU.add).then_inc(xs_masked, 1)
                        dve.wait_ge(xs_masked, SM * g + n + 1)
                        dve.tensor_reduce(xmax[:, n % XR, :], xs[n % XR][:, :, :], AX.X, ALU.max).then_inc(xs_max, 1)
                        if n >= 5 and n % 2 == 1:
                            finish((n - 5) // 2)
                    finish(GT - 2)
                    finish(GT - 1)
                    dve.wait_ge(xot_ready, 2 * g + 2)
                    dve.tensor_copy(xot[:, 1, :], bank[1][:, :]).then_inc(xot_by_dve, 1)
                    for k in range(2):
                        dve.wait_ge(xout_ready, 2 * g + k + 1)
                        last = dve.tensor_tensor(x_tiles(g, 2 * k, 2), bank[2 + k][:, :], x_tiles(g, 2 * k, 2), ALU.add)
                    last.then_inc(x_new, 1)

                def mix_experts(r):
                    g = 2 * i + r
                    normalise_other(4, r)
                    if r == 0:
                        wait_in(dve, "experts_in")
                    dve.wait_ge(logits1_ready, g + 1)
                    steps = Steps(dve, gate_steps, GATE_STEPS * g)
                    lg = logits[:, :, 0:NE]
                    steps.then(dve.tensor_copy(lg, bank[2][:, 0:GT * NE].rearrange("p (t n) -> p t n", n=NE)))
                    steps.then(dve.tensor_reduce(top[:, :], lg, AX.X, ALU.max))
                    dve.tensor_tensor(gate[:, :, :], lg, top[:, :].unsqueeze(2).broadcast_to([P, GT, NE]), ALU.subtract).then_inc(gate_shifted, 1)
                    n2 = GT * NE * NE
                    rank_below(dve, Steps(dve, rank_steps, RANK_STEPS * (4 * i + 2 + r)), lg, NE, tri1[:, :],
                               diff[:, 0:n2].rearrange(square, t=GT, i=NE), order[:, 0:n2].rearrange(square, t=GT, i=NE),
                               rank[:, :, 0:NE], keep[:, :, 0:NE], TOP1)
                    dve.wait_ge(gate_exp, g + 1)
                    steps.then(dve.tensor_tensor(gate[:, :, :], gate[:, :, :], keep[:, :, 0:NE], ALU.mult))
                    steps.then(dve.tensor_reduce(gsum[:, :], gate[:, :, :], AX.X, ALU.add))
                    steps.then(dve.reciprocal(ginv[:, :], gsum[:, :]))
                    steps.then(dve.tensor_tensor(gate[:, :, :], gate[:, :, :], ginv[:, :].unsqueeze(2).broadcast_to([P, GT, NE]), ALU.mult))
                    for t in range(GT):
                        for e in range(NE):
                            m = NE * t + e
                            if e % 2 == 0:
                                dve.wait_ge(expert_ready, GT * NE // 2 * g + m // 2 + 1)
                            if e > 0:
                                dve.wait_ge(expert_added, GT * NE * g + m)
                            dve.scalar_tensor_tensor(out=x_tile(g, t), in0=bank[3 + e // 2][:, D * (e % 2):D * (e % 2) + D], scalar=gate[:, t, e:e + 1],
                                                     in1=x_tile(g, t), op0=ALU.mult, op1=ALU.add).then_inc(expert_added, 1)
                        if t == 0:
                            dve.wait_ge(expert_added, GT * NE * g + NE)
                            dve.wait_ge(gate_bias_ready, g + 1)
                            for k in range(2):
                                last = dve.tensor_tensor(x_tiles(g, 2 * k, 2), bank[k][:, :], x_tiles(g, 2 * k, 2), ALU.add)
                            last.then_inc(gate_bias_added, 1)
                            dve.wait_ge(gate_bias_added, g + 1)
                    dve.wait_ge(expert_added, GT * NE * (g + 1))
                    dve.sem_inc(x_new, 1)

                for r in range(2):
                    attention(0, r)
                for r in range(2):
                    feed_forward(r)
                for r in range(2):
                    cross_attention(r)
                for r in range(2):
                    attention(1, r)
                for r in range(2):
                    mix_experts(r)

            with dve.Fori(0, NG // 2 - 1) as i:
                step(i, False)
            step(NG // 2 - 1, True)

        @block.tensor
        def _(pe):
            def step(i, is_last):
                def tile(t):
                    return slice(P * t, P * t + P)

                def cols(part, r):
                    n = 2 * PARTS * i + 2 * part + r
                    pe.wait_ge(rows_ready, n + 1)
                    for c in range(2):
                        for t in range(GT):
                            last = pe.transpose(bank[c][:, tile(t)], y[r][:, t, P * c:P * c + P], ident[:, :])
                        last.then_inc(cols_ready, 1)
                    pe.wait_ge(cols_copied, 2 * n + 2)
                    if part + r > 0 or is_last:
                        pe.wait_ge(x_new, n)

                def attention(s, r):
                    n = 4 * i + 2 * s + r
                    cols(3 * s, r)
                    lins = 4 - 2 * s
                    if r == 0:
                        wait_in(pe, f"att{s}_in")
                    for c in range(lins):
                        for k in range(2):
                            last = pe.matmul(bank[2 + c][:, :], att_w[s][:, k, c, :], yt[:, k, :], start=(k == 0), stop=(k == 1))
                        last.then_inc(lin_ready, 1)
                    def values(tiles):
                        for t in tiles:
                            for k in range(2):
                                last = pe.matmul(bank[6 + t // 2][:, D * (t % 2):D * (t % 2) + D], yt[:, k, tile(t)], att_vo[s][:, k, :], start=(k == 0), stop=(k == 1))
                        last.then_inc(vals_ready, 1)

                    values((0, 1))
                    pe.wait_ge(lin_copied, 12 * i + (8 + 2 * r if s else 4 * r) + lins)
                    parts = lins // 2
                    for t in range(GT):
                        for k in range(parts):
                            last = pe.matmul(bank[0][:, tile(t)], lin[:, k, tile(t)], lin[:, parts + k, tile(t)], start=(k == 0), stop=(k == parts - 1))
                    last.then_inc(att_ready, 1)
                    values((2, 3))
                    pe.wait_ge(att_exp, n + 1)
                    for t in range(GT):
                        last = pe.transpose(bank[1][:, tile(t)], att_p[:, t, :], ident[:, :])
                    last.then_inc(att_turned, 1)
                    pe.wait_ge(att_turned_copied, n + 1)
                    pe.wait_ge(vals_copied, n + 1)
                    pe.wait_ge(vals_by_dve, n + 1)
                    for t in range(GT):
                        last = pe.matmul(bank[2 + t // 2][:, D * (t % 2):D * (t % 2) + D], att_pt[:, tile(t)], vals[:, t, :], start=True, stop=True)
                        if t % 2:
                            last.then_inc(att_mixed, 1)

                def feed_forward(r):
                    g = 2 * i + r
                    cols(1, r)
                    if r == 0:
                        wait_in(pe, "ffn_in")
                    for t in range(GT):
                        for k in range(2):
                            last = pe.matmul(bank[2][:, NB0 * t:NB0 * t + NB0], yt[:, k, tile(t)], router0[:, k, :], start=(k == 0), stop=(k == 1))
                    last.then_inc(logits0_ready, 1)

                    def hidden_chunk(c):
                        if c >= 2:
                            pe.wait_ge(gelu_done, HC * g + c - 1)
                        for k in range(2):
                            last = pe.matmul(bank[3 + c % 2][:, :], w1[:, k, P * c:P * c + P], yt[:, k, :], start=(k == 0), stop=(k == 1))
                        last.then_inc(hidden_ready, 1)

                    def hidden_out(c):
                        pe.wait_ge(hidden_masked, HC * g + c + 1)
                        for t, k in enumerate(FFN_BANKS):
                            last = pe.matmul(bank[k][:, 0:D], hidden[:, c, tile(t)], w2[:, c, :], start=(c == 0), stop=(c == HC - 1))
                        if c == HC - 1:
                            last.then_inc(ffn_ready, 1)

                    def spread_blocks(c):
                        pe.matmul(bank[5 + c % 2][:, :], spread[:, c, :], keep_t[:, :], start=True, stop=True).then_inc(spread_ready, 1)

                    for c in range(HC - 1):
                        hidden_chunk(c)
                    pe.wait_ge(rank_steps, RANK_STEPS * (4 * i + r) + RANK_STEPS)
                    for t in range(GT):
                        last = pe.transpose(bank[7][0:NB0, tile(t)], keep[:, t, :], ident[:, :])
                    last.then_inc(keep_turned, 1)
                    hidden_chunk(HC - 1)
                    pe.wait_ge(keep_copied, g + 1)
                    for c in range(2):
                        spread_blocks(c)
                    pe.wait_ge(gelu_done, HC * g + HC)
                    for c in range(HC):
                        hidden_out(c)
                        if c + 2 < HC:
                            spread_blocks(c + 2)

                def cross_attention(r):
                    g = 2 * i + r
                    if r == 0:
                        wait_in(pe, "cross_in")
                    pe.wait_ge(first_in, 16 * g + 16)
                    for c in range(2):
                        pe.matmul(bank[5 + c][:, :], x_wk[:, P * c:P * c + P], ctx_first[:, :, 0, :], start=True, stop=True).then_inc(xk_ready, 1)
                    pe.wait_ge(x_new, 2 * PARTS * i + 4 + r)
                    for k in range(4):
                        for b2 in range(2):
                            last = pe.matmul(bank[XV_BANKS[k]][:, D * b2:D * b2 + D], ctx_first[:, 2 * k + b2, :, :].rearrange("p e s -> p (e s)"), x_wv[:, :],
                                             start=True, stop=True)
                        last.then_inc(xv_ready, 1)
                    cols(2, r)
                    for c in range(2):
                        for k in range(2):
                            last = pe.matmul(bank[c][:, :], x_wq[:, k, P * c:P * c + P], yt[:, k, :], start=(k == 0), stop=(k == 1))
                        last.then_inc(xq_ready, 1)
                    pe.wait_ge(xq_copied, 2 * g + 2)
                    pe.wait_ge(wide0_done, g + 1)
                    pe.wait_ge(wide1_done, g + 1)
                    pe.wait_ge(pair_v_done, 4 * g + 4)
                    for n in range(SM + 3):
                        if n < SM:
                            t, c = divmod(n, 2)
                            if n >= 2:
                                pe.wait_ge(xs_masked, SM * g + n - 1)
                            for b2 in range(2):
                                last = pe.matmul(bank[2 + n % 2][S * b2:S * b2 + S, :], xq[:, c, P * t + S * b2:P * t + S * b2 + S],
                                                 wide_k[c][:, 2 * t + b2, :, :].rearrange("p h s -> p (h s)"), start=True, stop=True)
                            last.then_inc(xs_ready, 1)
                        if 2 <= n <= SM + 1:
                            m = n - 2
                            pe.wait_ge(xp_done, SM * g + m + 1)
                            if m >= 2:
                                pe.wait_ge(xpt_copied, SM * g + m - 1)
                            for a2 in range(4):
                                last = pe.transpose(bank[4 + m % 2][:, tile(a2)], xp[m % 2][:, tile(a2)], ident[:, :])
                            last.then_inc(xpt_ready, 1)
                        if n >= 3:
                            m = n - 3
                            t, c = divmod(m, 2)
                            pe.wait_ge(xpt_copied, SM * g + m + 1)
                            if t >= 2 and c == 0:
                                pe.wait_ge(xo_done, GT * g + t - 1)
                            for a2 in range(4):
                                pair = 4 * c + a2
                                for b2 in range(2):
                                    last = pe.matmul(bank[6 + t % 2][S * b2:S * b2 + S, PV * pair:PV * pair + PV], xpt[m % 2][:, a2, S * b2:S * b2 + S],
                                                     pair_v[:, 2 * t + b2, pair, :], start=True, stop=True)
                            last.then_inc(xo_ready, 1)
                    pe.wait_ge(xo_done, GT * g + GT)
                    for c in range(2):
                        for t in range(GT):
                            last = pe.transpose(bank[c][:, tile(t)], xo[:, t, P * c:P * c + P], ident[:, :])
                        last.then_inc(xot_ready, 1)
                    pe.wait_ge(xot_by_act, g + 1)
                    pe.wait_ge(xot_by_dve, g + 1)
                    for t in range(GT):
                        for k in range(2):
                            last = pe.matmul(bank[2 + t // 2][:, D * (t % 2):D * (t % 2) + D], xot[:, k, tile(t)], x_wo[:, k, :], start=(k == 0), stop=(k == 1))
                        if t % 2:
                            last.then_inc(xout_ready, 1)

                def mix_experts(r):
                    g = 2 * i + r
                    cols(4, r)
                    if r == 0:
                        wait_in(pe, "experts_in")
                    for t in range(GT):
                        for k in range(2):
                            last = pe.matmul(bank[2][:, NE * t:NE * t + NE], yt[:, k, tile(t)], router1[:, k, :], start=(k == 0), stop=(k == 1))
                    last.then_inc(logits1_ready, 1)
                    for t in range(GT):
                        for e2 in range(NE // 2):
                            if t > 0:
                                pe.wait_ge(expert_added, GT * NE * g + NE * (t - 1) + 2 * e2 + 2)
                            for k in range(2):
                                last = pe.matmul(bank[3 + e2][:, :], yt[:, k, tile(t)], experts[:, k, 2 * e2:2 * e2 + 2, :].rearrange("p e d -> p (e d)"),
                                                 start=(k == 0), stop=(k == 1))
                            last.then_inc(expert_ready, 1)
                        if t == 0:
                            pe.wait_ge(gate_steps, GATE_STEPS * g + GATE_STEPS)
                            for t1 in range(GT):
                                last = pe.transpose(bank[7][0:NE, tile(t1)], gate[:, t1, :], ident[:, :])
                            last.then_inc(gate_turned, 1)
                            pe.wait_ge(gate_copied, g + 1)
                            for t1 in range(GT):
                                last = pe.matmul(bank[t1 // 2][:, D * (t1 % 2):D * (t1 % 2) + D], gate_t[:, tile(t1)], expert_b[:, :], start=True, stop=True)
                            last.then_inc(gate_bias_ready, 1)

                for r in range(2):
                    attention(0, r)
                for r in range(2):
                    feed_forward(r)
                for r in range(2):
                    cross_attention(r)
                for r in range(2):
                    attention(1, r)
                for r in range(2):
                    mix_experts(r)

            with pe.Fori(0, NG // 2 - 1) as i:
                step(i, False)
            step(NG // 2 - 1, True)


OWN = {"wv0": [P, 2, D],
       "wo0": [P, 2, D],
       "bv0": [P, 2, P],
       "bo0": [P, D],
       "wv1": [P, D], "wo1": [P, H, D], "bv1": [P, P], "bo1": [P, D]}


def load_own(sp, a, own, own_in):
    for name in OWN:
        sp.dma_start(own[name][tuple(slice(None) for _ in OWN[name])], a[name]).then_inc(own_in, 16)


def fold_values(nc, bank, own, att_vo, att_row, load_weights, normalise_first):
    with ExitStack() as ctx:
        def sb(name, shape, dt=F32):
            return ctx.enter_context(nc.sbuf_tensor(name, shape, dt))

        def sem(name):
            return ctx.enter_context(nc.semaphore(name))

        wv0, wo0, bv0, bo0, wv1, _, bv1, bo1 = (own[name] for name in OWN)
        wo1_sum = own["wo1_sum"]
        joined = sem("joined")
        joined_copied = sem("joined_copied")
        rows_made = sem("rows_made")
        block = ctx.enter_context(nc.Block())

        @block.sync
        def _(sp):
            load_weights(sp)

        @block.tensor
        def _(pe):
            for c in range(2):
                for k in range(2):
                    last = pe.matmul(bank[0][:, D * c:D * c + D], wv0[:, k, P * c:P * c + P], wo0[:, k, :], start=(k == 0), stop=(k == 1))
            last.then_inc(joined, 1)
            for k in range(2):
                last = pe.matmul(bank[1][:, 0:D], bv0[:, k, :], wo0[:, k, :], start=(k == 0), stop=(k == 1))
            last.then_inc(joined, 1)
            for c in range(2):
                last = pe.matmul(bank[2][:, D * c:D * c + D], wv1[:, P * c:P * c + P], wo1_sum[:, :], start=True, stop=True)
            last.then_inc(joined, 1)
            pe.matmul(bank[3][:, 0:D], bv1[:, :], wo1_sum[:, :], start=True, stop=True).then_inc(joined, 1)

        @block.scalar
        def _(act):
            for s in range(2):
                act.wait_ge(joined, 2 * s + 1)
                act.activation(att_vo[s][:, :, :].rearrange("p k d -> p (k d)"), bank[2 * s][:, :], ACT.Copy).then_inc(joined_copied, 1)

        @block.vector
        def _(dve):
            normalise_first(dve)
            for s, bo in enumerate((bo0, bo1)):
                dve.wait_ge(joined, 2 * s + 2)
                dve.tensor_tensor(att_row[s][:, :], bank[2 * s + 1][:, 0:D], bo[:, :], ALU.add).then_inc(rows_made, 1)


def bass_perceiver_two_layers(nc, a, out):
    with ExitStack() as ctx:
        x_res = ctx.enter_context(nc.sbuf_tensor("x_res", [P, NT, D], F32))
        ident = ctx.enter_context(nc.sbuf_tensor("ident", [P, P], F32))
        own = {name: ctx.enter_context(nc.sbuf_tensor(name, shape, F32)) for name, shape in OWN.items()}
        own["wo1_sum"] = ctx.enter_context(nc.sbuf_tensor("wo1_sum", [P, D], F32))
        own_in = ctx.enter_context(nc.semaphore("own_in"))
        part_one(nc, a, x_res, ident, own, own_in)
        part_two(nc, a, out, x_res, ident, own)


def _layouts(i):
    import numpy as np

    c = np.ascontiguousarray
    f = np.float32
    pos = np.concatenate([np.arange(FULL_P * KT).reshape(FULL_P, KT),
                          np.arange(L - (P - FULL_P) * KT, L).reshape(P - FULL_P, KT)])
    inv = (f(1.0) / (f(10000.0) ** (np.arange(0, DC, 2, dtype=f) / f(DC)))).astype(f)
    freqs = (pos[:, :, None].astype(f) * inv).astype(f)
    sin = np.repeat(np.sin(freqs), 2, axis=-1).astype(f)
    cos = np.repeat(np.cos(freqs), 2, axis=-1).astype(f)
    sin[:, :, :DC // 2] *= -1
    repeated = np.zeros((P, KT), bool)
    repeated[FULL_P:] = pos[FULL_P:] < FULL_P * KT
    k_rows = np.zeros((P - DC, KT, P), np.float16)
    k_rows[0:2] = 1
    k_rows[2] = np.where(repeated.T, -30000.0, 0.0)
    q_rows = np.zeros((P - DC, H, S), np.float16)
    q_rows[2] = 1
    out = {
        "x": i["x"].reshape(TOK, D), "ctx": i["ctx_512"],
        "cos": cos, "sin": sin, "k_rows": k_rows.reshape(P - DC, KEYS), "q_rows": q_rows,
        "pick": np.broadcast_to(np.eye(QT, dtype=f)[None], (P, QT, QT)),
        "unpick": np.concatenate([np.repeat(np.eye(QT, dtype=f).reshape(QT, 2, QT // 2).transpose(0, 2, 1), DC, axis=2), np.zeros((P - QT, QT // 2, P), f)]),
        "ident": np.eye(P, dtype=f), "ident16": np.eye(P, dtype=np.float16),
        "wq": i["L0_xattn_Wq"].reshape(H, P, D).transpose(1, 0, 2),
        "wkc": i["L0_xattn_w_kc_q"].reshape(H, P, 2, 96).transpose(3, 2, 0, 1),
        "wqr": i["L0_xattn_W_qr"].transpose(2, 0, 1), "wkr": i["L0_xattn_W_kr"].transpose(2, 0, 1),
        "wkv": i["L0_xattn_w_kc_kv"].transpose(1, 0, 2),
        "wo": i["L0_xattn_Wo"].reshape(D, H, P).transpose(2, 1, 0),
    }
    tok = np.arange(P)
    tri = lambda n: np.broadcast_to((np.arange(n)[None, :] < np.arange(n)[:, None]).astype(f).reshape(1, n * n), (P, n * n))
    rows = lambda v: np.broadcast_to(v[None, :], (P, v.shape[0]))
    chunks = lambda w: w.reshape(2, P, -1).transpose(1, 0, 2)
    spread = np.zeros((NB0, HC, P), np.float16)
    spread[(np.arange(HF) // (HF // NB0)), np.arange(HF) // P, np.arange(HF) % P] = 1
    pair_v = np.zeros((P, 2 * GT, HPC, PV), f)
    pair_v[:S, :, :, 2 * HD] = 1
    pair_v[S:, :, :, 2 * HD + 1] = 1
    w_qkv, b_qkv = i["L0_attn_w_qkv"], i["L0_attn_b_qkv"]
    first = i["ctx_512"][:, :S, :].transpose(2, 0, 1)
    out |= {
        "att0_w": w_qkv[:2 * D].reshape(4, P, 2, P).transpose(3, 2, 0, 1), "att0_b": b_qkv[:2 * D].reshape(4, P).T,
        "att1_w": np.stack([i["L1_attn_Wv"], i["L1_attn_Wk"]]).reshape(2, 2, P, P).transpose(2, 1, 0, 3),
        "att1_b": np.stack([i["L1_attn_bv"], i["L1_attn_bk"]], axis=1),
        "wv0": w_qkv[2 * D:].reshape(2, P, D).transpose(1, 0, 2), "wo0": chunks(i["L0_attn_w_out"].T),
        "bv0": np.broadcast_to(b_qkv[2 * D:].reshape(2, P).T[:, :, None], (P, 2, P)), "bo0": rows(i["L0_attn_b_out"]),
        "wv1": i["L1_attn_Wv"].T, "wo1": i["L1_attn_Wo"].reshape(H, P, D).transpose(1, 0, 2),
        "bv1": np.broadcast_to(i["L1_attn_bv"][:, None], (P, P)), "bo1": rows(i["L1_attn_bo"]),
        "router0": chunks(i["L0_ffn_Wr"].T), "router0_b": rows(i["L0_ffn_br"]),
        "w1": chunks(i["L0_ffn_W1"].T), "w2": i["L0_ffn_W2"].T.reshape(HC, P, D).transpose(1, 0, 2),
        "x_wq": chunks(i["L1_xattn_Wq"].T), "x_wk": i["L1_xattn_Wkv_expand"][:D].T, "x_wv": i["L1_xattn_Wkv_expand"][D:].T,
        "x_wo": chunks(i["L1_xattn_Wout"].T),
        "router1": chunks(i["L1_ffn_Wr"]), "experts": i["L1_ffn_We"].reshape(NE, 2, P, D).transpose(2, 1, 0, 3), "expert_b": i["L1_ffn_be"],
        "block_mask": np.where((tok[:, None] // S) == (tok[None, :] // S), 0.0, -1e30).astype(f),
        "causal": np.where(np.arange(S)[None, :] <= (tok % S)[:, None], 0.0, -1e30).astype(f),
        "head_mask": ((tok[:, None] // HD) == np.arange(HPC)[None, :]).astype(f),
        "pair_mask": ((np.arange(D)[None, :] // HD % 2) == (tok[:, None] // S)).astype(f),
        "tri0": tri(NB0), "tri1": tri(NE), "spread": spread, "pair_v": pair_v,
        "ctx_first": np.stack([first, first], axis=2),
    }
    return {k: c(v) for k, v in out.items()}


def kernel(**inputs):
    import numpy as _np
    import concourse.bacc as _bacc
    from concourse import mybir as _mybir
    from concourse.bass_utils import run_bass_kernel_spmd as _run

    nc = _bacc.Bacc("TRN2", target_bir_lowering=False, num_devices=1)
    arrays, args = {}, {}
    for name, v in _layouts({k: _np.asarray(v) for k, v in inputs.items()}).items():
        arrays[f"in_{name}"] = v
        args[name] = nc.dram_tensor(f"in_{name}", v.shape, _mybir.dt.from_np(v.dtype), kind="ExternalInput").ap()
    out = nc.dram_tensor("out", (TOK, D), _mybir.dt.float32, kind="ExternalOutput").ap()
    bass_perceiver_two_layers(nc, args, out)
    r = _run(nc, [arrays], core_ids=[0])
    return r.results[0]["out"].reshape(B, S, D)
```
